# Optimizing a Trainium2 kernel written in Bass

```python
import numpy as np
import jax
import jax.numpy as jnp

def _softmax(x, axis=-1):
    return jax.nn.softmax(x, axis=axis)

def _gelu(x):
    return jax.nn.gelu(x, approximate=True)

def _silu(x):
    return jax.nn.silu(x)

def _sigmoid(x):
    return jax.nn.sigmoid(x)

def _layernorm(x, axis=-1, eps=1e-05):
    m = jnp.mean(x, axis=axis, keepdims=True)
    v = jnp.var(x, axis=axis, keepdims=True)
    return (x - m) / jnp.sqrt(v + eps)

def _scatter_add(tgt, idx, src, axis=0):
    return tgt.at[idx].add(src)

def _segment_sum(src, seg, n):
    return jax.ops.segment_sum(src, seg, n)
kernel_name = 'mk_decoder_preln_d4_seqx_r4_38baa7'

def setup_inputs(seed: int=0):
    np.random.seed(seed)
    _w = jnp.asarray

    def _rec_inputs():
        import jax
        import jax.numpy as jnp
        _rk = jax.random.key(seed)
        x = -0.0002928 + 1 * jax.random.normal(jax.random.fold_in(_rk, 1), (16, 128, 256), jnp.float32)
        _lenS = 128 - jax.random.randint(jax.random.fold_in(_rk, 7), (16,), 0, max(1, 128 // 4) + 1, jnp.int32)
        _lenS2 = 128 - jax.random.randint(jax.random.fold_in(_rk, 8), (16,), 0, max(1, 128 // 4) + 1, jnp.int32)
        _ctx_768P = jax.random.normal(jax.random.fold_in(_rk, 11), (16, 16, 192), jnp.float32)
        _ctx_768c = jax.random.dirichlet(jax.random.fold_in(_rk, 511), 0.3 * jnp.ones((16,), jnp.float32), (16, 128))
        _ctx_768t = jnp.einsum('bsk,bkd->bsd', _ctx_768c, _ctx_768P)
        _ctx_768t = _ctx_768t * jax.lax.rsqrt(jnp.mean(jnp.square(_ctx_768t)) + 1e-12) * 0.953939
        ctx_768 = 2.09791e-05 + 1.00001 * (_ctx_768t + 0.3 * jax.random.normal(jax.random.fold_in(_rk, 611), (16, 128, 192), jnp.float32))
        return (x, ctx_768)
    x, ctx_768 = _rec_inputs()

    def _L0_attn_setup():
        import jax, jax.numpy as jnp
        import numpy as np
        import math
        DIM = 256
        NUM_HEADS = 16
        HEAD_DIM = DIM // NUM_HEADS
        B, S = (2, 512)
        key = jax.random.key(seed)
        ks = jax.random.split(key, 9)
        sc = 0.02
        return {'x': jax.random.normal(ks[0], (B, S, DIM), jnp.float32), 'Wq': jax.random.normal(ks[1], (DIM, DIM), jnp.float32) * sc, 'bq': jax.random.normal(ks[2], (DIM,), jnp.float32) * sc, 'Wk': jax.random.normal(ks[3], (DIM, DIM), jnp.float32) * sc, 'bk': jax.random.normal(ks[4], (DIM,), jnp.float32) * sc, 'Wv': jax.random.normal(ks[5], (DIM, DIM), jnp.float32) * sc, 'bv': jax.random.normal(ks[6], (DIM,), jnp.float32) * sc, 'Wo': jax.random.normal(ks[7], (DIM, DIM), jnp.float32) * sc, 'bo': jax.random.normal(ks[8], (DIM,), jnp.float32) * sc}
    _L0_attn_all = _L0_attn_setup()
    _L0_attn_in = {k: v for k, v in _L0_attn_all.items() if k in ('Wq', 'bq', 'Wk', 'bk', 'Wv', 'bv', 'Wo', 'bo')}
    del _L0_attn_all

    def _L0_xattn_setup():
        import jax, jax.numpy as jnp
        import numpy as np
        QUERY_DIM, KV_DIM, EMBED_DIM, NUM_HEADS = (256, 192, 256, 16)
        HEAD_DIM = EMBED_DIM // NUM_HEADS
        SCALE = HEAD_DIM ** (-0.5)
        LN_EPS = 1e-05

        def _l2norm(x, eps=1e-12):
            n = jnp.sqrt(jnp.sum(x * x, axis=-1, keepdims=True))
            return x / jnp.maximum(n, eps)
        key = jax.random.key(seed)
        ks = jax.random.split(key, 12)
        B, Nq, Nk = (2, 512, 512)
        s = lambda d: 1.0 / np.sqrt(d)
        return {'query': jax.random.normal(ks[0], (B, Nq, QUERY_DIM), jnp.float32), 'key': jax.random.normal(ks[1], (B, Nk, KV_DIM), jnp.float32), 'value': jax.random.normal(ks[2], (B, Nk, KV_DIM), jnp.float32), 'Wq': jax.random.normal(ks[3], (QUERY_DIM, EMBED_DIM), jnp.float32) * s(QUERY_DIM), 'bq': jnp.zeros((EMBED_DIM,), jnp.float32), 'Wk': jax.random.normal(ks[4], (KV_DIM, EMBED_DIM), jnp.float32) * s(KV_DIM), 'bk': jnp.zeros((EMBED_DIM,), jnp.float32), 'Wv': jax.random.normal(ks[5], (KV_DIM, EMBED_DIM), jnp.float32) * s(KV_DIM), 'bv': jnp.zeros((EMBED_DIM,), jnp.float32), 'Wo': jax.random.normal(ks[6], (EMBED_DIM, EMBED_DIM), jnp.float32) * s(EMBED_DIM), 'bo': jnp.zeros((EMBED_DIM,), jnp.float32), 'ln_gamma': jnp.ones((EMBED_DIM,), jnp.float32), 'ln_beta': jnp.zeros((EMBED_DIM,), jnp.float32)}
    _L0_xattn_all = _L0_xattn_setup()
    _L0_xattn_in = {k: v for k, v in _L0_xattn_all.items() if k in ('Wq', 'bq', 'Wk', 'bk', 'Wv', 'bv', 'Wo', 'bo', 'ln_gamma', 'ln_beta')}
    del _L0_xattn_all

    def _L0_ffn_setup():
        import jax, jax.numpy as jnp
        import numpy as np
        H, I, E, K = (256, 128, 32, 8)
        B, S = (4, 256)

        def silu(x):
            return x * jax.nn.sigmoid(x)
        key = jax.random.key(seed)
        ks = jax.random.split(key, 14)

        def w(k, shape, fan_in):
            return jax.random.normal(k, shape, jnp.float32) / np.float32(np.sqrt(fan_in))
        return {'hidden_states': jax.random.normal(ks[0], (B, S, H), jnp.float32), 'Wr': w(ks[1], (H, E), H), 'br': jnp.zeros((E,), jnp.float32), 'Wg_s': w(ks[2], (H, I), H), 'bg_s': jnp.zeros((I,), jnp.float32), 'Wu_s': w(ks[3], (H, I), H), 'bu_s': jnp.zeros((I,), jnp.float32), 'Wd_s': w(ks[4], (I, H), I), 'bd_s': jnp.zeros((H,), jnp.float32), 'Wg': w(ks[5], (E, H, I), H), 'bg': jnp.zeros((E, I), jnp.float32), 'Wu': w(ks[6], (E, H, I), H), 'bu': jnp.zeros((E, I), jnp.float32), 'Wd': w(ks[7], (E, I, H), I), 'bd': jnp.zeros((E, H), jnp.float32)}
    _L0_ffn_all = _L0_ffn_setup()
    _L0_ffn_in = {k: v for k, v in _L0_ffn_all.items() if k in ('Wr', 'br', 'Wg_s', 'bg_s', 'Wu_s', 'bu_s', 'Wd_s', 'bd_s', 'Wg', 'bg', 'Wu', 'bu', 'Wd', 'bd')}
    del _L0_ffn_all

    def _L1_attn_setup():
        import jax, jax.numpy as jnp
        import numpy as np
        B, N, DM = (8, 1024, 256)
        H, K = (16, 64)
        DH = DM // H
        EPS = 1e-06
        MIN_SCALE = 0.001

        def _affinity(t, centers, inv_two_sig2, amplitudes):
            t2 = jnp.sum(t * t, axis=-1, keepdims=True)
            c2 = jnp.sum(centers * centers, axis=-1)[None, :, None, :]
            tc = jnp.einsum('bhnd,hkd->bhnk', t, centers)
            d2 = jnp.maximum(t2 + c2 - 2.0 * tc, 0.0)
            return amplitudes[None, :, None, :] * jnp.exp(-d2 * inv_two_sig2[None, :, None, :])
        key = jax.random.key(seed)
        ks = jax.random.split(key, 8)
        s = 1.0 / np.sqrt(DM)
        return {'x': jax.random.normal(ks[0], (B, N, DM), jnp.float32), 'W_q': jax.random.normal(ks[1], (DM, DM), jnp.float32) * s, 'W_k': jax.random.normal(ks[2], (DM, DM), jnp.float32) * s, 'W_v': jax.random.normal(ks[3], (DM, DM), jnp.float32) * s, 'W_o': jax.random.normal(ks[4], (DM, DM), jnp.float32) * s, 'centers': jax.random.normal(ks[5], (H, K, DH), jnp.float32), 'log_scales': jax.random.normal(ks[6], (H, K), jnp.float32) * 0.1, 'amplitudes': jnp.ones((H, K), jnp.float32) + 0.1 * jax.random.normal(ks[7], (H, K), jnp.float32)}
    _L1_attn_all = _L1_attn_setup()
    _L1_attn_in = {k: v for k, v in _L1_attn_all.items() if k in ('W_q', 'W_k', 'W_v', 'W_o', 'centers', 'log_scales', 'amplitudes')}
    del _L1_attn_all

    def _L1_xattn_setup():
        import jax, jax.numpy as jnp
        import numpy as np
        HEADS = 16
        DIM_HEAD = 64
        SCALE = DIM_HEAD ** (-0.5)
        key = jax.random.key(seed)
        ks = jax.random.split(key, 7)
        B, Nq, Dq = (16, 1024, 256)
        Nc, Dc = (77, 192)
        inner = HEADS * DIM_HEAD
        return {'x': jax.random.normal(ks[0], (B, Nq, Dq), jnp.float32), 'context': jax.random.normal(ks[1], (B, Nc, Dc), jnp.float32), 'Wq': jax.random.normal(ks[2], (Dq, inner), jnp.float32) * Dq ** (-0.5), 'Wk': jax.random.normal(ks[3], (Dc, inner), jnp.float32) * Dc ** (-0.5), 'Wv': jax.random.normal(ks[4], (Dc, inner), jnp.float32) * Dc ** (-0.5), 'Wo': jax.random.normal(ks[5], (inner, Dq), jnp.float32) * inner ** (-0.5), 'bo': jnp.zeros((Dq,), jnp.float32)}
    _L1_xattn_all = _L1_xattn_setup()
    _L1_xattn_in = {k: v for k, v in _L1_xattn_all.items() if k in ('Wq', 'Wk', 'Wv', 'Wo', 'bo')}
    del _L1_xattn_all

    def _L1_ffn_setup():
        import jax, jax.numpy as jnp
        import numpy as np
        HIDDEN = 256
        INNER = 1024

        def _weight_quant(w):
            scale = 1.0 / jnp.clip(jnp.mean(jnp.abs(w)), 1e-05)
            wq = jnp.clip(jnp.round(w * scale), -1.0, 1.0) / scale
            return w + jax.lax.stop_gradient(wq - w)

        def _act_quant(x):
            scale = 127.0 / jnp.clip(jnp.max(jnp.abs(x), axis=-1, keepdims=True), 1e-05)
            xq = jnp.clip(jnp.round(x * scale), -128.0, 127.0) / scale
            return x + jax.lax.stop_gradient(xq - x)

        def _bitlinear(x, w):
            return jnp.einsum('bsi,oi->bso', _act_quant(x), _weight_quant(w))
        key = jax.random.key(seed)
        k0, k1, k2, k3 = jax.random.split(key, 4)
        x = jax.random.normal(k0, (4, 512, HIDDEN), dtype=jnp.float32)
        w_gate = jax.random.normal(k1, (INNER, HIDDEN), dtype=jnp.float32) / np.sqrt(HIDDEN)
        w_up = jax.random.normal(k2, (INNER, HIDDEN), dtype=jnp.float32) / np.sqrt(HIDDEN)
        w_down = jax.random.normal(k3, (HIDDEN, INNER), dtype=jnp.float32) / np.sqrt(INNER)
        return {'x': x, 'w_gate': w_gate, 'w_up': w_up, 'w_down': w_down}
    _L1_ffn_all = _L1_ffn_setup()
    _L1_ffn_in = {k: v for k, v in _L1_ffn_all.items() if k in ('w_gate', 'w_up', 'w_down')}
    del _L1_ffn_all

    def _L2_attn_setup():
        import jax, jax.numpy as jnp
        import numpy as np
        from jax import lax
        D_MODEL = 256
        D_STATE = 128
        D_CONV = 4
        EXPAND = 2
        HEADDIM = 64
        D_INNER = EXPAND * D_MODEL
        NHEADS = D_INNER // HEADDIM
        D_IN_PROJ = 2 * D_INNER + 2 * D_STATE + NHEADS
        CONV_CH = D_INNER + 2 * D_STATE
        CHUNK = 128
        EPS = 1e-05
        BATCH, SEQ = (2, 512)

        def silu(x):
            return x * jax.nn.sigmoid(x)

        def rmsnorm(x, w):
            return x * lax.rsqrt(jnp.mean(x * x, axis=-1, keepdims=True) + EPS) * w

        def segsum(a):
            q = a.shape[-1]
            cs = jnp.cumsum(a, axis=-1)
            seg = cs[..., :, None] - cs[..., None, :]
            mask = jnp.tril(jnp.ones((q, q), dtype=bool))
            return jnp.where(mask, seg, -jnp.inf)

        def ssd(xh, dt, A, B, C):
            b, l, h, p = xh.shape
            n = B.shape[-1]
            c = l // CHUNK
            X = (xh * dt[..., None]).reshape(b, c, CHUNK, h, p)
            Adt = (A * dt).reshape(b, c, CHUNK, h).transpose(0, 3, 1, 2)
            Bc = B.reshape(b, c, CHUNK, n)
            Cc = C.reshape(b, c, CHUNK, n)
            Acs = jnp.cumsum(Adt, axis=-1)
            L = jnp.exp(segsum(Adt))
            Y_diag = jnp.einsum('bcln,bcsn,bhcls,bcshp->bclhp', Cc, Bc, L, X)
            decay_states = jnp.exp(Acs[..., -1:] - Acs)
            states = jnp.einsum('bcln,bhcl,bclhp->bchpn', Bc, decay_states, X)
            chunk_decay = jnp.exp(Acs[..., -1])

            def step(s, inp):
                st, cd = inp
                return (s * cd[:, :, None, None] + st, s)
            init = jnp.zeros((b, h, p, n), dtype=xh.dtype)
            _, prev = lax.scan(step, init, (states.transpose(1, 0, 2, 3, 4), chunk_decay.transpose(2, 0, 1)))
            Y_off = jnp.einsum('bcln,cbhpn,bhcl->bclhp', Cc, prev, jnp.exp(Acs))
            return (Y_diag + Y_off).reshape(b, l, h, p)

        def mamba2(x, in_w, conv_w, conv_b, dt_bias, A_log, D, gnorm_w, out_w):
            b, l, _ = x.shape
            zxbcdt = x @ in_w.T
            z = zxbcdt[..., :D_INNER]
            xBC = zxbcdt[..., D_INNER:D_INNER + CONV_CH]
            dt = jax.nn.softplus(zxbcdt[..., D_INNER + CONV_CH:] + dt_bias)
            xp = jnp.pad(xBC, ((0, 0), (D_CONV - 1, 0), (0, 0)))
            conv = sum((xp[:, k:k + l, :] * conv_w[:, k] for k in range(D_CONV))) + conv_b
            xBC = silu(conv)
            xs = xBC[..., :D_INNER]
            B = xBC[..., D_INNER:D_INNER + D_STATE]
            C = xBC[..., D_INNER + D_STATE:]
            A = -jnp.exp(A_log)
            xh = xs.reshape(b, l, NHEADS, HEADDIM)
            y = ssd(xh, dt, A, B, C) + xh * D[None, None, :, None]
            y = y.reshape(b, l, D_INNER)
            y = rmsnorm(y * silu(z), gnorm_w)
            return y @ out_w.T
        key = jax.random.key(seed)
        ks = jax.random.split(key, 24)
        d = {}
        d['x'] = jax.random.normal(ks[0], (BATCH, SEQ, D_MODEL), dtype=jnp.float32)
        d['norm_w'] = jnp.ones((D_MODEL,), jnp.float32)
        d['out_w_blk'] = jax.random.normal(ks[1], (D_MODEL, 2 * D_MODEL), jnp.float32) * 0.02
        d['out_b_blk'] = jnp.zeros((D_MODEL,), jnp.float32)
        for i, pfx in enumerate(['f_', 'b_']):
            o = 2 + i * 10
            d[pfx + 'in_w'] = jax.random.normal(ks[o], (D_IN_PROJ, D_MODEL), jnp.float32) * 0.02
            d[pfx + 'conv_w'] = jax.random.normal(ks[o + 1], (CONV_CH, D_CONV), jnp.float32) * 0.2
            d[pfx + 'conv_b'] = jnp.zeros((CONV_CH,), jnp.float32)
            d[pfx + 'dt_bias'] = jax.random.normal(ks[o + 2], (NHEADS,), jnp.float32) * 0.1
            d[pfx + 'A_log'] = jnp.log(jax.random.uniform(ks[o + 3], (NHEADS,), jnp.float32, 1.0, 16.0))
            d[pfx + 'D'] = jnp.ones((NHEADS,), jnp.float32)
            d[pfx + 'gnorm_w'] = jnp.ones((D_INNER,), jnp.float32)
            d[pfx + 'out_w'] = jax.random.normal(ks[o + 4], (D_MODEL, D_INNER), jnp.float32) * 0.02
        return d
    _L2_attn_all = _L2_attn_setup()
    _L2_attn_in = {k: v for k, v in _L2_attn_all.items() if k in ('norm_w', 'out_w_blk', 'out_b_blk', 'f_in_w', 'f_conv_w', 'f_conv_b', 'f_dt_bias', 'f_A_log', 'f_D', 'f_gnorm_w', 'f_out_w', 'b_in_w', 'b_conv_w', 'b_conv_b', 'b_dt_bias', 'b_A_log', 'b_D', 'b_gnorm_w', 'b_out_w')}
    del _L2_attn_all

    def _L2_xattn_setup():
        import jax, jax.numpy as jnp
        import numpy as np
        HEADS = 8
        DIM_HEAD = 64
        SCALE = DIM_HEAD ** (-0.5)
        key = jax.random.key(seed)
        ks = jax.random.split(key, 7)
        b, n, m = (4, 512, 256)
        qd, cd, inner = (256, 192, HEADS * DIM_HEAD)
        s = lambda fan_in: 1.0 / np.sqrt(fan_in)
        return {'x': jax.random.normal(ks[0], (b, n, qd), jnp.float32), 'context': jax.random.normal(ks[1], (b, m, cd), jnp.float32), 'Wq': jax.random.normal(ks[2], (qd, inner), jnp.float32) * s(qd), 'Wk': jax.random.normal(ks[3], (cd, inner), jnp.float32) * s(cd), 'Wv': jax.random.normal(ks[4], (cd, inner), jnp.float32) * s(cd), 'Wout': jax.random.normal(ks[5], (inner, qd), jnp.float32) * s(inner), 'bout': jax.random.normal(ks[6], (qd,), jnp.float32) * 0.01}
    _L2_xattn_all = _L2_xattn_setup()
    _L2_xattn_in = {k: v for k, v in _L2_xattn_all.items() if k in ('Wq', 'Wk', 'Wv', 'Wout', 'bout')}
    del _L2_xattn_all

    def _L2_ffn_setup():
        import jax, jax.numpy as jnp
        import numpy as np
        key = jax.random.key(seed)
        k0, k1, k2, k3 = jax.random.split(key, 4)
        B, S, D, F, E = (8, 512, 256, 512, 8)
        x = jax.random.normal(k0, (B, S, D), dtype=jnp.float32)
        Wg = jax.random.normal(k1, (D, E), dtype=jnp.float32) * 0.02
        W1 = jax.random.normal(k2, (E, D, F), dtype=jnp.float32) * 0.02
        W2 = jax.random.normal(k3, (E, F, D), dtype=jnp.float32) * 0.02
        return {'x': x, 'Wg': Wg, 'W1': W1, 'W2': W2}
    _L2_ffn_all = _L2_ffn_setup()
    _L2_ffn_in = {k: v for k, v in _L2_ffn_all.items() if k in ('Wg', 'W1', 'W2')}
    del _L2_ffn_all

    def _L3_attn_setup():
        import jax, jax.numpy as jnp
        import numpy as np
        EMBED_DIM = 256
        NUM_HEADS = 16
        HEAD_DIM = EMBED_DIM // NUM_HEADS
        BATCH, SEQ = (2, 256)
        key = jax.random.key(seed)
        k1, k2, k3, k4, k5 = jax.random.split(key, 5)
        x = jax.random.normal(k1, (BATCH, SEQ, EMBED_DIM), dtype=jnp.float32)
        proj_w = jax.random.normal(k2, (EMBED_DIM, EMBED_DIM), dtype=jnp.float32) / np.sqrt(EMBED_DIM)
        proj_b = jax.random.normal(k3, (EMBED_DIM,), dtype=jnp.float32) * 0.01
        wq = jax.random.normal(k4, (NUM_HEADS, HEAD_DIM, HEAD_DIM), dtype=jnp.float32) / np.sqrt(HEAD_DIM)
        wk = jax.random.normal(k5, (NUM_HEADS, HEAD_DIM, HEAD_DIM), dtype=jnp.float32) / np.sqrt(HEAD_DIM)
        return {'x': x, 'proj_w': proj_w, 'proj_b': proj_b, 'wq': wq, 'wk': wk}
    _L3_attn_all = _L3_attn_setup()
    _L3_attn_in = {k: v for k, v in _L3_attn_all.items() if k in ('proj_w', 'proj_b', 'wq', 'wk')}
    del _L3_attn_all

    def _L3_xattn_setup():
        import jax, jax.numpy as jnp
        import numpy as np
        QUERY_DIM = 256
        CONTEXT_DIM = 192
        HEADS = 8
        DIM_HEAD = 64
        INNER = HEADS * DIM_HEAD
        key = jax.random.key(seed)
        ks = jax.random.split(key, 7)
        B, S, L = (8, 1024, 77)
        x = jax.random.normal(ks[0], (B, S, QUERY_DIM), dtype=jnp.float32)
        context = jax.random.normal(ks[1], (B, L, CONTEXT_DIM), dtype=jnp.float32)
        Wq = jax.random.normal(ks[2], (QUERY_DIM, INNER), dtype=jnp.float32) * QUERY_DIM ** (-0.5)
        Wk = jax.random.normal(ks[3], (CONTEXT_DIM, INNER), dtype=jnp.float32) * CONTEXT_DIM ** (-0.5)
        Wv = jax.random.normal(ks[4], (CONTEXT_DIM, INNER), dtype=jnp.float32) * CONTEXT_DIM ** (-0.5)
        Wo = jax.random.normal(ks[5], (INNER, QUERY_DIM), dtype=jnp.float32) * INNER ** (-0.5)
        bo = jax.random.normal(ks[6], (QUERY_DIM,), dtype=jnp.float32) * 0.01
        return {'x': x, 'context': context, 'Wq': Wq, 'Wk': Wk, 'Wv': Wv, 'Wo': Wo, 'bo': bo}
    _L3_xattn_all = _L3_xattn_setup()
    _L3_xattn_in = {k: v for k, v in _L3_xattn_all.items() if k in ('Wq', 'Wk', 'Wv', 'Wo', 'bo')}
    del _L3_xattn_all

    def _L3_ffn_setup():
        import jax, jax.numpy as jnp
        import numpy as np
        BITS = 8
        LORA_RANK = 16
        LORA_ALPHA = 32
        SCALING = LORA_ALPHA / LORA_RANK

        def fake_quant_weight(w, bits=BITS):
            qmax = 2.0 ** (bits - 1) - 1
            scale = jnp.max(jnp.abs(w)) / qmax
            wq = jnp.clip(jnp.round(w / scale), -qmax - 1, qmax) * scale
            return w + jax.lax.stop_gradient(wq - w)

        def qat_lora_linear(x, W, b, A, B):
            Wq = fake_quant_weight(W)
            base = jnp.einsum('bsi,oi->bso', x, Wq) + b
            lora = jnp.einsum('bsr,or->bso', jnp.einsum('bsi,ri->bsr', x, A), B)
            return base + SCALING * lora
        key = jax.random.key(seed)
        ks = jax.random.split(key, 9)
        d, f = (256, 1024)
        s_in = 1.0 / np.sqrt(d)
        s_ff = 1.0 / np.sqrt(f)
        return {'hidden_states': jax.random.normal(ks[0], (4, 512, d), jnp.float32), 'W_fc': jax.random.normal(ks[1], (f, d), jnp.float32) * s_in, 'b_fc': jnp.zeros((f,), jnp.float32), 'A_fc': jax.random.normal(ks[2], (LORA_RANK, d), jnp.float32) * s_in, 'B_fc': jnp.zeros((f, LORA_RANK), jnp.float32), 'W_proj': jax.random.normal(ks[3], (d, f), jnp.float32) * s_ff, 'b_proj': jnp.zeros((d,), jnp.float32), 'A_proj': jax.random.normal(ks[4], (LORA_RANK, f), jnp.float32) * s_ff, 'B_proj': jnp.zeros((d, LORA_RANK), jnp.float32)}
    _L3_ffn_all = _L3_ffn_setup()
    _L3_ffn_in = {k: v for k, v in _L3_ffn_all.items() if k in ('W_fc', 'b_fc', 'A_fc', 'B_fc', 'W_proj', 'b_proj', 'A_proj', 'B_proj')}
    del _L3_ffn_all
    return {'x': x, 'ctx_768': ctx_768, 'L0_attn_Wq': _L0_attn_in['Wq'], 'L0_attn_bq': _L0_attn_in['bq'], 'L0_attn_Wk': _L0_attn_in['Wk'], 'L0_attn_bk': _L0_attn_in['bk'], 'L0_attn_Wv': _L0_attn_in['Wv'], 'L0_attn_bv': _L0_attn_in['bv'], 'L0_attn_Wo': _L0_attn_in['Wo'], 'L0_attn_bo': _L0_attn_in['bo'], 'L0_xattn_Wq': _L0_xattn_in['Wq'], 'L0_xattn_bq': _L0_xattn_in['bq'], 'L0_xattn_Wk': _L0_xattn_in['Wk'], 'L0_xattn_bk': _L0_xattn_in['bk'], 'L0_xattn_Wv': _L0_xattn_in['Wv'], 'L0_xattn_bv': _L0_xattn_in['bv'], 'L0_xattn_Wo': _L0_xattn_in['Wo'], 'L0_xattn_bo': _L0_xattn_in['bo'], 'L0_xattn_ln_gamma': _L0_xattn_in['ln_gamma'], 'L0_xattn_ln_beta': _L0_xattn_in['ln_beta'], 'L0_ffn_Wr': _L0_ffn_in['Wr'], 'L0_ffn_br': _L0_ffn_in['br'], 'L0_ffn_Wg_s': _L0_ffn_in['Wg_s'], 'L0_ffn_bg_s': _L0_ffn_in['bg_s'], 'L0_ffn_Wu_s': _L0_ffn_in['Wu_s'], 'L0_ffn_bu_s': _L0_ffn_in['bu_s'], 'L0_ffn_Wd_s': _L0_ffn_in['Wd_s'], 'L0_ffn_bd_s': _L0_ffn_in['bd_s'], 'L0_ffn_Wg': _L0_ffn_in['Wg'], 'L0_ffn_bg': _L0_ffn_in['bg'], 'L0_ffn_Wu': _L0_ffn_in['Wu'], 'L0_ffn_bu': _L0_ffn_in['bu'], 'L0_ffn_Wd': _L0_ffn_in['Wd'], 'L0_ffn_bd': _L0_ffn_in['bd'], 'L1_attn_W_q': _L1_attn_in['W_q'], 'L1_attn_W_k': _L1_attn_in['W_k'], 'L1_attn_W_v': _L1_attn_in['W_v'], 'L1_attn_W_o': _L1_attn_in['W_o'], 'L1_attn_centers': _L1_attn_in['centers'], 'L1_attn_log_scales': _L1_attn_in['log_scales'], 'L1_attn_amplitudes': _L1_attn_in['amplitudes'], 'L1_xattn_Wq': _L1_xattn_in['Wq'], 'L1_xattn_Wk': _L1_xattn_in['Wk'], 'L1_xattn_Wv': _L1_xattn_in['Wv'], 'L1_xattn_Wo': _L1_xattn_in['Wo'], 'L1_xattn_bo': _L1_xattn_in['bo'], 'L1_ffn_w_gate': _L1_ffn_in['w_gate'], 'L1_ffn_w_up': _L1_ffn_in['w_up'], 'L1_ffn_w_down': _L1_ffn_in['w_down'], 'L2_attn_norm_w': _L2_attn_in['norm_w'], 'L2_attn_out_w_blk': _L2_attn_in['out_w_blk'], 'L2_attn_out_b_blk': _L2_attn_in['out_b_blk'], 'L2_attn_f_in_w': _L2_attn_in['f_in_w'], 'L2_attn_f_conv_w': _L2_attn_in['f_conv_w'], 'L2_attn_f_conv_b': _L2_attn_in['f_conv_b'], 'L2_attn_f_dt_bias': _L2_attn_in['f_dt_bias'], 'L2_attn_f_A_log': _L2_attn_in['f_A_log'], 'L2_attn_f_D': _L2_attn_in['f_D'], 'L2_attn_f_gnorm_w': _L2_attn_in['f_gnorm_w'], 'L2_attn_f_out_w': _L2_attn_in['f_out_w'], 'L2_attn_b_in_w': _L2_attn_in['b_in_w'], 'L2_attn_b_conv_w': _L2_attn_in['b_conv_w'], 'L2_attn_b_conv_b': _L2_attn_in['b_conv_b'], 'L2_attn_b_dt_bias': _L2_attn_in['b_dt_bias'], 'L2_attn_b_A_log': _L2_attn_in['b_A_log'], 'L2_attn_b_D': _L2_attn_in['b_D'], 'L2_attn_b_gnorm_w': _L2_attn_in['b_gnorm_w'], 'L2_attn_b_out_w': _L2_attn_in['b_out_w'], 'L2_xattn_Wq': _L2_xattn_in['Wq'], 'L2_xattn_Wk': _L2_xattn_in['Wk'], 'L2_xattn_Wv': _L2_xattn_in['Wv'], 'L2_xattn_Wout': _L2_xattn_in['Wout'], 'L2_xattn_bout': _L2_xattn_in['bout'], 'L2_ffn_Wg': _L2_ffn_in['Wg'], 'L2_ffn_W1': _L2_ffn_in['W1'], 'L2_ffn_W2': _L2_ffn_in['W2'], 'L3_attn_proj_w': _L3_attn_in['proj_w'], 'L3_attn_proj_b': _L3_attn_in['proj_b'], 'L3_attn_wq': _L3_attn_in['wq'], 'L3_attn_wk': _L3_attn_in['wk'], 'L3_xattn_Wq': _L3_xattn_in['Wq'], 'L3_xattn_Wk': _L3_xattn_in['Wk'], 'L3_xattn_Wv': _L3_xattn_in['Wv'], 'L3_xattn_Wo': _L3_xattn_in['Wo'], 'L3_xattn_bo': _L3_xattn_in['bo'], 'L3_ffn_W_fc': _L3_ffn_in['W_fc'], 'L3_ffn_b_fc': _L3_ffn_in['b_fc'], 'L3_ffn_A_fc': _L3_ffn_in['A_fc'], 'L3_ffn_B_fc': _L3_ffn_in['B_fc'], 'L3_ffn_W_proj': _L3_ffn_in['W_proj'], 'L3_ffn_b_proj': _L3_ffn_in['b_proj'], 'L3_ffn_A_proj': _L3_ffn_in['A_proj'], 'L3_ffn_B_proj': _L3_ffn_in['B_proj']}

def reference(x, ctx_768, L0_attn_Wq, L0_attn_bq, L0_attn_Wk, L0_attn_bk, L0_attn_Wv, L0_attn_bv, L0_attn_Wo, L0_attn_bo, L0_xattn_Wq, L0_xattn_bq, L0_xattn_Wk, L0_xattn_bk, L0_xattn_Wv, L0_xattn_bv, L0_xattn_Wo, L0_xattn_bo, L0_xattn_ln_gamma, L0_xattn_ln_beta, L0_ffn_Wr, L0_ffn_br, L0_ffn_Wg_s, L0_ffn_bg_s, L0_ffn_Wu_s, L0_ffn_bu_s, L0_ffn_Wd_s, L0_ffn_bd_s, L0_ffn_Wg, L0_ffn_bg, L0_ffn_Wu, L0_ffn_bu, L0_ffn_Wd, L0_ffn_bd, L1_attn_W_q, L1_attn_W_k, L1_attn_W_v, L1_attn_W_o, L1_attn_centers, L1_attn_log_scales, L1_attn_amplitudes, L1_xattn_Wq, L1_xattn_Wk, L1_xattn_Wv, L1_xattn_Wo, L1_xattn_bo, L1_ffn_w_gate, L1_ffn_w_up, L1_ffn_w_down, L2_attn_norm_w, L2_attn_out_w_blk, L2_attn_out_b_blk, L2_attn_f_in_w, L2_attn_f_conv_w, L2_attn_f_conv_b, L2_attn_f_dt_bias, L2_attn_f_A_log, L2_attn_f_D, L2_attn_f_gnorm_w, L2_attn_f_out_w, L2_attn_b_in_w, L2_attn_b_conv_w, L2_attn_b_conv_b, L2_attn_b_dt_bias, L2_attn_b_A_log, L2_attn_b_D, L2_attn_b_gnorm_w, L2_attn_b_out_w, L2_xattn_Wq, L2_xattn_Wk, L2_xattn_Wv, L2_xattn_Wout, L2_xattn_bout, L2_ffn_Wg, L2_ffn_W1, L2_ffn_W2, L3_attn_proj_w, L3_attn_proj_b, L3_attn_wq, L3_attn_wk, L3_xattn_Wq, L3_xattn_Wk, L3_xattn_Wv, L3_xattn_Wo, L3_xattn_bo, L3_ffn_W_fc, L3_ffn_b_fc, L3_ffn_A_fc, L3_ffn_B_fc, L3_ffn_W_proj, L3_ffn_b_proj, L3_ffn_A_proj, L3_ffn_B_proj):
    import jax
    import jax.numpy as jnp

    def _L0_attn_ref(x, Wq, bq, Wk, bk, Wv, bv, Wo, bo):
        import jax, jax.numpy as jnp
        import numpy as np
        import math
        DIM = 256
        NUM_HEADS = 16
        HEAD_DIM = DIM // NUM_HEADS
        B, S = (2, 512)
        b, s, d = x.shape
        h, hd = (NUM_HEADS, HEAD_DIM)

        def split_heads(t):
            return t.reshape(b, s, h, hd).transpose(0, 2, 1, 3)
        q = split_heads(x @ Wq + bq)
        k = split_heads(x @ Wk + bk)
        v = split_heads(x @ Wv + bv)
        scores = jnp.einsum('bhqd,bhkd->bhqk', q, k) / math.sqrt(hd)
        causal = jnp.tril(jnp.ones((s, s), dtype=bool))
        scores = jnp.where(causal[None, None], scores, jnp.asarray(-10000.0, scores.dtype))
        probs = jax.nn.softmax(scores, axis=-1)
        ctx = jnp.einsum('bhqk,bhkd->bhqd', probs, v)
        ctx = ctx.transpose(0, 2, 1, 3).reshape(b, s, d)
        return ctx @ Wo + bo

    def _L0_xattn_ref(query, key, value, Wq, bq, Wk, bk, Wv, bv, Wo, bo, ln_gamma, ln_beta):
        import jax, jax.numpy as jnp
        import numpy as np
        QUERY_DIM, KV_DIM, EMBED_DIM, NUM_HEADS = (256, 192, 256, 16)
        HEAD_DIM = EMBED_DIM // NUM_HEADS
        SCALE = HEAD_DIM ** (-0.5)
        LN_EPS = 1e-05

        def _l2norm(x, eps=1e-12):
            n = jnp.sqrt(jnp.sum(x * x, axis=-1, keepdims=True))
            return x / jnp.maximum(n, eps)
        B, Nq, _ = query.shape
        Nk = key.shape[1]
        Qp = query @ Wq + bq
        K = _l2norm(key @ Wk + bk)
        V = value @ Wv + bv
        Q = _l2norm(Qp)
        Q = Q.reshape(B, Nq, NUM_HEADS, HEAD_DIM).transpose(0, 2, 1, 3)
        K = K.reshape(B, Nk, NUM_HEADS, HEAD_DIM).transpose(0, 2, 1, 3)
        V = V.reshape(B, Nk, NUM_HEADS, HEAD_DIM).transpose(0, 2, 1, 3)
        scores = jnp.einsum('bhqd,bhkd->bhqk', Q, K) * SCALE
        attn = jax.nn.softmax(scores, axis=-1)
        out = jnp.einsum('bhqk,bhkd->bhqd', attn, V)
        out = out.transpose(0, 2, 1, 3).reshape(B, Nq, EMBED_DIM)
        out = out @ Wo + bo
        x = out + Qp
        mu = jnp.mean(x, axis=-1, keepdims=True)
        var = jnp.mean((x - mu) ** 2, axis=-1, keepdims=True)
        return (x - mu) / jnp.sqrt(var + LN_EPS) * ln_gamma + ln_beta

    def _L0_ffn_ref(hidden_states, Wr, br, Wg_s, bg_s, Wu_s, bu_s, Wd_s, bd_s, Wg, bg, Wu, bu, Wd, bd):
        import jax, jax.numpy as jnp
        import numpy as np
        H, I, E, K = (256, 128, 32, 8)
        B, S = (4, 256)

        def silu(x):
            return x * jax.nn.sigmoid(x)
        b, s, h = hidden_states.shape
        T = b * s
        x = hidden_states.reshape(T, h)
        logits = jnp.dot(x.astype(jnp.float32), Wr) + br
        aff = jax.nn.sigmoid(logits)
        top_v, top_i = jax.lax.top_k(aff, K)
        top_w = top_v / (jnp.sum(top_v, axis=-1, keepdims=True) + 1e-09)
        top_w = top_w.astype(hidden_states.dtype)
        e_total = Wr.shape[1]
        w_full = jnp.zeros((T, e_total), hidden_states.dtype)
        w_full = w_full.at[jnp.arange(T)[:, None], top_i].set(top_w)
        shared = jnp.dot(silu(jnp.dot(x, Wg_s) + bg_s) * (jnp.dot(x, Wu_s) + bu_s), Wd_s) + bd_s
        gate = silu(jnp.einsum('th,ehi->eti', x, Wg) + bg[:, None, :])
        up = jnp.einsum('th,ehi->eti', x, Wu) + bu[:, None, :]
        down = jnp.einsum('eti,eih->eth', gate * up, Wd) + bd[:, None, :]
        routed = jnp.einsum('te,eth->th', w_full, down)
        return (shared + routed).reshape(b, s, h)

    def _L1_attn_ref(x, W_q, W_k, W_v, W_o, centers, log_scales, amplitudes):
        import jax, jax.numpy as jnp
        import numpy as np
        B, N, DM = (8, 1024, 256)
        H, K = (16, 64)
        DH = DM // H
        EPS = 1e-06
        MIN_SCALE = 0.001

        def _affinity(t, centers, inv_two_sig2, amplitudes):
            t2 = jnp.sum(t * t, axis=-1, keepdims=True)
            c2 = jnp.sum(centers * centers, axis=-1)[None, :, None, :]
            tc = jnp.einsum('bhnd,hkd->bhnk', t, centers)
            d2 = jnp.maximum(t2 + c2 - 2.0 * tc, 0.0)
            return amplitudes[None, :, None, :] * jnp.exp(-d2 * inv_two_sig2[None, :, None, :])
        b, n, dm = x.shape
        h, k, dh = centers.shape

        def split_heads(t):
            return t.reshape(b, n, h, dh).transpose(0, 2, 1, 3)
        q = split_heads(x @ W_q)
        kk = split_heads(x @ W_k)
        v = split_heads(x @ W_v)
        scales = jnp.maximum(jnp.exp(log_scales), MIN_SCALE)
        inv_two_sig2 = 0.5 / (scales * scales)
        q_aff = _affinity(q, centers, inv_two_sig2, amplitudes)
        k_aff = _affinity(kk, centers, inv_two_sig2, amplitudes)
        v_agg = jnp.einsum('bhnk,bhnd->bhkd', k_aff, v)
        k_sum = jnp.sum(k_aff, axis=2)
        num = jnp.einsum('bhnk,bhkd->bhnd', q_aff, v_agg)
        den = jnp.einsum('bhnk,bhk->bhn', q_aff, k_sum) + EPS
        out = num / den[..., None]
        out = out.transpose(0, 2, 1, 3).reshape(b, n, dm)
        return out @ W_o

    def _L1_xattn_ref(x, context, Wq, Wk, Wv, Wo, bo):
        import jax, jax.numpy as jnp
        import numpy as np
        HEADS = 16
        DIM_HEAD = 64
        SCALE = DIM_HEAD ** (-0.5)
        B, Nq, _ = x.shape
        Nc = context.shape[1]
        q = (x @ Wq).reshape(B, Nq, HEADS, DIM_HEAD).transpose(0, 2, 1, 3)
        k = (context @ Wk).reshape(B, Nc, HEADS, DIM_HEAD).transpose(0, 2, 1, 3)
        v = (context @ Wv).reshape(B, Nc, HEADS, DIM_HEAD).transpose(0, 2, 1, 3)
        sim = jnp.einsum('bhid,bhjd->bhij', q, k) * SCALE
        attn = jax.nn.softmax(sim, axis=-1)
        out = jnp.einsum('bhij,bhjd->bhid', attn, v)
        out = out.transpose(0, 2, 1, 3).reshape(B, Nq, HEADS * DIM_HEAD)
        return out @ Wo + bo

    def _L1_ffn_ref(x, w_gate, w_up, w_down):
        import jax, jax.numpy as jnp
        import numpy as np
        HIDDEN = 256
        INNER = 1024

        def _weight_quant(w):
            scale = 1.0 / jnp.clip(jnp.mean(jnp.abs(w)), 1e-05)
            wq = jnp.clip(jnp.round(w * scale), -1.0, 1.0) / scale
            return w + jax.lax.stop_gradient(wq - w)

        def _act_quant(x):
            scale = 127.0 / jnp.clip(jnp.max(jnp.abs(x), axis=-1, keepdims=True), 1e-05)
            xq = jnp.clip(jnp.round(x * scale), -128.0, 127.0) / scale
            return x + jax.lax.stop_gradient(xq - x)

        def _bitlinear(x, w):
            return jnp.einsum('bsi,oi->bso', _act_quant(x), _weight_quant(w))
        gate = jax.nn.silu(_bitlinear(x, w_gate))
        up = _bitlinear(x, w_up)
        return _bitlinear(gate * up, w_down)

    def _L2_attn_ref(x, norm_w, out_w_blk, out_b_blk, f_in_w, f_conv_w, f_conv_b, f_dt_bias, f_A_log, f_D, f_gnorm_w, f_out_w, b_in_w, b_conv_w, b_conv_b, b_dt_bias, b_A_log, b_D, b_gnorm_w, b_out_w):
        import jax, jax.numpy as jnp
        import numpy as np
        from jax import lax
        D_MODEL = 256
        D_STATE = 128
        D_CONV = 4
        EXPAND = 2
        HEADDIM = 64
        D_INNER = EXPAND * D_MODEL
        NHEADS = D_INNER // HEADDIM
        D_IN_PROJ = 2 * D_INNER + 2 * D_STATE + NHEADS
        CONV_CH = D_INNER + 2 * D_STATE
        CHUNK = 128
        EPS = 1e-05
        BATCH, SEQ = (2, 512)

        def silu(x):
            return x * jax.nn.sigmoid(x)

        def rmsnorm(x, w):
            return x * lax.rsqrt(jnp.mean(x * x, axis=-1, keepdims=True) + EPS) * w

        def segsum(a):
            q = a.shape[-1]
            cs = jnp.cumsum(a, axis=-1)
            seg = cs[..., :, None] - cs[..., None, :]
            mask = jnp.tril(jnp.ones((q, q), dtype=bool))
            return jnp.where(mask, seg, -jnp.inf)

        def ssd(xh, dt, A, B, C):
            b, l, h, p = xh.shape
            n = B.shape[-1]
            c = l // CHUNK
            X = (xh * dt[..., None]).reshape(b, c, CHUNK, h, p)
            Adt = (A * dt).reshape(b, c, CHUNK, h).transpose(0, 3, 1, 2)
            Bc = B.reshape(b, c, CHUNK, n)
            Cc = C.reshape(b, c, CHUNK, n)
            Acs = jnp.cumsum(Adt, axis=-1)
            L = jnp.exp(segsum(Adt))
            Y_diag = jnp.einsum('bcln,bcsn,bhcls,bcshp->bclhp', Cc, Bc, L, X)
            decay_states = jnp.exp(Acs[..., -1:] - Acs)
            states = jnp.einsum('bcln,bhcl,bclhp->bchpn', Bc, decay_states, X)
            chunk_decay = jnp.exp(Acs[..., -1])

            def step(s, inp):
                st, cd = inp
                return (s * cd[:, :, None, None] + st, s)
            init = jnp.zeros((b, h, p, n), dtype=xh.dtype)
            _, prev = lax.scan(step, init, (states.transpose(1, 0, 2, 3, 4), chunk_decay.transpose(2, 0, 1)))
            Y_off = jnp.einsum('bcln,cbhpn,bhcl->bclhp', Cc, prev, jnp.exp(Acs))
            return (Y_diag + Y_off).reshape(b, l, h, p)

        def mamba2(x, in_w, conv_w, conv_b, dt_bias, A_log, D, gnorm_w, out_w):
            b, l, _ = x.shape
            zxbcdt = x @ in_w.T
            z = zxbcdt[..., :D_INNER]
            xBC = zxbcdt[..., D_INNER:D_INNER + CONV_CH]
            dt = jax.nn.softplus(zxbcdt[..., D_INNER + CONV_CH:] + dt_bias)
            xp = jnp.pad(xBC, ((0, 0), (D_CONV - 1, 0), (0, 0)))
            conv = sum((xp[:, k:k + l, :] * conv_w[:, k] for k in range(D_CONV))) + conv_b
            xBC = silu(conv)
            xs = xBC[..., :D_INNER]
            B = xBC[..., D_INNER:D_INNER + D_STATE]
            C = xBC[..., D_INNER + D_STATE:]
            A = -jnp.exp(A_log)
            xh = xs.reshape(b, l, NHEADS, HEADDIM)
            y = ssd(xh, dt, A, B, C) + xh * D[None, None, :, None]
            y = y.reshape(b, l, D_INNER)
            y = rmsnorm(y * silu(z), gnorm_w)
            return y @ out_w.T
        xn = rmsnorm(x, norm_w)
        y_fwd = mamba2(xn, f_in_w, f_conv_w, f_conv_b, f_dt_bias, f_A_log, f_D, f_gnorm_w, f_out_w)
        y_bwd = jnp.flip(mamba2(jnp.flip(xn, axis=1), b_in_w, b_conv_w, b_conv_b, b_dt_bias, b_A_log, b_D, b_gnorm_w, b_out_w), axis=1)
        out = jnp.concatenate([y_fwd, y_bwd], axis=-1) @ out_w_blk.T + out_b_blk
        return x + out

    def _L2_xattn_ref(x, context, Wq, Wk, Wv, Wout, bout):
        import jax, jax.numpy as jnp
        import numpy as np
        HEADS = 8
        DIM_HEAD = 64
        SCALE = DIM_HEAD ** (-0.5)
        b, n, _ = x.shape
        m = context.shape[1]
        q = (x @ Wq).reshape(b, n, HEADS, DIM_HEAD)
        k = (context @ Wk).reshape(b, m, HEADS, DIM_HEAD)
        v = (context @ Wv).reshape(b, m, HEADS, DIM_HEAD)
        sim = jnp.einsum('bihd,bjhd->bhij', q, k) * SCALE
        attn = jax.nn.softmax(sim, axis=-1)
        out = jnp.einsum('bhij,bjhd->bihd', attn, v).reshape(b, n, HEADS * DIM_HEAD)
        return out @ Wout + bout

    def _L2_ffn_ref(x, Wg, W1, W2):
        import jax, jax.numpy as jnp
        import numpy as np
        B, S, D = x.shape
        E = Wg.shape[1]
        T = B * S
        cap = max(1, T // E)
        xt = x.reshape(T, D)
        logits = xt @ Wg
        probs = jax.nn.softmax(logits, axis=-1)
        pT = probs.T
        _, top_idx = jax.lax.top_k(pT, cap)
        sel = jnp.zeros((E, T), dtype=bool).at[jnp.arange(E)[:, None], top_idx].set(True)
        masked = jnp.where(sel, pT, -jnp.inf)
        assigned = sel.any(axis=0)
        tok2exp = jnp.where(assigned, jnp.argmax(masked, axis=0), jnp.argmax(pT, axis=0))
        weights = jnp.take_along_axis(probs, tok2exp[:, None], axis=1)[:, 0]
        out = jnp.zeros_like(xt)
        for e in range(E):
            gate = jnp.where(tok2exp == e, weights, 0.0)
            h = jax.nn.gelu(xt @ W1[e], approximate=False) @ W2[e]
            out = out + gate[:, None] * h
        return out.reshape(B, S, D)

    def _L3_attn_ref(x, proj_w, proj_b, wq, wk):
        import jax, jax.numpy as jnp
        import numpy as np
        EMBED_DIM = 256
        NUM_HEADS = 16
        HEAD_DIM = EMBED_DIM // NUM_HEADS
        BATCH, SEQ = (2, 256)
        B, S, D = x.shape
        H, hd = (NUM_HEADS, HEAD_DIM)
        proj = jnp.einsum('bsd,ed->bse', x, proj_w) + proj_b
        flat = jnp.transpose(proj.reshape(B, S, H, hd), (2, 0, 1, 3)).reshape(H, B * S, hd)
        q = jnp.einsum('hnd,hde->hne', flat, wq)
        k = jnp.einsum('hnd,hde->hne', flat, wk)
        logits = jnp.einsum('hne,hme->hnm', q, k) / jnp.sqrt(jnp.asarray(D, x.dtype))
        attn = jax.nn.softmax(logits, axis=-1)
        out = jnp.einsum('hnm,hmd->hnd', attn, flat)
        out = jnp.transpose(out.reshape(H, B, S, hd), (1, 2, 0, 3)).reshape(B, S, D)
        return out

    def _L3_xattn_ref(x, context, Wq, Wk, Wv, Wo, bo):
        import jax, jax.numpy as jnp
        import numpy as np
        QUERY_DIM = 256
        CONTEXT_DIM = 192
        HEADS = 8
        DIM_HEAD = 64
        INNER = HEADS * DIM_HEAD
        B, S, _ = x.shape
        L = context.shape[1]
        scale = DIM_HEAD ** (-0.5)
        q = (x @ Wq).reshape(B, S, HEADS, DIM_HEAD).transpose(0, 2, 1, 3)
        k = (context @ Wk).reshape(B, L, HEADS, DIM_HEAD).transpose(0, 2, 1, 3)
        v = (context @ Wv).reshape(B, L, HEADS, DIM_HEAD).transpose(0, 2, 1, 3)
        attn = jnp.einsum('bhsd,bhld->bhsl', q, k) * scale
        attn = jax.nn.softmax(attn, axis=-1)
        out = jnp.einsum('bhsl,bhld->bhsd', attn, v)
        out = out.transpose(0, 2, 1, 3).reshape(B, S, INNER)
        return out @ Wo + bo

    def _L3_ffn_ref(hidden_states, W_fc, b_fc, A_fc, B_fc, W_proj, b_proj, A_proj, B_proj):
        import jax, jax.numpy as jnp
        import numpy as np
        BITS = 8
        LORA_RANK = 16
        LORA_ALPHA = 32
        SCALING = LORA_ALPHA / LORA_RANK

        def fake_quant_weight(w, bits=BITS):
            qmax = 2.0 ** (bits - 1) - 1
            scale = jnp.max(jnp.abs(w)) / qmax
            wq = jnp.clip(jnp.round(w / scale), -qmax - 1, qmax) * scale
            return w + jax.lax.stop_gradient(wq - w)

        def qat_lora_linear(x, W, b, A, B):
            Wq = fake_quant_weight(W)
            base = jnp.einsum('bsi,oi->bso', x, Wq) + b
            lora = jnp.einsum('bsr,or->bso', jnp.einsum('bsi,ri->bsr', x, A), B)
            return base + SCALING * lora
        h = qat_lora_linear(hidden_states, W_fc, b_fc, A_fc, B_fc)
        h = jax.nn.gelu(h, approximate=False)
        h = qat_lora_linear(h, W_proj, b_proj, A_proj, B_proj)
        return h
    x = x + _L0_attn_ref(_layernorm(x, axis=-1), L0_attn_Wq, L0_attn_bq, L0_attn_Wk, L0_attn_bk, L0_attn_Wv, L0_attn_bv, L0_attn_Wo, L0_attn_bo)
    x = x + _L0_xattn_ref(_layernorm(x, axis=-1), ctx_768, ctx_768, L0_xattn_Wq, L0_xattn_bq, L0_xattn_Wk, L0_xattn_bk, L0_xattn_Wv, L0_xattn_bv, L0_xattn_Wo, L0_xattn_bo, L0_xattn_ln_gamma, L0_xattn_ln_beta)
    x = x + _L0_ffn_ref(_layernorm(x, axis=-1), L0_ffn_Wr, L0_ffn_br, L0_ffn_Wg_s, L0_ffn_bg_s, L0_ffn_Wu_s, L0_ffn_bu_s, L0_ffn_Wd_s, L0_ffn_bd_s, L0_ffn_Wg, L0_ffn_bg, L0_ffn_Wu, L0_ffn_bu, L0_ffn_Wd, L0_ffn_bd)
    x = x + _L1_attn_ref(_layernorm(x, axis=-1), L1_attn_W_q, L1_attn_W_k, L1_attn_W_v, L1_attn_W_o, L1_attn_centers, L1_attn_log_scales, L1_attn_amplitudes)
    x = x + _L1_xattn_ref(_layernorm(x, axis=-1), ctx_768, L1_xattn_Wq, L1_xattn_Wk, L1_xattn_Wv, L1_xattn_Wo, L1_xattn_bo)
    x = x + _L1_ffn_ref(_layernorm(x, axis=-1), L1_ffn_w_gate, L1_ffn_w_up, L1_ffn_w_down)
    x = x + _L2_attn_ref(_layernorm(x, axis=-1), L2_attn_norm_w, L2_attn_out_w_blk, L2_attn_out_b_blk, L2_attn_f_in_w, L2_attn_f_conv_w, L2_attn_f_conv_b, L2_attn_f_dt_bias, L2_attn_f_A_log, L2_attn_f_D, L2_attn_f_gnorm_w, L2_attn_f_out_w, L2_attn_b_in_w, L2_attn_b_conv_w, L2_attn_b_conv_b, L2_attn_b_dt_bias, L2_attn_b_A_log, L2_attn_b_D, L2_attn_b_gnorm_w, L2_attn_b_out_w)
    x = x + _L2_xattn_ref(_layernorm(x, axis=-1), ctx_768, L2_xattn_Wq, L2_xattn_Wk, L2_xattn_Wv, L2_xattn_Wout, L2_xattn_bout)
    x = x + _L2_ffn_ref(_layernorm(x, axis=-1), L2_ffn_Wg, L2_ffn_W1, L2_ffn_W2)
    x = x + _L3_attn_ref(_layernorm(x, axis=-1), L3_attn_proj_w, L3_attn_proj_b, L3_attn_wq, L3_attn_wk)
    x = x + _L3_xattn_ref(_layernorm(x, axis=-1), ctx_768, L3_xattn_Wq, L3_xattn_Wk, L3_xattn_Wv, L3_xattn_Wo, L3_xattn_bo)
    x = x + _L3_ffn_ref(_layernorm(x, axis=-1), L3_ffn_W_fc, L3_ffn_b_fc, L3_ffn_A_fc, L3_ffn_B_fc, L3_ffn_W_proj, L3_ffn_b_proj, L3_ffn_A_proj, L3_ffn_B_proj)
    return x

_drawn_inputs = setup_inputs


def setup_inputs(seed=0):
    import zlib

    import numpy as np

    out = dict(_drawn_inputs(seed))
    spreads = {'L0_xattn_bq': (0.0, 0.1),
     'L0_xattn_bk': (0.0, 2.0),
     'L0_xattn_bv': (0.0, 0.1),
     'L0_xattn_bo': (0.0, 0.1),
     'L0_xattn_ln_gamma': (1.0, 0.2),
     'L0_xattn_ln_beta': (0.0, 0.1),
     'L0_ffn_br': (0.0, 0.1),
     'L0_ffn_bg_s': (0.0, 0.1),
     'L0_ffn_bu_s': (0.0, 0.1),
     'L0_ffn_bd_s': (0.0, 0.1),
     'L0_ffn_bg': (0.0, 0.601),
     'L0_ffn_bu': (0.0, 0.62),
     'L0_ffn_bd': (0.0, 0.353),
     'L1_xattn_bo': (0.0, 0.1),
     'L2_attn_norm_w': (1.0, 0.6),
     'L2_attn_out_b_blk': (0.0, 0.1),
     'L2_attn_f_conv_b': (0.0, 0.1),
     'L2_attn_f_D': (1.0, 0.6),
     'L2_attn_f_gnorm_w': (1.0, 0.6),
     'L2_attn_b_conv_b': (0.0, 0.1),
     'L2_attn_b_D': (1.0, 0.6),
     'L2_attn_b_gnorm_w': (1.0, 0.6),
     'L3_ffn_b_fc': (0.0, 0.291),
     'L3_ffn_B_fc': (0.0, 0.1),
     'L3_ffn_b_proj': (0.0, 0.268),
     'L3_ffn_B_proj': (0.0, 0.1)}
    factors = {'L0_attn_Wq': 8.0,
     'L0_attn_bq': 8.0,
     'L0_attn_Wk': 8.0,
     'L0_attn_bk': 64.0,
     'L0_attn_bv': 5.145,
     'L0_xattn_Wk': 8.0,
     'L1_attn_amplitudes': 4.723,
     'L2_attn_f_dt_bias': 8.0,
     'L2_attn_f_A_log': 8.0,
     'L2_attn_b_dt_bias': 8.0,
     'L2_attn_b_A_log': 8.0,
     'L2_xattn_bout': 8.0,
     'L2_ffn_Wg': 8.0,
     'L2_ffn_W1': 8.0,
     'L2_ffn_W2': 8.0,
     'L3_attn_proj_b': 27.528,
     'L3_xattn_bo': 29.243,
     'L3_attn_wq': 4.309,
     'L3_attn_wk': 4.497}
    for name, (base, spread) in spreads.items():
        noise = np.random.default_rng([zlib.crc32(name.encode()), seed]).standard_normal(out[name].shape)
        drawn = base * np.exp(spread * noise) if base else spread * noise
        out[name] = jnp.asarray(drawn.astype(out[name].dtype))
    for name, factor in factors.items():
        out[name] = (out[name] * factor).astype(out[name].dtype)
    return out
```

```python
from contextlib import ExitStack, contextmanager

import numpy as np

import concourse.bass as bass
from concourse import mybir

F32 = mybir.dt.float32
BF16 = mybir.dt.bfloat16
I32 = mybir.dt.int32
ALU = mybir.AluOpType
ACT = mybir.ActivationFunctionType
AX = mybir.AxisListType

P = 128
BATCH, SEQ, DIM = 16, 128, 256
KD = DIM // P
CTX = 192
GROUP = 4
GROUPS = BATCH // GROUP
GT = GROUP * SEQ
TOKENS = BATCH * SEQ
PAD = 32
LN_EPS = 1e-5
MAGIC = 12582912.0
CTX_ROWS = (P, CTX - P)
SIGNALS = 16


def sl(i, n=P):
    return slice(i * n, (i + 1) * n)


class Core:

    def __init__(self, nc, w):
        self.nc, self.w = nc, w
        self.turn = self.count = self.names = 0



@contextmanager
def phase(k, title, signals):
    nc = k.nc
    mine, other = k.banks[k.turn], k.banks[1 - k.turn]
    k.turn = 1 - k.turn
    k.count += 1
    with ExitStack() as stack:
        sems = {}
        for number, name in zip(mine, signals.split()):
            sems[name] = stack.enter_context(nc.semaphore(f"{title}{k.count}_{name}", num=number))
        with nc.Block() as block:
            @block.sync
            def _(sp):
                sp.sem_clear(range(other[0], other[-1] + 1))
            yield block, sems


class Link:

    def __init__(self, engine, sem):
        self.engine, self.sem, self.count = engine, sem, 0

    def __call__(self, instruction):
        instruction.then_inc(self.sem, 1)
        self.count += 1
        self.engine.wait_ge(self.sem, self.count)


def load_phase(k, pairs):
    with phase(k, "load", "loaded") as (block, s):
        @block.sync
        def _(sp):
            for dst, src in pairs:
                sp.dma_start(dst, src).then_inc(s["loaded"], 16)
            sp.wait_ge(s["loaded"], 16 * len(pairs))


def gemm_phase(k, title, jobs):
    nc = k.nc
    place, counts = [], {"act": 0, "dve": 0}
    for _, _, _, engine, _ in jobs:
        place.append((engine, counts[engine]))
        counts[engine] += 1

    with phase(k, title, "product_ready act_took dve_took") as (block, s):
        took = {"act": s["act_took"], "dve": s["dve_took"]}

        def bank(n):
            rows, columns = jobs[n][:2]
            return k.ps[0:rows, n % 8, 0:columns]

        @block.tensor
        def _(pe):
            for n, job in enumerate(jobs):
                if n >= 8:
                    engine, at = place[n - 8]
                    pe.wait_ge(took[engine], at + 1)
                job[2](nc, bank(n)).then_inc(s["product_ready"], 1)

        @block.scalar
        def _(act):
            for n, job in enumerate(jobs):
                if job[3] == "act":
                    act.wait_ge(s["product_ready"], n + 1)
                    job[4](nc, 'act', bank(n)).then_inc(s["act_took"], 1)

        @block.vector
        def _(dve):
            for n, job in enumerate(jobs):
                if job[3] == "dve":
                    dve.wait_ge(s["product_ready"], n + 1)
                    job[4](nc, 'dve', bank(n)).then_inc(s["dve_took"], 1)


def products(pairs):
    def fill(nc, bank):
        for i, (stationary, moving) in enumerate(pairs):
            last = nc.tensor.matmul(bank, stationary, moving, start=i == 0, stop=i == len(pairs) - 1)
        return last
    return fill


def turned(blocks, ident):
    def fill(nc, bank):
        if blocks[0].dtype == BF16:
            bank = bank.bitcast(BF16)
        for i, block in enumerate(blocks):
            last = nc.tensor.transpose(bank[:, sl(i)], block, ident)
        return last
    return fill


def to_copy(dst):
    def evacuate(nc, engine, bank):
        if engine == "act":
            return nc.scalar.activation(dst, bank, ACT.Copy)
        return nc.vector.tensor_copy(dst, bank)
    return evacuate


def to_bias(dst, bias):
    def evacuate(nc, engine, bank):
        if engine == "act":
            return nc.scalar.activation(dst, bank, ACT.Identity, bias=bias)
        return nc.vector.tensor_scalar(dst, bank, bias, None, ALU.add)
    return evacuate


def to_sum(dst, other):
    def evacuate(nc, engine, bank):
        return nc.vector.tensor_tensor(dst, bank, other, ALU.add)
    return evacuate


def turns(n):
    return "act" if n % 2 == 0 else "dve"


def feature_jobs(dst, weights, source, rows, width, bias=None, n0=0):
    jobs = []
    for m in range(width // P):
        pairs = [(weights[0:r, i, sl(m)], source[0:r, i, :]) for i, r in enumerate(rows)]
        out = dst[:, m, :]
        jobs.append((P, GT, products(pairs), turns(n0 + m), to_copy(out) if bias is None else to_bias(out, bias[:, m:m + 1])))
    return jobs


def token_pairs(k, source, rows, j, weights, columns, bias=None):
    pairs = [(source[0:r, i, sl(j)], weights[0:r, i, columns]) for i, r in enumerate(rows)]
    if bias is not None:
        pairs.append((k.ones[0:1, 0:P], bias[0:1, columns]))
    return products(pairs)


def residual_jobs(k, g, source, tiles, weights, bias=None):
    jobs = []
    for j in range(GROUP):
        x = k.x[:, bass.ds(g * GROUP + j, 1), :]
        jobs.append((P, DIM, token_pairs(k, source, [P] * tiles, j, weights, slice(0, DIM), bias), "dve",
                     lambda nc, engine, bank, x=x: nc.vector.tensor_tensor(x, bank.rearrange("p (o d) -> p o d", o=1), x, ALU.add)))
    return jobs


def row_stats(k, dve, link, source, measured):
    nc = k.nc
    for j in range(GROUP):
        last = nc.vector.bn_stats(k.stats[:, j, :], source(j))
    link(last)
    for j in range(GROUP):
        last = nc.vector.bn_aggr(k.moments[:, j, :], k.stats[:, j, :])
    link(last)
    link(nc.vector.tensor_scalar(k.rstd[:, :], k.moments[:, :, 1], LN_EPS, None, ALU.add))
    nc.vector.reciprocal(k.rstd[:, :], k.rstd[:, :]).then_inc(measured, 1)


def row_rstd(k, act, measured, rooted):
    act.wait_ge(measured, 1)
    k.nc.scalar.activation(k.rstd[:, :], k.rstd[:, :], ACT.Sqrt).then_inc(rooted, 1)


def norm_phase(k, g, dst):
    nc = k.nc

    def source(j):
        return k.x[:, bass.ds(g * GROUP + j, 1), :].rearrange("p o d -> p (o d)")

    with phase(k, "norm", "step measured rooted normed turned") as (block, s):
        @block.vector
        def _(dve):
            row_stats(k, dve, Link(dve, s["step"]), source, s["measured"])
            dve.wait_ge(s["rooted"], 1)
            for j in range(GROUP):
                nc.vector.tensor_scalar(k.normed[:, j, :], source(j), k.moments[:, j, 0:1], k.rstd[:, j:j + 1],
                                        ALU.subtract, ALU.mult).then_inc(s["normed"], 1)
            dve.wait_ge(s["turned"], GROUP)
            nc.vector.tensor_copy(dst(1), k.ps[:, 1, :])

        @block.tensor
        def _(pe):
            for j in range(GROUP):
                pe.wait_ge(s["normed"], j + 1)
                for kt in range(KD):
                    last = nc.tensor.transpose(k.ps[:, kt, sl(j)], k.normed[:, j, sl(kt)], k.ident[:, :])
                last.then_inc(s["turned"], 1)

        @block.scalar
        def _(act):
            row_rstd(k, act, s["measured"], s["rooted"])
            act.wait_ge(s["turned"], GROUP)
            nc.scalar.activation(dst(0), k.ps[:, 0, :], ACT.Copy)


def attention_phase(k, heads, width, q_of, k_of, v_of, out_of, scale, causal=False):
    nc = k.nc
    units = [(j, u) for j in range(GROUP) for u in range(heads // 4)]
    SB, WB, TB, OB = 3, 4, 2, 2
    per = P // width
    blocks = 4 * width // P

    def head(u, i):
        return (u // per * 4 + i) * per + u % per

    def scores(n):
        return k.ps[:, n % SB, :].rearrange("p (h t) -> p h t", h=4)

    def weights(n):
        return k.attn_w[:, n % WB, :, :]

    def turned(n):
        return k.ps[:, 3 + n % TB, :]

    def output(n):
        return k.ps[:, 5 + n % OB, 0:blocks * P]

    with phase(k, "attention", "scored step read summed exped scaled turned copied mixed taken") as (block, s):
        @block.tensor
        def _(pe):
            def score(n):
                if n >= SB:
                    pe.wait_ge(s["read"], n - SB + 1)
                j, u = units[n]
                for i in range(4):
                    last = nc.tensor.matmul(scores(n)[:, i, :], q_of(j, head(u, i)), k_of(j, head(u, i)), start=True, stop=True)
                last.then_inc(s["scored"], 1)

            def turn(n):
                pe.wait_ge(s["scaled"], n + 1)
                if n >= TB:
                    pe.wait_ge(s["copied"], n - TB + 1)
                for i in range(4):
                    last = nc.tensor.transpose(turned(n)[:, sl(i)], weights(n)[:, i, :], k.ident[:, :])
                last.then_inc(s["turned"], 1)

            def mix(n):
                pe.wait_ge(s["copied"], n + 1)
                if n >= OB:
                    pe.wait_ge(s["taken"], n - OB + 1)
                j, u = units[n]
                for i in range(4):
                    at = i * width
                    last = nc.tensor.matmul(output(n)[at % P:at % P + width, sl(at // P)], v_of(j, head(u, i)),
                                            k.attn_wT[:, n % TB, sl(i)], start=True, stop=True)
                last.then_inc(s["mixed"], 1)

            for n in range(len(units) + 3):
                if n < len(units):
                    score(n)
                if 0 <= n - 2 < len(units):
                    turn(n - 2)
                if 0 <= n - 3:
                    mix(n - 3)

        @block.vector
        def _(dve):
            link = Link(dve, s["step"])

            def subtract_max(n):
                dve.wait_ge(s["scored"], n + 1)
                if causal:
                    link(nc.vector.copy_predicated(scores(n), k.future[:, :, :], k.minus[:, :, :]))
                link(nc.vector.tensor_reduce(k.peak[:, n % WB, :], scores(n), AX.X, ALU.max))
                if n >= WB:
                    dve.wait_ge(s["turned"], n - WB + 1)
                nc.vector.tensor_tensor(weights(n), scores(n), k.peak[:, n % WB, :].unsqueeze(2).broadcast_to([P, 4, P]),
                                        ALU.subtract).then_inc(s["read"], 1)

            def total(n):
                dve.wait_ge(s["exped"], n + 1)
                link(nc.vector.tensor_reduce(k.total[:, n % WB, :], weights(n), AX.X, ALU.add))
                nc.vector.reciprocal(k.share[:, n % WB, :], k.total[:, n % WB, :]).then_inc(s["summed"], 1)

            def take(n):
                dve.wait_ge(s["mixed"], n + 1)
                j, u = units[n]
                nc.vector.tensor_copy(out_of(j, u), output(n).rearrange("p (b t) -> p b t", b=blocks)).then_inc(s["taken"], 1)

            for n in range(len(units) + 3):
                if n < len(units):
                    subtract_max(n)
                if 0 <= n - 1 < len(units):
                    total(n - 1)
                if 0 <= n - 3:
                    take(n - 3)

        @block.scalar
        def _(act):
            for n in range(len(units) + 2):
                if n < len(units):
                    act.wait_ge(s["read"], n + 1)
                    nc.scalar.activation(weights(n), weights(n), ACT.Exp, scale=scale).then_inc(s["exped"], 1)
                if n >= 2:
                    m = n - 2
                    act.wait_ge(s["turned"], m + 1)
                    if m >= TB:
                        act.wait_ge(s["mixed"], m - TB + 1)
                    nc.scalar.activation(k.attn_wT[:, m % TB, :], turned(m), ACT.Copy).then_inc(s["copied"], 1)

        @block.gpsimd
        def _(pool):
            for n in range(len(units)):
                pool.wait_ge(s["summed"], n + 1)
                nc.gpsimd.tensor_tensor(weights(n), weights(n), k.share[:, n % WB, :].unsqueeze(2).broadcast_to([P, 4, P]),
                                        ALU.mult).then_inc(s["scaled"], 1)


def attention_memory(k, stack):
    k.attn_w = sb(k, stack, "attn_w", [P, 4, 4, P])
    k.attn_wT = sb(k, stack, "attn_wT", [P, 2, 4 * P])
    k.peak, k.total, k.share = (sb(k, stack, f"attn_{name}", [P, 4, 4]) for name in ("peak", "total", "share"))


def sb(k, stack, name, shape, dtype=F32):
    k.names += 1
    return stack.enter_context(k.nc.sbuf_tensor(f"{name}_{k.names}", shape, dtype))


def rows_of(dram, tiles):
    return dram.rearrange("(t p) n -> p t n", p=P)


def ctx_weights(k, stack, name, width):
    w = sb(k, stack, name, [P, 2, width])
    dram = k.w[name]
    return w, [(w[0:P, 0, :], dram[0:P, :]), (w[0:CTX - P, 1, :], dram[P:CTX, :])]


def weights(k, stack, name, tiles, width):
    w = sb(k, stack, name, [P, tiles, width])
    return w, [(w[:, :, :], rows_of(k.w[name], tiles))]


def bias_row(k, stack, name, width):
    w = sb(k, stack, name, [1, width])
    return w, [(w[0:1, :], k.w[name])]


def bias_columns(k, stack, name, tiles):
    w = sb(k, stack, name, [P, tiles])
    return w, [(w[:, :], k.w[name])]


def l0_attn(k):
    nc = k.nc
    H, W = 16, 16 * PAD
    T = W // P
    with ExitStack() as stack:
        attention_memory(k, stack)
        wq, a = weights(k, stack, "L0_attn_Wq", KD, W)
        wk, b = weights(k, stack, "L0_attn_Wk", KD, W)
        wv, c = weights(k, stack, "L0_attn_Wv", KD, W)
        wo, d = weights(k, stack, "L0_attn_Wo", T, DIM)
        bq, e = bias_columns(k, stack, "L0_attn_bq", T)
        bk, f = bias_columns(k, stack, "L0_attn_bk", T)
        bv, g_ = bias_row(k, stack, "L0_attn_bv", W)
        bo, h_ = bias_row(k, stack, "L0_attn_bo", DIM)
        qT, kT, oT = (sb(k, stack, n, [P, T, GT]) for n in ("qT", "kT", "oT"))
        v = sb(k, stack, "v", [P, GROUP, W])
        k.future = sb(k, stack, "future", [P, 4, P], I32)
        k.minus = sb(k, stack, "minus", [P, 4, P])
        load_phase(k, a + b + c + d + e + f + g_ + h_ + [(k.future[:, :, :], k.w["future"])])
        with phase(k, "fill", "step") as (block, s):
            @block.vector
            def _(dve):
                nc.vector.memset(k.minus[:, :, :], -10000.0 * 4.0)
        with nc.Fori(0, GROUPS) as g:
            norm_phase(k, g, lambda kt: k.xT[:, kt, :])
            jobs = feature_jobs(qT, wq, k.xT, [P] * KD, W, bq) + feature_jobs(kT, wk, k.xT, [P] * KD, W, bk)
            jobs += [(P, W, token_pairs(k, k.xT, [P] * KD, j, wv, slice(0, W), bv), turns(j), to_copy(v[:, j, :]))
                     for j in range(GROUP)]
            gemm_phase(k, "qkv", jobs)

            def head(t):
                return lambda j, h: t[PAD * (h % 4):PAD * (h % 4) + PAD, h // 4, sl(j)]
            attention_phase(k, H, PAD, head(qT), head(kT), lambda j, h: v[:, j, sl(h, PAD)],
                            lambda j, u: oT[:, u:u + 1, sl(j)], 0.25, causal=True)
            gemm_phase(k, "project", residual_jobs(k, g, oT, T, wo, bo))


def cross_attention(k, layer, heads, wo_name, bo_name):
    nc = k.nc
    W = heads * 64
    T = W // P
    with ExitStack() as stack:
        attention_memory(k, stack)
        wq, a = weights(k, stack, f"{layer}_Wq", KD, W)
        wk, b = ctx_weights(k, stack, f"{layer}_Wk", W)
        wv, c = ctx_weights(k, stack, f"{layer}_Wv", W)
        wo, d = weights(k, stack, wo_name, T, DIM)
        bo, e = bias_row(k, stack, bo_name, DIM)
        qT, kT, oT = (sb(k, stack, n, [P, T, GT]) for n in ("qT", "kT", "oT"))
        v = sb(k, stack, "v", [P, GROUP, W])
        load_phase(k, a + b + c + d + e)
        with nc.Fori(0, GROUPS) as g:
            norm_phase(k, g, lambda kt: k.xT[:, kt, :])
            ctx_group_phase(k, g)
            jobs = feature_jobs(qT, wq, k.xT, [P] * KD, W) + feature_jobs(kT, wk, k.ctxG, CTX_ROWS, W)
            for j in range(GROUP):
                for c0 in range(0, W, 512):
                    jobs.append((P, 512, token_pairs(k, k.ctxG, CTX_ROWS, j, wv, slice(c0, c0 + 512)), turns(len(jobs)),
                                 to_copy(v[:, j, c0:c0 + 512])))
            gemm_phase(k, "qkv", jobs)

            def head(t):
                return lambda j, h: t[64 * (h % 2):64 * (h % 2) + 64, h // 2, sl(j)]
            attention_phase(k, heads, 64, head(qT), head(kT), lambda j, h: v[:, j, sl(h, 64)],
                            lambda j, u: oT[:, 2 * u:2 * u + 2, sl(j)], 0.125)
            gemm_phase(k, "project", residual_jobs(k, g, oT, T, wo, bo))
            empty_phase(k)


def empty_phase(k):
    with phase(k, "turn", "none") as (block, s):
        pass


def ctx_group_phase(k, g):
    nc = k.nc
    with phase(k, "context", "none") as (block, s):
        @block.vector
        def _(dve):
            nc.vector.tensor_copy(k.ctxG[:, 0, :], k.ctxT[:, 0, bass.ds(g * GT, GT)])

        @block.scalar
        def _(act):
            nc.scalar.activation(k.ctxG[0:CTX - P, 1, :], k.ctxT[0:CTX - P, 1, bass.ds(g * GT, GT)], ACT.Copy)


def l0_xattn(k):
    nc = k.nc
    H, W = 16, 16 * PAD
    T = W // P
    n = "L0_xattn_"
    with ExitStack() as stack:
        attention_memory(k, stack)
        wq, a = weights(k, stack, n + "Wq", KD, DIM)
        wk, b = ctx_weights(k, stack, n + "Wk", DIM)
        wv, c = ctx_weights(k, stack, n + "Wv", W)
        wo, d = weights(k, stack, n + "Wo", T, DIM)
        loads = a + b + c + d
        bq, bk, bo = (sb(k, stack, m, [1, DIM]) for m in ("bq", "bk", "bo"))
        bv = sb(k, stack, "bv", [1, W])
        gamma, beta = sb(k, stack, "gamma", [P, DIM]), sb(k, stack, "beta", [P, DIM])
        loads += [(bq[:, :], k.w[n + "bq"]), (bk[:, :], k.w[n + "bk"]), (bo[:, :], k.w[n + "bo"]), (bv[:, :], k.w[n + "bv"]),
                  (gamma[:, :], k.w[n + "ln_gamma"]), (beta[:, :], k.w[n + "ln_beta"])]
        qT, kT, oT = (sb(k, stack, m, [P, T, GT]) for m in ("qT", "kT", "oT"))
        v = sb(k, stack, "v", [P, GROUP, W])
        qp, kp, square, y = (sb(k, stack, m, [P, GROUP, DIM]) for m in ("qp", "kp", "square", "y"))
        padded = sb(k, stack, "padded", [P, 2, GROUP, W])
        length = sb(k, stack, "length", [P, 2, GROUP])
        load_phase(k, loads)
        with phase(k, "fill", "none") as (block, s):
            @block.vector
            def _(dve):
                nc.vector.memset(padded[:, :, :, :], 0.0)

        with nc.Fori(0, GROUPS) as g:
            norm_phase(k, g, lambda kt: k.xT[:, kt, :])
            ctx_group_phase(k, g)
            jobs = []
            for j in range(GROUP):
                jobs.append((P, DIM, token_pairs(k, k.xT, [P] * KD, j, wq, slice(0, DIM), bq), "act", to_copy(qp[:, j, :])))
                jobs.append((P, DIM, token_pairs(k, k.ctxG, CTX_ROWS, j, wk, slice(0, DIM), bk), "dve", to_copy(kp[:, j, :])))
                jobs.append((P, W, token_pairs(k, k.ctxG, CTX_ROWS, j, wv, slice(0, W), bv), "act", to_copy(v[:, j, :])))
            gemm_phase(k, "qkv", jobs)

            with phase(k, "unit", "step squared rooted unit turned copied") as (block, s):
                @block.vector
                def _(dve):
                    link = Link(dve, s["step"])
                    for i, rows in enumerate((qp, kp)):
                        for j in range(GROUP):
                            last = nc.vector.tensor_tensor_reduce(square[:, j, :], rows[:, j, :], rows[:, j, :], 1.0, 0.0,
                                                                  ALU.mult, ALU.add, length[:, i, j:j + 1])
                        if i == 0:
                            link(last)
                    last.then_inc(s["squared"], 1)
                    dve.wait_ge(s["rooted"], 1)
                    link(nc.vector.tensor_scalar(length[:, :, :], length[:, :, :], 1e-12, None, ALU.max))
                    link(nc.vector.reciprocal(length[:, :, :], length[:, :, :]))
                    for i, rows in enumerate((qp, kp)):
                        for j in range(GROUP):
                            nc.vector.tensor_scalar(padded[:, i, j, :].rearrange("p (h d) -> p h d", d=PAD)[:, :, 0:16],
                                                    rows[:, j, :].rearrange("p (h d) -> p h d", d=16),
                                                    length[:, i, j:j + 1], None, ALU.mult).then_inc(s["unit"], 1)
                    for m in range(T):
                        dve.wait_ge(s["turned"], T + m + 1)
                        nc.vector.tensor_copy(kT[:, m, :], k.ps[:, T + m, :])

                @block.scalar
                def _(act):
                    act.wait_ge(s["squared"], 1)
                    nc.scalar.activation(length[:, :, :], length[:, :, :], ACT.Sqrt).then_inc(s["rooted"], 1)
                    for m in range(T):
                        act.wait_ge(s["turned"], m + 1)
                        nc.scalar.activation(qT[:, m, :], k.ps[:, m, :], ACT.Copy)

                @block.tensor
                def _(pe):
                    for i in range(2):
                        pe.wait_ge(s["unit"], GROUP * (i + 1))
                        for m in range(T):
                            for j in range(GROUP):
                                last = nc.tensor.transpose(k.ps[:, T * i + m, sl(j)], padded[:, i, j, sl(m)], k.ident[:, :])
                            last.then_inc(s["turned"], 1)

            def head(t):
                return lambda j, h: t[PAD * (h % 4):PAD * (h % 4) + PAD, h // 4, sl(j)]
            attention_phase(k, H, PAD, head(qT), head(kT), lambda j, h: v[:, j, sl(h, PAD)],
                            lambda j, u: oT[:, u:u + 1, sl(j)], 0.25)
            gemm_phase(k, "project", [(P, DIM, token_pairs(k, oT, [P] * T, j, wo, slice(0, DIM), bo), "dve",
                                       to_sum(y[:, j, :], qp[:, j, :])) for j in range(GROUP)])

            with phase(k, "outer", "step measured rooted") as (block, s):
                @block.vector
                def _(dve):
                    link = Link(dve, s["step"])
                    row_stats(k, dve, link, lambda j: y[:, j, :], s["measured"])
                    dve.wait_ge(s["rooted"], 1)
                    for j in range(GROUP):
                        last = nc.vector.tensor_scalar(y[:, j, :], y[:, j, :], k.moments[:, j, 0:1], k.rstd[:, j:j + 1],
                                                       ALU.subtract, ALU.mult)
                    link(last)
                    link(nc.vector.tensor_tensor(y[:, :, :], y[:, :, :], gamma[:, :].unsqueeze(1).broadcast_to([P, GROUP, DIM]), ALU.mult))
                    link(nc.vector.tensor_tensor(y[:, :, :], y[:, :, :], beta[:, :].unsqueeze(1).broadcast_to([P, GROUP, DIM]), ALU.add))
                    x = k.x[:, bass.ds(g * GROUP, GROUP), :]
                    nc.vector.tensor_tensor(x, x, y[:, :, :], ALU.add)

                @block.scalar
                def _(act):
                    row_rstd(k, act, s["measured"], s["rooted"])
            empty_phase(k)


def keep_turned_phase(k, g, all_tokens):
    nc = k.nc
    with phase(k, "keep", "none") as (block, s):
        @block.vector
        def _(dve):
            nc.vector.tensor_copy(all_tokens[:, 0, bass.ds(g * GT, GT)], k.xT[:, 0, :])

        @block.scalar
        def _(act):
            nc.scalar.activation(all_tokens[:, 1, bass.ds(g * GT, GT)], k.xT[:, 1, :], ACT.Copy)


def l0_ffn(k):
    nc = k.nc
    E, TOP, INNER, SET = 32, 8, 128, 3
    SETS = (E + 1) // SET
    COLS = 2 * KD * INNER + DIM + 2
    n = "L0_ffn_"
    with ExitStack() as stack:
        wr, a = weights(k, stack, n + "Wr", KD, E)
        br, b = bias_row(k, stack, n + "br", E)
        bd = sb(k, stack, "bd", [E + 1, DIM])
        xA = sb(k, stack, "xA", [P, KD, TOKENS])
        share = sb(k, stack, "share", [P, BATCH, E + 1])
        affinity, rest = sb(k, stack, "affinity", [P, GROUP, E]), sb(k, stack, "rest", [P, GROUP, E])
        chosen = sb(k, stack, "chosen", [P, GROUP, E + 1])
        top, total = sb(k, stack, "top", [P, GROUP, TOP]), sb(k, stack, "total", [P, GROUP])
        chosenT = sb(k, stack, "chosenT", [E + 1, GROUP, P])
        experts = [sb(k, stack, f"experts{i}", [P, SET, COLS]) for i in range(2)]
        load_phase(k, a + b + [(bd[:, :], k.w[n + "bd"]), (experts[0][:, :, :], k.w[n + "experts"][0])])
        with phase(k, "fill", "none") as (block, s):
            @block.vector
            def _(dve):
                nc.vector.memset(chosen[:, :, :], 1.0)

        with nc.Fori(0, GROUPS) as g:
            norm_phase(k, g, lambda kt: k.xT[:, kt, :])
            keep_turned_phase(k, g, xA)

            def to_sigmoid(dst):
                return lambda nc, engine, bank: nc.scalar.activation(dst, bank, ACT.Sigmoid)
            gemm_phase(k, "router", [(P, E, token_pairs(k, k.xT, [P] * KD, j, wr, slice(0, E), br), "act",
                                      to_sigmoid(affinity[:, j, :])) for j in range(GROUP)])

            with phase(k, "choose", "step chosen") as (block, s):
                @block.vector
                def _(dve):
                    link = Link(dve, s["step"])
                    for j in range(GROUP):
                        last = nc.vector.max(top[:, j, :], affinity[:, j, :])
                    link(last)
                    for j in range(GROUP):
                        last = nc.vector.match_replace(rest[:, j, :], top[:, j, :], affinity[:, j, :], -1.0)
                    link(last)
                    link(nc.vector.tensor_reduce(total[:, :], top[:, :, :], AX.X, ALU.add))
                    link(nc.vector.tensor_scalar(total[:, :], total[:, :], 1e-9, None, ALU.add))
                    link(nc.vector.reciprocal(total[:, :], total[:, :]))
                    link(nc.vector.scalar_tensor_tensor(chosen[:, :, 0:E], rest[:, :, :], 0.0, affinity[:, :, :], ALU.is_lt, ALU.mult))
                    link(nc.vector.tensor_tensor(chosen[:, :, 0:E], chosen[:, :, 0:E],
                                                 total[:, :].unsqueeze(2).broadcast_to([P, GROUP, E]), ALU.mult))
                    nc.vector.tensor_copy(share[:, bass.ds(g * GROUP, GROUP), :], chosen[:, :, :])

            def turn_chosen(j):
                return lambda nc, bank: nc.tensor.transpose(bank, chosen[:, j, :], k.ident[:, :])
            gemm_phase(k, "turn", [(E + 1, P, turn_chosen(j), turns(j), to_copy(chosenT[:, j, :])) for j in range(GROUP)])

            jobs = []
            for j in range(GROUP):
                x = k.x[:, bass.ds(g * GROUP + j, 1), :]
                jobs.append((P, DIM, products([(chosenT[:, j, :], bd[:, :])]), "dve",
                             lambda nc, engine, bank, x=x: nc.vector.tensor_tensor(x, bank.rearrange("p (o d) -> p o d", o=1), x, ALU.add)))
            gemm_phase(k, "biases", jobs)

        with ExitStack() as inner:
            silu_gate = sb(k, inner, "silu_gate", [P, 2, GT])
            hidden = sb(k, inner, "hidden", [P, 2, GT])
            share_now = sb(k, inner, "share_now", [P, BATCH, SET])

            def set_phase(now, first, later=None):
                units = [(e, c) for e in range(SET) for c in range(GROUPS)]
                up_at = KD * INNER
                down_at = 2 * KD * INNER
                with phase(k, "experts", "loaded gated upped silued multiplied downed fetched added") as (block, s):
                    @block.sync
                    def _(sp):
                        if later is not None:
                            dst, index = later
                            sp.dma_start(dst[:, :, :].rearrange("p e c -> p (e c)"),
                                         k.w[n + "experts"].rearrange("i p e c -> (i p) (e c)")[bass.ds(index * P, P), :]).then_inc(s["loaded"], 16)
                            sp.wait_ge(s["loaded"], 16)

                    @block.tensor
                    def _(pe):
                        def down(m):
                            e, c = units[m]
                            pe.wait_ge(s["multiplied"], m + 1)
                            if m >= 2:
                                pe.wait_ge(s["added"], m - 1)
                            for j in range(GROUP):
                                last = nc.tensor.matmul(k.ps[:, 4 + 2 * (m % 2) + j // 2, sl(j % 2, DIM)], hidden[:, m % 2, sl(j)],
                                                        now[:, e, down_at:down_at + DIM], start=True, stop=True)
                            last.then_inc(s["downed"], 1)

                        for m, (e, c) in enumerate(units):
                            if m >= 2:
                                pe.wait_ge(s["silued"], m - 1)
                                pe.wait_ge(s["multiplied"], m - 1)
                            for at, base, sem in ((0, 0, s["gated"]), (up_at, 2, s["upped"])):
                                for kt in range(KD):
                                    last = nc.tensor.matmul(k.ps[:, base + m % 2, :], now[:, e, at + kt * INNER:at + (kt + 1) * INNER],
                                                            xA[:, kt, sl(c, GT)], start=kt == 0, stop=kt == KD - 1)
                                last.then_inc(sem, 1)
                            if m >= 1:
                                down(m - 1)
                        down(len(units) - 1)

                    @block.scalar
                    def _(act):
                        for m, (e, c) in enumerate(units):
                            act.wait_ge(s["gated"], m + 1)
                            if m >= 2:
                                act.wait_ge(s["multiplied"], m - 1)
                            nc.scalar.activation(silu_gate[:, m % 2, :], k.ps[:, m % 2, :], ACT.Silu,
                                                 bias=now[:, e, COLS - 2:COLS - 1]).then_inc(s["silued"], 1)

                    @block.vector
                    def _(dve):
                        nc.vector.tensor_copy(share_now[:, :, :], share[:, :, bass.ds(first, SET)]).then_inc(s["fetched"], 1)

                        def add(m):
                            e, c = units[m]
                            dve.wait_ge(s["downed"], m + 1)
                            if m == 0:
                                dve.wait_ge(s["fetched"], 1)
                            if m >= GROUPS:
                                dve.wait_ge(s["added"], m - GROUPS + 1)
                            for j in range(GROUP):
                                t = GROUP * c + j
                                last = nc.vector.scalar_tensor_tensor(k.x[:, t, :], k.ps[:, 4 + 2 * (m % 2) + j // 2, sl(j % 2, DIM)],
                                                                      share_now[:, t, e:e + 1], k.x[:, t, :], ALU.mult, ALU.add)
                            last.then_inc(s["added"], 1)

                        for m, (e, c) in enumerate(units):
                            dve.wait_ge(s["upped"], m + 1)
                            dve.wait_ge(s["silued"], m + 1)
                            if m >= 2:
                                dve.wait_ge(s["downed"], m - 1)
                            nc.vector.scalar_tensor_tensor(hidden[:, m % 2, :], k.ps[:, 2 + m % 2, :], now[:, e, COLS - 1:COLS],
                                                           silu_gate[:, m % 2, :], ALU.add, ALU.mult).then_inc(s["multiplied"], 1)
                            if m >= 1:
                                add(m - 1)
                        add(len(units) - 1)

            with nc.Fori(0, SETS // 2) as i:
                set_phase(experts[0], i * 2 * SET, (experts[1], 2 * i + 1))
                set_phase(experts[1], (2 * i + 1) * SET, (experts[0], 2 * i + 2))
            set_phase(experts[0], (SETS - 1) * SET)


def l2_ffn(k):
    nc = k.nc
    E, INNER, TOP = 8, 512, TOKENS // 8
    M = INNER // P
    n = "L2_ffn_"
    COLS = KD * INNER + M * DIM
    with ExitStack() as stack:
        wg, a = weights(k, stack, n + "Wg", KD, E)
        xA = sb(k, stack, "xA", [P, KD, TOKENS])
        share = sb(k, stack, "share", [P, BATCH, E])
        experts = [sb(k, stack, f"expert{i}", [P, COLS]) for i in range(2)]
        order = sb(k, stack, "order", [P, BATCH, E])
        logits = sb(k, stack, "logits", [P, GROUP, E])
        probs = sb(k, stack, "probs", [P, BATCH, E])
        load_phase(k, a + [(experts[0][:, :], k.w[n + "experts"][0]), (order[:, :, :], k.w["order"])])
        with nc.Fori(0, GROUPS) as g:
            norm_phase(k, g, lambda kt: k.xT[:, kt, :])
            keep_turned_phase(k, g, xA)
            gemm_phase(k, "router", [(P, E, token_pairs(k, k.xT, [P] * KD, j, wg, slice(0, E)), "act",
                                      to_copy(logits[:, j, :])) for j in range(GROUP)])
            with phase(k, "keep", "none") as (block, s):
                @block.vector
                def _(dve):
                    nc.vector.tensor_copy(probs[:, bass.ds(g * GROUP, GROUP), :], logits[:, :, :])

        with ExitStack() as inner:
            peak = sb(k, inner, "peak", [P, BATCH])
            first, second = sb(k, inner, "first", [P, BATCH, E]), sb(k, inner, "second", [P, BATCH, E])
            probsT, restT = sb(k, inner, "probsT", [E, TOKENS]), sb(k, inner, "restT", [E, TOKENS])
            best = sb(k, inner, "best", [E, 2, 8])
            all_e = [P, BATCH, E]

            def spread(t):
                return t[:, :].unsqueeze(2).broadcast_to(all_e)

            with phase(k, "softmax", "step shifted exped") as (block, s):
                @block.vector
                def _(dve):
                    link = Link(dve, s["step"])
                    link(nc.vector.tensor_reduce(peak[:, :], probs[:, :, :], AX.X, ALU.max))
                    nc.vector.tensor_tensor(first[:, :, :], probs[:, :, :], spread(peak), ALU.subtract).then_inc(s["shifted"], 1)
                    dve.wait_ge(s["exped"], 1)
                    link(nc.vector.tensor_reduce(peak[:, :], first[:, :, :], AX.X, ALU.add))
                    link(nc.vector.reciprocal(peak[:, :], peak[:, :]))
                    nc.vector.tensor_tensor(probs[:, :, :], first[:, :, :], spread(peak), ALU.mult)

                @block.scalar
                def _(act):
                    act.wait_ge(s["shifted"], 1)
                    nc.scalar.activation(first[:, :, :], first[:, :, :], ACT.Exp).then_inc(s["exped"], 1)

            def turn4(i, source, rows, columns):
                def fill(nc, bank):
                    for j in range(4):
                        last = nc.tensor.transpose(bank[:, j * columns:(j + 1) * columns], source(4 * i + j), k.ident[0:rows, 0:rows])
                    return last
                return fill
            gemm_phase(k, "turn", [(E, GT, turn4(i, lambda t: probs[:, t, :], P, P), turns(i), to_copy(probsT[:, sl(i, GT)]))
                                   for i in range(GROUPS)])

            with phase(k, "top", "step") as (block, s):
                @block.vector
                def _(dve):
                    link = Link(dve, s["step"])
                    for r in range(TOP // 8):
                        source = probsT if r == 0 else restT
                        link(nc.vector.max(best[:, r % 2, :], source[:, :]))
                        link(nc.vector.match_replace(restT[:, :], best[:, r % 2, :], source[:, :], -1.0))
            gemm_phase(k, "turn", [(P, 4 * E, turn4(i, lambda t: restT[:, sl(t)], E, E), turns(i),
                                    to_copy(first[:, sl(i, 4), :].rearrange("p t e -> p (t e)"))) for i in range(GROUPS)])

            with phase(k, "assign", "step") as (block, s):
                @block.vector
                def _(dve):
                    link = Link(dve, s["step"])
                    v = nc.vector
                    link(v.tensor_scalar(first[:, :, :], first[:, :, :], 0.0, None, ALU.is_lt))
                    link(v.tensor_reduce(peak[:, :], first[:, :, :], AX.X, ALU.max))
                    link(v.tensor_tensor(second[:, :, :], first[:, :, :], spread(peak), ALU.is_ge))
                    link(v.scalar_tensor_tensor(first[:, :, :], probs[:, :, :], 1.0, second[:, :, :], ALU.add, ALU.mult))
                    link(v.tensor_reduce(peak[:, :], first[:, :, :], AX.X, ALU.max))
                    link(v.tensor_tensor(second[:, :, :], first[:, :, :], spread(peak), ALU.is_equal))
                    link(v.tensor_tensor(second[:, :, :], second[:, :, :], order[:, :, :], ALU.mult))
                    link(v.tensor_reduce(peak[:, :], second[:, :, :], AX.X, ALU.max))
                    link(v.tensor_tensor(second[:, :, :], second[:, :, :], spread(peak), ALU.is_equal))
                    v.tensor_tensor(share[:, :, :], second[:, :, :], probs[:, :, :], ALU.mult)

        with ExitStack() as inner:
            hidden = sb(k, inner, "hidden", [P, 2, M, GT])
            share_now = sb(k, inner, "share_now", [P, BATCH])

            def expert_phase(now, e, later=None):
                with phase(k, "expert", "loaded upped gelued downed fetched added") as (block, s):
                    @block.sync
                    def _(sp):
                        if later is not None:
                            dst, index = later
                            sp.dma_start(dst[:, :], k.w[n + "experts"].rearrange("i p c -> (i p) c")[bass.ds(index * P, P), :]).then_inc(s["loaded"], 16)
                            sp.wait_ge(s["loaded"], 16)

                    @block.tensor
                    def _(pe):
                        def down(c):
                            pe.wait_ge(s["gelued"], M * (c + 1))
                            if c >= 2:
                                pe.wait_ge(s["added"], c - 1)
                            for j in range(GROUP):
                                for m in range(M):
                                    at = KD * INNER + m * DIM
                                    last = nc.tensor.matmul(k.ps[:, 4 + 2 * (c % 2) + j // 2, sl(j % 2, DIM)], hidden[:, c % 2, m, sl(j)],
                                                            now[:, at:at + DIM], start=m == 0, stop=m == M - 1)
                            last.then_inc(s["downed"], 1)

                        for c in range(GROUPS):
                            for m in range(M):
                                if c >= 1:
                                    pe.wait_ge(s["gelued"], M * (c - 1) + m + 1)
                                for kt in range(KD):
                                    at = kt * INNER + m * P
                                    last = nc.tensor.matmul(k.ps[:, m, :], now[:, at:at + P], xA[:, kt, sl(c, GT)],
                                                            start=kt == 0, stop=kt == KD - 1)
                                last.then_inc(s["upped"], 1)
                            if c >= 1:
                                down(c - 1)
                        down(GROUPS - 1)

                    @block.scalar
                    def _(act):
                        for c in range(GROUPS):
                            if c >= 2:
                                act.wait_ge(s["downed"], c - 1)
                            for m in range(M):
                                act.wait_ge(s["upped"], M * c + m + 1)
                                nc.scalar.activation(hidden[:, c % 2, m, :], k.ps[:, m, :], ACT.Gelu).then_inc(s["gelued"], 1)

                    @block.vector
                    def _(dve):
                        nc.vector.tensor_copy(share_now[:, :].unsqueeze(2), share[:, :, bass.ds(e, 1)]).then_inc(s["fetched"], 1)
                        dve.wait_ge(s["fetched"], 1)
                        for c in range(GROUPS):
                            dve.wait_ge(s["downed"], c + 1)
                            for j in range(GROUP):
                                t = GROUP * c + j
                                last = nc.vector.scalar_tensor_tensor(k.x[:, t, :], k.ps[:, 4 + 2 * (c % 2) + j // 2, sl(j % 2, DIM)],
                                                                      share_now[:, t:t + 1], k.x[:, t, :], ALU.mult, ALU.add)
                            last.then_inc(s["added"], 1)

            with nc.Fori(0, E // 2 - 1) as i:
                expert_phase(experts[0], 2 * i, (experts[1], 2 * i + 1))
                expert_phase(experts[1], 2 * i + 1, (experts[0], 2 * i + 2))
            expert_phase(experts[0], E - 2, (experts[1], E - 1))
            expert_phase(experts[1], E - 1)


def l3_ffn(k):
    nc = k.nc
    INNER, RANK = 1024, 16
    M = INNER // P
    n = "L3_ffn_"
    with ExitStack() as stack:
        wf, a = weights(k, stack, n + "W_fc", KD, INNER)
        wp, b = weights(k, stack, n + "W_proj", M, DIM)
        bf, c = bias_columns(k, stack, n + "b_fc", M)
        bp, d = bias_row(k, stack, n + "b_proj", DIM)
        af, bfT = sb(k, stack, "af", [RANK, DIM]), sb(k, stack, "bfT", [RANK, INNER])
        ap, bpT = sb(k, stack, "ap", [RANK, INNER]), sb(k, stack, "bpT", [RANK, DIM])
        load_phase(k, a + b + c + d + [(af[:, :], k.w[n + "A_fc"]), (bfT[:, :], k.w[n + "B_fc"]),
                                       (ap[:, :], k.w[n + "A_proj"]), (bpT[:, :], k.w[n + "B_proj"])])
        hT = sb(k, stack, "hT", [P, M, GT])
        size = sb(k, stack, "size", [P, 2, 4])
        row_ = sb(k, stack, "row", [1, 4])

        for which, w in enumerate((wf, wp)):
            flat = w[:, :, :]
            peak, step, inverse = size[:, which, 0:1], size[:, which, 1:2], size[:, which, 2:3]
            with phase(k, "round", "step peaked turned maxed spread") as (block, s):
                @block.vector
                def _(dve):
                    link = Link(dve, s["step"])
                    v = nc.vector
                    v.tensor_reduce(peak, w[:, :, :], AX.XY, ALU.max, apply_absolute_value=True).then_inc(s["peaked"], 1)
                    dve.wait_ge(s["turned"], 1)
                    link(v.tensor_reduce(row_[:, 0:1], k.ps[0:1, 0, 0:P], AX.X, ALU.max))
                    v.tensor_scalar(row_[:, 1:2], row_[:, 0:1], 1.0 / 127.0, None, ALU.mult).then_inc(s["maxed"], 1)
                    dve.wait_ge(s["spread"], 1)
                    link(v.tensor_copy(step, k.ps[:, 1, 0:1]))
                    link(v.reciprocal(inverse, step))
                    link(v.tensor_scalar(flat, flat, inverse, MAGIC, ALU.mult, ALU.add))
                    link(v.tensor_scalar(flat, flat, MAGIC, 127.0, ALU.subtract, ALU.min))
                    v.tensor_scalar(flat, flat, -128.0, step, ALU.max, ALU.mult)

                @block.tensor
                def _(pe):
                    pe.wait_ge(s["peaked"], 1)
                    nc.tensor.transpose(k.ps[0:1, 0, 0:P], peak, k.ident[:, :]).then_inc(s["turned"], 1)
                    pe.wait_ge(s["maxed"], 1)
                    nc.tensor.matmul(k.ps[:, 1, 0:1], k.ones[0:1, 0:P], row_[:, 1:2], start=True, stop=True).then_inc(s["spread"], 1)

        def to_twice(dst):
            return lambda nc, engine, bank: nc.vector.scalar_tensor_tensor(dst, bank, 2.0, dst, ALU.mult, ALU.add)
        jobs = [(P, 512, products([(af[:, sl(kt)], bfT[:, sl(c, 512)])]), "dve", to_twice(wf[:, kt, sl(c, 512)]))
                for kt in range(KD) for c in range(INNER // 512)]
        jobs += [(P, DIM, products([(ap[:, sl(m)], bpT[:, :])]), "dve", to_twice(wp[:, m, :])) for m in range(M)]
        gemm_phase(k, "lora", jobs)

        def to_gelu(m):
            return lambda nc, engine, bank: nc.scalar.activation(hT[:, m, :], bank, ACT.Gelu, bias=bf[:, m:m + 1])
        with nc.Fori(0, GROUPS) as g:
            norm_phase(k, g, lambda kt: k.xT[:, kt, :])
            gemm_phase(k, "up", [(P, GT, products([(wf[:, kt, sl(m)], k.xT[:, kt, :]) for kt in range(KD)]), "act", to_gelu(m))
                                 for m in range(M)])
            gemm_phase(k, "down", residual_jobs(k, g, hT, M, wp, bp))
            empty_phase(k)


def l1_attn(k):
    nc = k.nc
    H, D, C = 16, 16, 64
    PAIRS, T = H // 2, H * PAD // P
    VW = D + 1
    n = "L1_attn_"
    with ExitStack() as stack:
        wq, a = weights(k, stack, n + "W_q", KD, H * PAD)
        wk, b = weights(k, stack, n + "W_k", KD, H * PAD)
        wv, c = weights(k, stack, n + "W_v", KD, DIM)
        wo, d = weights(k, stack, n + "W_o", KD, DIM)
        centers, e = sb(k, stack, "centers", [P, PAIRS, P]), None
        where = sb(k, stack, "where", [P, PAIRS, P])
        scales, amplitude = sb(k, stack, "scales", [P, PAIRS]), sb(k, stack, "amplitude", [P, PAIRS])
        center2 = sb(k, stack, "center2", [P, PAIRS])
        qT, kT = (sb(k, stack, m, [P, T, GT]) for m in ("qT", "kT"))
        square = [sb(k, stack, f"square{i}", [P, T, GT]) for i in range(2)]
        near = [sb(k, stack, f"near{i}", [P, PAIRS, GT]) for i in range(2)]
        keysT = sb(k, stack, "keysT", [P, GROUP, PAIRS, P])
        values = sb(k, stack, "values", [P, GROUP, H, VW])
        pooled = sb(k, stack, "pooled", [P, GROUP, PAIRS, 2 * VW])
        share = sb(k, stack, "share", [P, GROUP, H])
        mixed = sb(k, stack, "mixed", [P, GROUP, DIM])
        oT = sb(k, stack, "oT", [P, KD, GT])
        load_phase(k, a + b + c + d + [(centers[:, :, :], k.w[n + "centers"]), (where[:, :, :], k.w[n + "where"]),
                                       (scales[:, :], k.w[n + "log_scales"]), (amplitude[:, :], k.w[n + "amplitudes"])])
        with phase(k, "centers", "step exped squared summed") as (block, s):
            @block.vector
            def _(dve):
                link = Link(dve, s["step"])
                v = nc.vector
                v.tensor_tensor(near[0][:, :, 0:P], centers[:, :, :], centers[:, :, :], ALU.mult).then_inc(s["squared"], 1)
                v.memset(values[:, :, :, :], 1.0)
                v.memset(pooled[:, :, :, :], 0.0)
                dve.wait_ge(s["exped"], 1)
                link(v.tensor_scalar(scales[:, :], scales[:, :], 1e-3, None, ALU.max))
                link(v.tensor_tensor(scales[:, :], scales[:, :], scales[:, :], ALU.mult))
                link(v.reciprocal(scales[:, :], scales[:, :]))
                v.tensor_scalar(scales[:, :], scales[:, :], -0.5, None, ALU.mult)
                v.tensor_tensor(amplitude[:, :], amplitude[:, :], amplitude[:, :], ALU.mult)
                dve.wait_ge(s["summed"], 1)
                v.tensor_copy(center2[:, :], k.ps[:, 0, 0:PAIRS])
                v.tensor_scalar(centers[:, :, :], centers[:, :, :], -2.0, None, ALU.mult)

            @block.scalar
            def _(act):
                nc.scalar.activation(scales[:, :], scales[:, :], ACT.Exp).then_inc(s["exped"], 1)

            @block.tensor
            def _(pe):
                pe.wait_ge(s["squared"], 1)
                for p in range(PAIRS):
                    last = nc.tensor.matmul(k.ps[:, 0, p:p + 1], near[0][:, p, 0:P], k.ones[:, 0:1], start=True, stop=True)
                last.then_inc(s["summed"], 1)

        with nc.Fori(0, GROUPS) as g:
            norm_phase(k, g, lambda kt: k.xT[:, kt, :])
            jobs = feature_jobs(qT, wq, k.xT, [P] * KD, H * PAD) + feature_jobs(kT, wk, k.xT, [P] * KD, H * PAD)

            def to_values(j):
                def evacuate(nc, engine, bank):
                    source, dst = bank.rearrange("p (h d) -> p h d", d=D), values[:, j, :, 0:D]
                    if engine == "act":
                        return nc.scalar.activation(dst, source, ACT.Copy)
                    return nc.vector.tensor_copy(dst, source)
                return evacuate
            jobs += [(P, DIM, token_pairs(k, k.xT, [P] * KD, j, wv, slice(0, DIM)), turns(j), to_values(j)) for j in range(GROUP)]
            gemm_phase(k, "qkv", jobs)

            with phase(k, "affinity", "squared keys_squared measured bounded") as (block, s):
                jobs = [(side, p) for side in range(2) for p in range(PAIRS)]

                @block.scalar
                def _(act):
                    nc.scalar.activation(square[0][:, :, :], qT[:, :, :], ACT.Square).then_inc(s["squared"], 1)
                    for m, (side, p) in enumerate(jobs):
                        act.wait_ge(s["bounded"], m + 1)
                        nc.scalar.activation(near[side][:, p, :], near[side][:, p, :], ACT.Exp, scale=scales[:, p:p + 1])

                @block.gpsimd
                def _(pool):
                    nc.gpsimd.tensor_tensor(square[1][:, :, :], kT[:, :, :], kT[:, :, :], ALU.mult).then_inc(s["keys_squared"], 1)

                @block.tensor
                def _(pe):
                    for m, (side, p) in enumerate(jobs):
                        if p == 0:
                            pe.wait_ge((s["squared"], s["keys_squared"])[side], 1)
                        if m >= 8:
                            pe.wait_ge(s["bounded"], m - 7)
                        source = (qT, kT)[side]
                        nc.tensor.matmul(k.ps[:, m % 8, :], centers[:, p, :], source[:, p // 2, :], start=True, stop=False)
                        nc.tensor.matmul(k.ps[:, m % 8, :], where[:, p, :], square[side][:, p // 2, :],
                                         start=False, stop=True).then_inc(s["measured"], 1)

                @block.vector
                def _(dve):
                    for m, (side, p) in enumerate(jobs):
                        dve.wait_ge(s["measured"], m + 1)
                        nc.vector.tensor_scalar(near[side][:, p, :], k.ps[:, m % 8, :], center2[:, p:p + 1], 0.0,
                                                ALU.add, ALU.max).then_inc(s["bounded"], 1)

            gemm_phase(k, "turn", [(P, GT, turned([near[1][:, 4 * i + p, sl(j)] for p in range(4)], k.ident[:, :]),
                                    turns(i), to_copy(keysT[:, j, sl(i, 4), :].rearrange("p a b -> p (a b)")))
                                   for j in range(GROUP) for i in range(PAIRS // 4)])

            def pool_values(j):
                def fill(nc, bank):
                    for p in range(PAIRS):
                        last = nc.tensor.matmul(bank[:, sl(p, 2 * VW)], keysT[:, j, p, :],
                                                values[:, j, sl(p, 2), :].rearrange("p h d -> p (h d)"), start=True, stop=True)
                    return last
                return fill

            def to_pooled(j):
                def evacuate(nc, engine, bank):
                    for i in range(2):
                        rows = slice(C * i, C * i + C)
                        source = bank[rows, :].rearrange("p (a d) -> p a d", d=2 * VW)[:, :, sl(i, VW)]
                        last = nc.vector.tensor_tensor(pooled[rows, j, :, sl(i, VW)], source,
                                                       amplitude[rows, :].unsqueeze(2).broadcast_to([C, PAIRS, VW]), ALU.mult)
                    return last
                return evacuate
            gemm_phase(k, "pool", [(P, H * VW, pool_values(j), "dve", to_pooled(j)) for j in range(GROUP)])

            with phase(k, "mix", "step mixed divided turned") as (block, s):
                @block.tensor
                def _(pe):
                    for j in range(GROUP):
                        for p in range(PAIRS):
                            last = nc.tensor.matmul(k.ps[:, j, sl(p, 2 * VW)], near[0][:, p, sl(j)], pooled[:, j, p, :], start=True, stop=True)
                        last.then_inc(s["mixed"], 1)
                    for j in range(GROUP):
                        pe.wait_ge(s["divided"], j + 1)
                        for kt in range(KD):
                            last = nc.tensor.transpose(k.ps[:, 4 + kt, sl(j)], mixed[:, j, sl(kt)], k.ident[:, :])
                        last.then_inc(s["turned"], 1)

                @block.vector
                def _(dve):
                    link = Link(dve, s["step"])
                    for j in range(GROUP):
                        dve.wait_ge(s["mixed"], j + 1)
                        bank = k.ps[:, j, 0:H * VW].rearrange("p (h d) -> p h d", d=VW)
                        link(nc.vector.tensor_scalar(share[:, j, :].unsqueeze(2), bank[:, :, D:VW], 1e-6, None, ALU.add))
                        link(nc.vector.reciprocal(share[:, j, :], share[:, j, :]))
                        nc.vector.tensor_tensor(mixed[:, j, :].rearrange("p (h d) -> p h d", d=D), bank[:, :, 0:D],
                                                share[:, j, :].unsqueeze(2).broadcast_to([P, H, D]), ALU.mult).then_inc(s["divided"], 1)
                    dve.wait_ge(s["turned"], GROUP)
                    nc.vector.tensor_copy(oT[:, 1, :], k.ps[:, 5, :])

                @block.scalar
                def _(act):
                    act.wait_ge(s["turned"], GROUP)
                    nc.scalar.activation(oT[:, 0, :], k.ps[:, 4, :], ACT.Copy)
            gemm_phase(k, "project", residual_jobs(k, g, oT, KD, wo))
            empty_phase(k)


def l1_ffn(k):
    nc = k.nc
    INNER = 1024
    M = INNER // P
    n = "L1_ffn_"
    with ExitStack() as stack:
        wg, a = weights(k, stack, n + "w_gate", KD, INNER)
        wu, b = weights(k, stack, n + "w_up", KD, INNER)
        wd, c = weights(k, stack, n + "w_down", M, DIM)
        ternary = [sb(k, stack, f"ternary{i}", [P, 2 * INNER], BF16) for i in range(3)]
        size = sb(k, stack, "size", [P, 3, 3])
        identb = sb(k, stack, "identb", [P, P], BF16)
        rows = sb(k, stack, "rows", [P, GROUP, INNER])
        gate = sb(k, stack, "gate", [P, GROUP, INNER])
        rounded = sb(k, stack, "rounded", [P, GROUP, INNER], BF16)
        roundedT = sb(k, stack, "roundedT", [P, M, GT], BF16)
        peak, inverse = sb(k, stack, "peak", [P, GROUP]), sb(k, stack, "inverse", [P, GROUP])
        factor = sb(k, stack, "factor", [P, 3, GROUP])
        load_phase(k, a + b + c)
        flat = [w[:, :, :].rearrange("p a b -> p (a b)") for w in (wg, wu, wd)]
        with phase(k, "ternary", "step summed spread") as (block, s):
            @block.vector
            def _(dve):
                link = Link(dve, s["step"])
                v = nc.vector
                v.tensor_copy(identb[:, :], k.ident[:, :])
                for i in range(3):
                    last = v.tensor_reduce(size[:, i, 0:1], flat[i], AX.X, ALU.add, apply_absolute_value=True)
                last.then_inc(s["summed"], 1)
                dve.wait_ge(s["spread"], 1)
                link(v.tensor_scalar(size[:, :, 1], k.ps[:, 0, 0:3], 1.0 / (DIM * INNER), 1e-5, ALU.mult, ALU.max))
                link(v.reciprocal(size[:, :, 2], size[:, :, 1]))
                for i in range(3):
                    link(v.tensor_scalar(flat[i], flat[i], size[:, i, 2:3], MAGIC, ALU.mult, ALU.add))
                    link(v.tensor_scalar(flat[i], flat[i], MAGIC, 1.0, ALU.subtract, ALU.min))
                    v.tensor_scalar(ternary[i][:, :], flat[i], -1.0, None, ALU.max)

            @block.tensor
            def _(pe):
                pe.wait_ge(s["summed"], 1)
                nc.tensor.matmul(k.ps[:, 0, 0:3], k.ones[:, :], size[:, :, 0], start=True, stop=True).then_inc(s["spread"], 1)

        def round_rows(dve, link, source, width):
            v = nc.vector
            rows_ = source[:, :, 0:width]
            link(v.tensor_reduce(peak[:, :], rows_, AX.X, ALU.max, apply_absolute_value=True))
            link(v.tensor_scalar(peak[:, :], peak[:, :], 1e-5, None, ALU.max))
            link(v.reciprocal(inverse[:, :], peak[:, :]))
            link(v.tensor_scalar(inverse[:, :], inverse[:, :], 127.0, None, ALU.mult))
            for j in range(GROUP):
                last = v.tensor_scalar(source[:, j, 0:width], source[:, j, 0:width], inverse[:, j:j + 1], MAGIC, ALU.mult, ALU.add)
            link(last)
            link(v.tensor_scalar(rounded[:, :, 0:width], rows_, MAGIC, 127.0, ALU.subtract, ALU.min))
            for i in range(3):
                last = v.tensor_scalar(factor[:, i, :], peak[:, :], 1.0 / 127.0, size[:, i, 1:2], ALU.mult, ALU.mult)
            link(last)

        def turn_jobs(width):
            return [(P, GT // 2, turned([rounded[:, j, sl(m)] for j in range(GROUP)], identb[:, :]), turns(m),
                     lambda nc, engine, bank, m=m: to_copy(roundedT[:, m, :])(nc, engine, bank.bitcast(BF16)))
                    for m in range(width // P)]

        with nc.Fori(0, GROUPS) as g:
            with phase(k, "norm", "step measured rooted") as (block, s):
                def source(j):
                    return k.x[:, bass.ds(g * GROUP + j, 1), :].rearrange("p o d -> p (o d)")

                @block.vector
                def _(dve):
                    link = Link(dve, s["step"])
                    row_stats(k, dve, link, source, s["measured"])
                    dve.wait_ge(s["rooted"], 1)
                    for j in range(GROUP):
                        last = nc.vector.tensor_scalar(k.normed[:, j, :], source(j), k.moments[:, j, 0:1], k.rstd[:, j:j + 1],
                                                       ALU.subtract, ALU.mult)
                    link(last)
                    round_rows(dve, link, k.normed, DIM)

                @block.scalar
                def _(act):
                    row_rstd(k, act, s["measured"], s["rooted"])
            gemm_phase(k, "turn", turn_jobs(DIM))

            with phase(k, "up", "gated upped silued multiplied") as (block, s):
                units = [(j, c) for j in range(GROUP) for c in range(INNER // 512)]

                @block.tensor
                def _(pe):
                    for m, (j, c) in enumerate(units):
                        if m >= 4:
                            pe.wait_ge(s["silued"], m - 3)
                            pe.wait_ge(s["multiplied"], m - 3)
                        for i, sem in enumerate((s["gated"], s["upped"])):
                            for kt in range(KD):
                                last = nc.tensor.matmul(k.ps[:, 4 * i + m % 4, :], roundedT[:, kt, sl(j)],
                                                        ternary[i][:, kt * INNER + c * 512:kt * INNER + (c + 1) * 512],
                                                        start=kt == 0, stop=kt == KD - 1)
                            last.then_inc(sem, 1)

                @block.scalar
                def _(act):
                    for m, (j, c) in enumerate(units):
                        act.wait_ge(s["gated"], m + 1)
                        nc.scalar.activation(gate[:, j, sl(c, 512)], k.ps[:, m % 4, :], ACT.Silu,
                                             scale=factor[:, 0, j:j + 1]).then_inc(s["silued"], 1)

                @block.vector
                def _(dve):
                    for m, (j, c) in enumerate(units):
                        dve.wait_ge(s["upped"], m + 1)
                        dve.wait_ge(s["silued"], m + 1)
                        nc.vector.scalar_tensor_tensor(rows[:, j, sl(c, 512)], k.ps[:, 4 + m % 4, :], factor[:, 1, j:j + 1],
                                                       gate[:, j, sl(c, 512)], ALU.mult, ALU.mult).then_inc(s["multiplied"], 1)

            with phase(k, "round", "step") as (block, s):
                @block.vector
                def _(dve):
                    round_rows(dve, Link(dve, s["step"]), rows, INNER)
            gemm_phase(k, "turn", turn_jobs(INNER))

            jobs = []
            for j in range(GROUP):
                x = k.x[:, bass.ds(g * GROUP + j, 1), :]
                jobs.append((P, DIM, products([(roundedT[:, m, sl(j)], ternary[2][:, sl(m, DIM)]) for m in range(M)]), "dve",
                             lambda nc, engine, bank, x=x, j=j: nc.vector.scalar_tensor_tensor(
                                 x, bank.rearrange("p (o d) -> p o d", o=1), factor[:, 2, j:j + 1], x, ALU.mult, ALU.add)))
            gemm_phase(k, "down", jobs)


def l2_attn(k):
    nc = k.nc
    INNER, STATE, HEADS, WIDTH, TAPS = 512, 128, 8, 64, 4
    M, CH = INNER // P, (INNER + 2 * STATE) // P
    COLS = 2 * INNER + 2 * STATE + HEADS
    LONG = SEQ + TAPS - 1
    n = "L2_attn_"
    ways = "fb"
    with ExitStack() as stack:
        in_w = {d: weights(k, stack, f"{n}{d}_in_w", KD, COLS) for d in ways}
        folded = {d: sb(k, stack, f"folded_{d}", [P, M, DIM]) for d in ways}
        small = {}
        loads = []
        for d in ways:
            loads += in_w[d][1]
            for name, shape in (("conv_w", [P, CH, TAPS]), ("conv_b", [P, CH]), ("A", [P, HEADS]), ("D", [P, HEADS]),
                                ("dt_bias", [1, HEADS]), ("mask", [P, P])):
                small[d, name] = sb(k, stack, f"{name}_{d}", shape)
                loads.append((small[d, name][tuple(slice(None) for _ in shape)], k.w[f"{n}{d}_{name}"]))
        norm_w, a = bias_columns(k, stack, n + "norm_w", KD)
        out_b, b = bias_row(k, stack, n + "out_b", DIM)
        select = sb(k, stack, "select", [HEADS, HEADS, P])
        loads += a + b + [(select[:, :, :], k.w[n + "select"])]
        with ExitStack() as inner:
            out_w = {d: weights(k, inner, f"{n}{d}_out_w", KD, INNER) for d in ways}
            block_w = {d: weights(k, inner, f"{n}{d}_block_w", KD, DIM) for d in ways}
            gnorm = {d: bias_columns(k, inner, f"{n}{d}_gnorm_w", M) for d in ways}
            for d in ways:
                loads += out_w[d][1] + block_w[d][1] + gnorm[d][1]
            load_phase(k, loads)

            def to_scaled(dst, scale):
                return lambda nc, engine, bank: nc.vector.tensor_scalar(dst, bank, scale, None, ALU.mult)
            gemm_phase(k, "fold", [(P, DIM, products([(out_w[d][0][:, kt, sl(m)], block_w[d][0][:, kt, :]) for kt in range(KD)]),
                                    "dve", to_scaled(folded[d][:, m, :], gnorm[d][0][:, m:m + 1])) for d in ways for m in range(M)])

        square = sb(k, stack, "square", [P, DIM])
        around = {d: sb(k, stack, f"around_{d}", [P, CH, GROUP, LONG]) for d in ways}
        conved = sb(k, stack, "conved", [P, CH, GT])
        gate = sb(k, stack, "gate", [P, GROUP, INNER])
        raw, dt, decay, e, u, miss, late, total = (sb(k, stack, m, [P, GROUP, HEADS])
                                                   for m in ("raw", "dt", "decay", "e", "u", "miss", "late", "total"))
        totalT = sb(k, stack, "totalT", [HEADS, GT])
        pairs = sb(k, stack, "pairs", [P, GROUP, P])
        inputs, skipped = sb(k, stack, "inputs", [P, GROUP, INNER]), sb(k, stack, "skipped", [P, GROUP, INNER])
        LB = 4
        lasting = sb(k, stack, "lasting", [P, LB, GROUP, P])
        y = sb(k, stack, "y", [P, GROUP, INNER])
        yT = {d: sb(k, stack, f"yT_{d}", [P, M, GT]) for d in ways}
        with phase(k, "rates", "exped") as (block, s):
            @block.scalar
            def _(act):
                for d in ways:
                    last = nc.scalar.activation(small[d, "A"][:, :], small[d, "A"][:, :], ACT.Exp)
                last.then_inc(s["exped"], 1)

            @block.vector
            def _(dve):
                for d in ways:
                    nc.vector.memset(around[d][:, :, :, :], 0.0)
                dve.wait_ge(s["exped"], 1)
                for d in ways:
                    nc.vector.tensor_scalar(small[d, "A"][:, :], small[d, "A"][:, :], -1.0, None, ALU.mult)

        with nc.Fori(0, GROUPS) as g:
            with phase(k, "norm", "step measured rooted squared rooted2 normed turned") as (block, s):
                x4 = k.x[:, bass.ds(g * GROUP, GROUP), :]

                def source(j):
                    return k.x[:, bass.ds(g * GROUP + j, 1), :].rearrange("p o d -> p (o d)")

                @block.vector
                def _(dve):
                    link = Link(dve, s["step"])
                    row_stats(k, dve, link, source, s["measured"])
                    dve.wait_ge(s["rooted"], 1)
                    for j in range(GROUP):
                        last = nc.vector.tensor_scalar(k.normed[:, j, :], source(j), k.moments[:, j, 0:1], k.rstd[:, j:j + 1],
                                                       ALU.subtract, ALU.mult)
                    link(last)
                    nc.vector.tensor_tensor(x4, x4, k.normed[:, :, :], ALU.add)
                    for j in range(GROUP):
                        last = nc.vector.tensor_tensor_reduce(y[:, j, 0:DIM], k.normed[:, j, :], k.normed[:, j, :], 1.0, 0.0,
                                                              ALU.mult, ALU.add, k.rstd[:, j:j + 1])
                    link(last)
                    link(nc.vector.tensor_scalar(k.rstd[:, :], k.rstd[:, :], 1.0 / DIM, LN_EPS, ALU.mult, ALU.add))
                    nc.vector.reciprocal(k.rstd[:, :], k.rstd[:, :]).then_inc(s["squared"], 1)
                    dve.wait_ge(s["rooted2"], 1)
                    for j in range(GROUP):
                        nc.vector.tensor_scalar(k.normed[:, j, :], k.normed[:, j, :], k.rstd[:, j:j + 1], None, ALU.mult).then_inc(s["normed"], 1)
                    dve.wait_ge(s["turned"], GROUP)
                    nc.vector.tensor_scalar(k.xT[:, 1, :], k.ps[:, 1, :], norm_w[:, 1:2], None, ALU.mult)

                @block.scalar
                def _(act):
                    row_rstd(k, act, s["measured"], s["rooted"])
                    row_rstd(k, act, s["squared"], s["rooted2"])
                    act.wait_ge(s["turned"], GROUP)
                    nc.scalar.activation(k.xT[:, 0, :], k.ps[:, 0, :], ACT.Copy, scale=norm_w[:, 0:1])

                @block.tensor
                def _(pe):
                    for j in range(GROUP):
                        pe.wait_ge(s["normed"], j + 1)
                        for kt in range(KD):
                            last = nc.tensor.transpose(k.ps[:, kt, sl(j)], k.normed[:, j, sl(kt)], k.ident[:, :])
                        last.then_inc(s["turned"], 1)

            for d in ways:
                w = in_w[d][0]
                lead = TAPS - 1 if d == "f" else 0

                def to_silu(dst):
                    return lambda nc, engine, bank: nc.scalar.activation(dst, bank, ACT.Silu)

                def to_around(m):
                    return lambda nc, engine, bank: nc.vector.tensor_copy(around[d][:, m, :, lead:lead + SEQ],
                                                                          bank.rearrange("p (j t) -> p j t", j=GROUP))
                jobs = []
                for j in range(GROUP):
                    jobs.append((P, INNER, token_pairs(k, k.xT, [P] * KD, j, w, slice(0, INNER)), "act", to_silu(gate[:, j, :])))
                    pairs_dt = [(k.xT[:, kt, sl(j)], w[:, kt, COLS - HEADS:COLS]) for kt in range(KD)]
                    pairs_dt.append((k.ones[0:1, 0:P], small[d, "dt_bias"][0:1, :]))
                    jobs.append((P, HEADS, products(pairs_dt), "dve", to_copy(raw[:, j, :])))
                for m in range(CH):
                    jobs.append((P, GT, products([(w[:, kt, INNER + m * P:INNER + (m + 1) * P], k.xT[:, kt, :]) for kt in range(KD)]),
                                 "dve", to_around(m)))
                gemm_phase(k, "in", jobs)

                with phase(k, "conv", "step sized exped plussed logged conved") as (block, s):
                    @block.vector
                    def _(dve):
                        link = Link(dve, s["step"])
                        v = nc.vector
                        for m in range(CH):
                            out = conved[:, m, :].rearrange("p (j t) -> p j t", j=GROUP)
                            for tap in range(TAPS):
                                at = tap if d == "f" else TAPS - 1 - tap
                                window, weight = around[d][:, m, :, at:at + SEQ], small[d, "conv_w"][:, m, tap:tap + 1]
                                if tap == 0:
                                    last = v.tensor_scalar(out, window, weight, None, ALU.mult)
                                else:
                                    last = v.scalar_tensor_tensor(out, window, weight, out, ALU.mult, ALU.add)
                                if tap < TAPS - 1:
                                    link(last)
                            last.then_inc(s["conved"], 1)
                        dve.wait_ge(s["exped"], 1)
                        v.tensor_scalar(u[:, :, :], e[:, :, :], 1.0, None, ALU.add).then_inc(s["plussed"], 1)
                        dve.wait_ge(s["plussed"], 1)
                        link(v.tensor_scalar(late[:, :, :], u[:, :, :], 1.0, None, ALU.subtract))
                        link(v.tensor_scalar(miss[:, :, :], late[:, :, :], 0.0, None, ALU.is_equal))
                        link(v.tensor_tensor(late[:, :, :], late[:, :, :], miss[:, :, :], ALU.add))
                        link(v.reciprocal(late[:, :, :], late[:, :, :]))
                        link(v.tensor_tensor(late[:, :, :], late[:, :, :], e[:, :, :], ALU.mult))
                        link(v.tensor_tensor(miss[:, :, :], miss[:, :, :], e[:, :, :], ALU.mult))
                        dve.wait_ge(s["logged"], 1)
                        link(v.tensor_tensor(u[:, :, :], u[:, :, :], late[:, :, :], ALU.mult))
                        link(v.tensor_tensor(u[:, :, :], u[:, :, :], miss[:, :, :], ALU.add))
                        link(v.scalar_tensor_tensor(dt[:, :, :], raw[:, :, :], 0.0, u[:, :, :], ALU.max, ALU.add))
                        v.tensor_tensor(decay[:, :, :], dt[:, :, :], small[d, "A"][:, :].unsqueeze(1).broadcast_to([P, GROUP, HEADS]),
                                        ALU.mult)

                    @block.scalar
                    def _(act):
                        nc.scalar.activation(e[:, :, :], raw[:, :, :], ACT.Abs).then_inc(s["sized"], 1)
                        act.wait_ge(s["sized"], 1)
                        nc.scalar.activation(e[:, :, :], e[:, :, :], ACT.Exp, scale=-1.0).then_inc(s["exped"], 1)
                        for m in range(CH):
                            act.wait_ge(s["conved"], m + 1)
                            nc.scalar.activation(conved[:, m, :], conved[:, m, :], ACT.Silu, bias=small[d, "conv_b"][:, m:m + 1])
                        act.wait_ge(s["plussed"], 1)
                        act.wait_ge(s["step"], CH * (TAPS - 1) + 1)
                        nc.scalar.activation(u[:, :, :], u[:, :, :], ACT.Ln).then_inc(s["logged"], 1)

                with phase(k, "sum", "summed copied turned paired") as (block, s):
                    @block.tensor
                    def _(pe):
                        nc.tensor.matmul(k.ps[:, 0, 0:GROUP * HEADS], small[d, "mask"][:, :],
                                         decay[:, :, :].rearrange("p j h -> p (j h)"), start=True, stop=True).then_inc(s["summed"], 1)
                        for j in range(GROUP):
                            last = nc.tensor.matmul(k.ps[:, 2, sl(j)], conved[:, M, sl(j)], conved[:, M + 1, sl(j)], start=True, stop=True)
                        last.then_inc(s["paired"], 1)
                        pe.wait_ge(s["copied"], 1)
                        for j in range(GROUP):
                            last = nc.tensor.transpose(k.ps[0:HEADS, 1, sl(j)], total[:, j, :], k.ident[:, :])
                        last.then_inc(s["turned"], 1)

                    @block.vector
                    def _(dve):
                        dve.wait_ge(s["summed"], 1)
                        nc.vector.tensor_copy(total[:, :, :].rearrange("p j h -> p (j h)"), k.ps[:, 0, 0:GROUP * HEADS]).then_inc(s["copied"], 1)
                        dve.wait_ge(s["paired"], 1)
                        nc.vector.tensor_tensor(pairs[:, :, :], k.ps[:, 2, :].rearrange("p (j t) -> p j t", j=GROUP),
                                                small[d, "mask"][:, :].unsqueeze(1).broadcast_to([P, GROUP, P]), ALU.mult)

                    @block.scalar
                    def _(act):
                        act.wait_ge(s["turned"], 1)
                        nc.scalar.activation(totalT[:, :], k.ps[0:HEADS, 1, :], ACT.Copy)

                def to_inputs(j):
                    def evacuate(nc, engine, bank):
                        heads = bank.rearrange("p (h d) -> p h d", d=WIDTH)
                        nc.vector.tensor_tensor(inputs[:, j, :].rearrange("p (h d) -> p h d", d=WIDTH), heads,
                                                dt[:, j, :].unsqueeze(2).broadcast_to([P, HEADS, WIDTH]), ALU.mult)
                        return nc.vector.tensor_tensor(skipped[:, j, :].rearrange("p (h d) -> p h d", d=WIDTH), heads,
                                                       small[d, "D"][:, :].unsqueeze(2).broadcast_to([P, HEADS, WIDTH]), ALU.mult)
                    return evacuate
                gemm_phase(k, "turn", [(P, INNER, turned([conved[:, m, sl(j)] for m in range(M)], k.ident[:, :]), "dve", to_inputs(j))
                                       for j in range(GROUP)])

                with phase(k, "scan", "spread read capped exped weighted mixed") as (block, s):
                    @block.tensor
                    def _(pe):
                        def mix(h):
                            pe.wait_ge(s["weighted"], h + 1)
                            for j in range(GROUP):
                                last = nc.tensor.matmul(k.ps[:, 4 + j, sl(h, WIDTH)], lasting[:, h % LB, j, :],
                                                        inputs[:, j, sl(h, WIDTH)], start=True, stop=True)
                            last.then_inc(s["mixed"], 1)

                        for h in range(HEADS):
                            if h >= 4:
                                pe.wait_ge(s["read"], h - 3)
                            nc.tensor.matmul(k.ps[:, h % 4, :], select[:, h, :], totalT[:, :], start=True, stop=True).then_inc(s["spread"], 1)
                            if h >= 3:
                                mix(h - 3)
                        for h in range(HEADS - 3, HEADS):
                            mix(h)

                    @block.vector
                    def _(dve):
                        def weight(h):
                            dve.wait_ge(s["exped"], h + 1)
                            nc.vector.tensor_tensor(lasting[:, h % LB, :, :], lasting[:, h % LB, :, :], pairs[:, :, :],
                                                    ALU.mult).then_inc(s["weighted"], 1)

                        for h in range(HEADS):
                            dve.wait_ge(s["spread"], h + 1)
                            if h >= LB:
                                dve.wait_ge(s["mixed"], h - LB + 1)
                            nc.vector.tensor_tensor(lasting[:, h % LB, :, :], k.ps[:, h % 4, :].rearrange("p (j t) -> p j t", j=GROUP),
                                                    total[:, :, h].unsqueeze(2).broadcast_to([P, GROUP, P]), ALU.subtract).then_inc(s["read"], 1)
                            if h >= 2:
                                weight(h - 2)
                        weight(HEADS - 2)
                        weight(HEADS - 1)

                    @block.gpsimd
                    def _(pool):
                        for h in range(HEADS):
                            pool.wait_ge(s["read"], h + 1)
                            nc.gpsimd.tensor_scalar(lasting[:, h % LB, :, :], lasting[:, h % LB, :, :], 0.0, None, ALU.min).then_inc(s["capped"], 1)

                    @block.scalar
                    def _(act):
                        for h in range(HEADS):
                            act.wait_ge(s["capped"], h + 1)
                            nc.scalar.activation(lasting[:, h % LB, :, :], lasting[:, h % LB, :, :], ACT.Exp).then_inc(s["exped"], 1)

                with phase(k, "gate", "step squared rooted") as (block, s):
                    @block.vector
                    def _(dve):
                        link = Link(dve, s["step"])
                        v = nc.vector
                        for j in range(GROUP):
                            last = v.tensor_tensor(y[:, j, :], k.ps[:, 4 + j, :], skipped[:, j, :], ALU.add)
                        link(last)
                        link(v.tensor_tensor(y[:, :, :], y[:, :, :], gate[:, :, :], ALU.mult))
                        for j in range(GROUP):
                            last = v.tensor_tensor_reduce(skipped[:, j, :], y[:, j, :], y[:, j, :], 1.0, 0.0, ALU.mult, ALU.add,
                                                          k.rstd[:, j:j + 1])
                        link(last)
                        link(v.tensor_scalar(k.rstd[:, :], k.rstd[:, :], 1.0 / INNER, LN_EPS, ALU.mult, ALU.add))
                        v.reciprocal(k.rstd[:, :], k.rstd[:, :]).then_inc(s["squared"], 1)
                        dve.wait_ge(s["rooted"], 1)
                        for j in range(GROUP):
                            v.tensor_scalar(y[:, j, :], y[:, j, :], k.rstd[:, j:j + 1], None, ALU.mult)

                    @block.scalar
                    def _(act):
                        row_rstd(k, act, s["squared"], s["rooted"])
                gemm_phase(k, "turn", [(P, GT, turned([y[:, j, sl(m)] for j in range(GROUP)], k.ident[:, :]), turns(m),
                                        to_copy(yT[d][:, m, :])) for m in range(M)])

            jobs = []
            for j in range(GROUP):
                x = k.x[:, bass.ds(g * GROUP + j, 1), :]
                both = [(yT[d][:, m, sl(j)], folded[d][:, m, :]) for d in ways for m in range(M)]
                both.append((k.ones[0:1, 0:P], out_b[0:1, :]))
                jobs.append((P, DIM, products(both), "dve",
                             lambda nc, engine, bank, x=x: nc.vector.tensor_tensor(x, bank.rearrange("p (o d) -> p o d", o=1), x, ALU.add)))
            gemm_phase(k, "out", jobs)


def l3_attn(k):
    nc = k.nc
    H, D = 16, 16
    QT = TOKENS // P
    Q_PARTS, K_PARTS = (0, 0, 1, 0, 2, 1), (0, 1, 0, 2, 0, 1)
    ROWS = len(Q_PARTS) * D
    DEEP = ROWS + 3
    VW = D + 1
    CHUNK = 512
    n = "L3_attn_"
    parts_dram = nc.dram_tensor("parts", (6 * DIM, TOKENS), BF16, kind="Internal").ap()
    with ExitStack() as stack:
        wp, a = weights(k, stack, n + "proj_w", KD, DIM)
        wq, b = weights(k, stack, n + "wq", KD, P)
        wk, c = weights(k, stack, n + "wk", KD, P)
        bp, d = bias_columns(k, stack, n + "proj_b", KD)
        bp_row, e = bias_row(k, stack, n + "proj_b_row", DIM)
        values = sb(k, stack, "values", [P, QT, H, VW])
        load_phase(k, a + b + c + d + e)
        with ExitStack() as inner:
            flat = sb(k, inner, "flat", [P, KD, GT])
            whole, left = sb(k, inner, "whole", [P, 2 * KD, GT]), sb(k, inner, "left", [P, 2 * KD, GT])
            parts = sb(k, inner, "parts", [P, 3, 2 * KD, GT], BF16)
            with phase(k, "fill", "none") as (block, s):
                @block.vector
                def _(dve):
                    nc.vector.memset(values[:, :, :, :], 1.0)
            with nc.Fori(0, GROUPS) as g:
                norm_phase(k, g, lambda kt: k.xT[:, kt, :])

                def to_values(j):
                    def evacuate(nc, engine, bank):
                        return nc.vector.tensor_copy(values[:, bass.ds(g * GROUP + j, 1), :, 0:D],
                                                     bank.rearrange("p (o h d) -> p o h d", o=1, d=D))
                    return evacuate
                jobs = feature_jobs(flat, wp, k.xT, [P] * KD, DIM, bp)
                jobs += [(P, DIM, token_pairs(k, k.xT, [P] * KD, j, wp, slice(0, DIM), bp_row), "dve", to_values(j))
                         for j in range(GROUP)]
                gemm_phase(k, "flat", jobs)
                gemm_phase(k, "qk", [(P, GT, products([(w[:, m, :], flat[:, m, :])]), turns(m), to_copy(whole[:, KD * i + m, :]))
                                     for i, w in enumerate((wq, wk)) for m in range(KD)])
                with phase(k, "split", "step stored") as (block, s):
                    @block.vector
                    def _(dve):
                        link = Link(dve, s["step"])
                        v = nc.vector
                        link(v.tensor_copy(parts[:, 0], whole[:, :, :]))
                        link(v.tensor_tensor(left[:, :, :], whole[:, :, :], parts[:, 0], ALU.subtract))
                        link(v.tensor_copy(parts[:, 1], left[:, :, :]))
                        link(v.tensor_tensor(parts[:, 2], left[:, :, :], parts[:, 1], ALU.subtract))

                    @block.sync
                    def _(sp):
                        for part, ready in enumerate((1, 3, 4)):
                            sp.wait_ge(s["step"], ready)
                            for i in range(2 * KD):
                                row0 = ((i // KD) * 3 + part) * DIM + (i % KD) * P
                                sp.dma_start(parts_dram[row0:row0 + P, bass.ds(g * GT, GT)], parts[:, part, i, :]).then_inc(s["stored"], 16)
                        sp.wait_ge(s["stored"], 16 * 3 * 2 * KD)

        queries = [sb(k, stack, f"queries{i}", [P, TOKENS], BF16) for i in range(3)]
        keys = [sb(k, stack, f"keys{i}", [P, TOKENS], BF16) for i in range(3)]
        attn = sb(k, stack, "attn", [P, 2, TOKENS])
        head_values = sb(k, stack, "head_values", [P, QT, PAD])
        peaks = sb(k, stack, "peaks", [P, QT, TOKENS // CHUNK])
        minus, left = sb(k, stack, "minus", [P, QT]), sb(k, stack, "left", [P, QT])
        minus_b = sb(k, stack, "minus_b", [P, QT], BF16)
        minus_parts = sb(k, stack, "minus_parts", [P, 3, QT])
        minus_rows = sb(k, stack, "minus_rows", [3 * QT, P], BF16)
        output = sb(k, stack, "output", [P, CHUNK])
        share, fresh = sb(k, stack, "share", [P, QT]), sb(k, stack, "fresh", [P, 4, 4, D])

        def load_head(sp, loaded, i, head):
            for side, (dst, order) in enumerate(((queries[i], Q_PARTS), (keys[i], K_PARTS))):
                for block_, part in enumerate(order):
                    sp.dma_start(dst[sl(block_, D), :], parts_dram[bass.ds(head * D + (side * 3 + part) * DIM, D), :]).then_inc(loaded, 16)

        with phase(k, "start", "loaded") as (block, s):
            @block.vector
            def _(dve):
                nc.vector.memset(head_values[:, :, :], 0.0)
                for i in range(3):
                    nc.vector.memset(keys[i][ROWS:P, :], 1.0)

            @block.sync
            def _(sp):
                for i in range(2):
                    load_head(sp, s["loaded"], i, i)
                sp.wait_ge(s["loaded"], 16 * 24)

        PROBES = QT * TOKENS // CHUNK
        PER_STEP = 5

        def head_phase(here, ahead, later, head):
            with phase(k, "head", "step loaded scored exped mixed probed maxed parted turned rowed moved fetched emptied finished") as (block, s):
                @block.sync
                def _(sp):
                    if later is not None:
                        load_head(sp, s["loaded"], *later)
                        sp.wait_ge(s["loaded"], 16 * 12)
                    if ahead is not None:
                        sp.wait_ge(s["rowed"], 1)
                        for part in range(3):
                            sp.dma_start(queries[ahead][ROWS + part:ROWS + part + 1, :].rearrange("o (t q) -> o t q", q=P),
                                         minus_rows[sl(part, QT), :]).then_inc(s["moved"], 16)
                        sp.wait_ge(s["moved"], 48)

                @block.gpsimd
                def _(pool):
                    if here is not None:
                        nc.gpsimd.tensor_copy(head_values[:, :, 0:VW].unsqueeze(2), values[:, :, bass.ds(head, 1), :]).then_inc(s["fetched"], 1)

                @block.tensor
                def _(pe):
                    def score(kt):
                        for half in range(2):
                            if kt >= 1:
                                pe.wait_ge(s["exped"], 2 * (kt - 1) + half + 1)
                            for c in range(2 * half, 2 * half + 2):
                                last = nc.tensor.matmul(k.ps[:, c, :], keys[here][0:DEEP, sl(kt)], queries[here][0:DEEP, sl(c, CHUNK)],
                                                        start=True, stop=True)
                            last.then_inc(s["scored"], 1)

                    def probe(u):
                        if u >= 2:
                            pe.wait_ge(s["maxed"], u - 1)
                        nc.tensor.matmul(k.ps[:, 5 + u % 2, :], queries[ahead][0:ROWS, sl(u // 4)], keys[ahead][0:ROWS, sl(u % 4, CHUNK)],
                                         start=True, stop=True).then_inc(s["probed"], 1)

                    def mix(kt):
                        pe.wait_ge(s["exped"], 2 * kt + 2)
                        if kt == 0:
                            pe.wait_ge(s["fetched"], 1)
                        for c in range(4):
                            last = nc.tensor.matmul(k.ps[sl(c, PAD), 4, :], head_values[:, kt, :], attn[:, kt % 2, sl(c, CHUNK)],
                                                    start=kt == 0, stop=kt == QT - 1)
                        last.then_inc(s["mixed"], 1)

                    for kt in range(QT):
                        if here is not None:
                            score(kt)
                        if ahead is not None:
                            for u in range(PER_STEP * kt, min(PER_STEP * kt + PER_STEP, PROBES)):
                                probe(u)
                        if here is not None and kt >= 1:
                            mix(kt - 1)
                    if ahead is not None:
                        pe.wait_ge(s["parted"], 1)
                        nc.tensor.transpose(k.ps[0:3 * QT, 7, 0:P], minus_parts[:, :, :].rearrange("p a b -> p (a b)"),
                                            k.ident[:, :]).then_inc(s["turned"], 1)
                    if here is not None:
                        mix(QT - 1)
                        pe.wait_ge(s["emptied"], 1)
                        if ahead is not None:
                            pe.wait_ge(s["rowed"], 1)
                        for b_ in range(4):
                            last = nc.tensor.transpose(k.ps[:, 7, sl(b_)], output[:, sl(b_)], k.ident[:, :])
                        last.then_inc(s["finished"], 1)

                @block.scalar
                def _(act):
                    if here is not None:
                        for kt in range(QT):
                            for half in range(2):
                                act.wait_ge(s["scored"], 2 * kt + half + 1)
                                if kt >= 2:
                                    act.wait_ge(s["mixed"], kt - 1)
                                nc.scalar.activation(attn[:, kt % 2, sl(half, 2 * CHUNK)].rearrange("p (c q) -> p c q", c=2),
                                                     k.ps[:, 2 * half:2 * half + 2, :], ACT.Exp, scale=1.0 / 16.0).then_inc(s["exped"], 1)
                    if ahead is not None:
                        act.wait_ge(s["turned"], 1)
                        nc.scalar.activation(minus_rows[:, :], k.ps[0:3 * QT, 7, 0:P], ACT.Copy).then_inc(s["rowed"], 1)
                    if here is not None:
                        act.wait_ge(s["mixed"], QT)
                        nc.scalar.activation(output[:, :], k.ps[:, 4, :], ACT.Copy).then_inc(s["emptied"], 1)

                @block.vector
                def _(dve):
                    link = Link(dve, s["step"])
                    v = nc.vector
                    if ahead is not None:
                        for u in range(PROBES):
                            dve.wait_ge(s["probed"], u + 1)
                            v.tensor_reduce(peaks[:, u // 4, u % 4:u % 4 + 1], k.ps[:, 5 + u % 2, :], AX.X, ALU.max).then_inc(s["maxed"], 1)
                        dve.wait_ge(s["maxed"], PROBES)
                        link(v.tensor_reduce(minus[:, :], peaks[:, :, :], AX.X, ALU.max))
                        link(v.tensor_scalar(minus[:, :], minus[:, :], -1.0, None, ALU.mult))
                        link(v.tensor_copy(minus_b[:, :], minus[:, :]))
                        link(v.tensor_copy(minus_parts[:, 0, :], minus_b[:, :]))
                        link(v.tensor_tensor(left[:, :], minus[:, :], minus_parts[:, 0, :], ALU.subtract))
                        link(v.tensor_copy(minus_b[:, :], left[:, :]))
                        link(v.tensor_copy(minus_parts[:, 1, :], minus_b[:, :]))
                        v.tensor_tensor(minus_parts[:, 2, :], left[:, :], minus_parts[:, 1, :], ALU.subtract).then_inc(s["parted"], 1)
                    if here is not None:
                        dve.wait_ge(s["finished"], 1)
                        turned_ = k.ps[:, 7, :].rearrange("p (b c w) -> p b c w", b=4, c=4)
                        share_ = share[:, :].rearrange("p (b c) -> p b c", b=4)
                        link(v.reciprocal(share_.unsqueeze(3), turned_[:, :, :, D:VW]))
                        link(v.tensor_tensor(fresh[:, :, :, :], turned_[:, :, :, 0:D], share_.unsqueeze(3).broadcast_to([P, 4, 4, D]), ALU.mult))
                        for b_ in range(4):
                            x = k.x[:, :, bass.ds(head * D, D)].rearrange("p (c b) d -> p c b d", b=4)[:, :, b_, :]
                            v.tensor_tensor(x, x, fresh[:, b_, :, :], ALU.add)

        head_phase(None, 0, None, None)
        with nc.Fori(0, 4) as i:
            for m in range(3):
                head_phase(m, (m + 1) % 3, ((m + 2) % 3, 3 * i + m + 2), 3 * i + m)
            empty_phase(k)
        for h in range(12, H):
            head_phase(h % 3, (h + 1) % 3 if h + 1 < H else None, ((h + 2) % 3, h + 2) if h + 2 < H else None, h)


def lay_out_rest(i, w):
    n = "L0_xattn_"
    w[n + "Wq"], w[n + "Wk"], w[n + "Wv"] = i[n + "Wq"], i[n + "Wk"], pad_heads(i[n + "Wv"], 1)
    w[n + "Wo"] = wo_order(pad_heads(i[n + "Wo"], 0), 16, PAD)
    w[n + "bv"] = row(pad_heads(i[n + "bv"], 0))
    for m in ("bq", "bk", "bo"):
        w[n + m] = row(i[n + m])
    for m in ("ln_gamma", "ln_beta"):
        w[n + m] = np.repeat(row(i[n + m]), P, axis=0)

    n = "L0_ffn_"
    w[n + "Wr"], w[n + "br"] = i[n + "Wr"], row(i[n + "br"])
    w[n + "bd"] = np.concatenate([i[n + "bd"], row(i[n + "bd_s"])])

    def expert_parts(name):
        return np.concatenate([i[n + name], i[n + name + "_s"][None]])

    def by_partition(a, tiles):
        return a.reshape(len(a), tiles, P, -1).transpose(0, 2, 1, 3).reshape(len(a), P, -1)
    packed = np.concatenate([by_partition(expert_parts("Wg"), 2), by_partition(expert_parts("Wu"), 2), expert_parts("Wd"),
                             expert_parts("bg")[:, :, None], expert_parts("bu")[:, :, None]], axis=2)
    w[n + "experts"] = packed.reshape(11, 3, P, -1).transpose(0, 2, 1, 3)

    n = "L2_ffn_"
    w[n + "Wg"] = i[n + "Wg"]
    w[n + "experts"] = np.concatenate([by_partition(i[n + "W1"], 2), by_partition(i[n + "W2"], 4)], axis=2)
    w["order"] = np.broadcast_to(np.arange(8, 0, -1, dtype=np.float32), (P, BATCH, 8))

    n = "L3_ffn_"
    for m in ("W_fc", "W_proj", "B_fc", "B_proj"):
        w[n + m] = i[n + m].T
    w[n + "A_fc"], w[n + "A_proj"] = i[n + "A_fc"], i[n + "A_proj"]
    w[n + "b_fc"], w[n + "b_proj"] = columns(i[n + "b_fc"]), row(i[n + "b_proj"])

    n = "L1_attn_"
    w[n + "W_q"], w[n + "W_k"] = pad_heads(i[n + "W_q"], 1), pad_heads(i[n + "W_k"], 1)
    w[n + "W_v"], w[n + "W_o"] = i[n + "W_v"], i[n + "W_o"]
    blocks, where = np.zeros((P, 8, P), np.float32), np.zeros((P, 8, P), np.float32)
    for h in range(16):
        at = PAD * (h % 4)
        blocks[at:at + 16, h // 2, sl(h % 2, 64)] = i[n + "centers"][h].T
        where[at:at + 16, h // 2, sl(h % 2, 64)] = 1
    w[n + "centers"], w[n + "where"] = blocks, where
    for m in ("log_scales", "amplitudes"):
        w[n + m] = columns(i[n + m].reshape(-1))

    n = "L1_ffn_"
    for m in ("w_gate", "w_up", "w_down"):
        w[n + m] = i[n + m].T

    n = "L2_attn_"
    w[n + "norm_w"], w[n + "out_b"] = columns(i[n + "norm_w"]), row(i[n + "out_b_blk"])
    w[n + "select"] = np.repeat(np.eye(8, dtype=np.float32)[:, :, None], P, axis=2)
    for number, d in enumerate("fb"):
        m = n + d + "_"
        w[m + "in_w"], w[m + "out_w"] = i[m + "in_w"].T, i[m + "out_w"]
        w[m + "block_w"] = i[n + "out_w_blk"][:, sl(number, DIM)].T
        w[m + "gnorm_w"], w[m + "conv_b"] = columns(i[m + "gnorm_w"]), columns(i[m + "conv_b"])
        w[m + "conv_w"] = i[m + "conv_w"].reshape(6, P, 4).transpose(1, 0, 2)
        w[m + "A"], w[m + "D"] = np.repeat(row(i[m + "A_log"]), P, axis=0), np.repeat(row(i[m + "D"]), P, axis=0)
        w[m + "dt_bias"] = row(i[m + "dt_bias"])
        w[m + "mask"] = np.tri(P, dtype=np.float32).T if d == "f" else np.tri(P, dtype=np.float32)

    n = "L3_attn_"
    w[n + "proj_w"] = i[n + "proj_w"].T
    w[n + "proj_b"], w[n + "proj_b_row"] = columns(i[n + "proj_b"]), row(i[n + "proj_b"])
    for m in ("wq", "wk"):
        blocks = np.zeros((2, P, P), np.float32)
        for h in range(16):
            blocks[h // 8, sl(h % 8, 16), sl(h % 8, 16)] = i[n + m][h]
        w[n + m] = blocks.reshape(2 * P, P)


def layers(k):
    l0_attn(k)
    l0_xattn(k)
    l0_ffn(k)
    l1_attn(k)
    cross_attention(k, "L1_xattn", 16, "L1_xattn_Wo", "L1_xattn_bo")
    l1_ffn(k)
    l2_attn(k)
    cross_attention(k, "L2_xattn", 8, "L2_xattn_Wout", "L2_xattn_bout")
    l2_ffn(k)
    l3_attn(k)
    cross_attention(k, "L3_xattn", 8, "L3_xattn_Wo", "L3_xattn_bo")
    l3_ffn(k)


def build(nc, w, out):
    with ExitStack() as stack:
        k = Core(nc, w)
        free = sorted(nc.free_semaphores)[-2 * SIGNALS:]
        k.banks = (free[:SIGNALS], free[SIGNALS:])
        k.ps = stack.enter_context(nc.psum_tensor("ps", [P, 8, 512], F32))
        k.x = sb(k, stack, "x", [P, BATCH, DIM])
        k.ctxT = sb(k, stack, "ctxT", [P, 2, TOKENS])
        k.ctxG = sb(k, stack, "ctxG", [P, 2, GT])
        k.xT = sb(k, stack, "xT", [P, KD, GT])
        k.normed = sb(k, stack, "normed", [P, GROUP, DIM])
        k.ident = sb(k, stack, "ident", [P, P])
        k.ones = sb(k, stack, "ones", [P, P])
        k.stats = sb(k, stack, "stats", [P, GROUP, 6])
        k.moments = sb(k, stack, "moments", [P, GROUP, 2])
        k.rstd = sb(k, stack, "rstd", [P, GROUP])
        load_phase(k, [(k.x[:, :, :], w["x"].rearrange("b t d -> t b d")), (k.ident[:, :], w["ident"]),
                       (k.ones[:, :], w["ones"]),
                       (k.ctxT[:, 0, :], w["ctxT"][0:P, :]), (k.ctxT[0:CTX - P, 1, :], w["ctxT"][P:CTX, :])])
        layers(k)
        with phase(k, "store", "stored") as (block, s):
            @block.sync
            def _(sp):
                sp.dma_start(out.rearrange("b t d -> t b d"), k.x[:, :, :]).then_inc(s["stored"], 16)
                sp.wait_ge(s["stored"], 16)


def pad_heads(a, axis):
    a = np.moveaxis(a, axis, -1)
    b = np.zeros(a.shape[:-1] + (16, PAD), a.dtype)
    b[..., :16] = a.reshape(a.shape[:-1] + (16, 16))
    return np.ascontiguousarray(np.moveaxis(b.reshape(a.shape[:-1] + (16 * PAD,)), -1, axis))


def columns(b):
    return np.ascontiguousarray(b.reshape(-1, P).T)


def row(b):
    return b.reshape(1, -1)


def wo_order(a, heads, width):
    per = P // width
    order = [(u // per * 4 + i) * per + u % per for u in range(heads // 4) for i in range(4)]
    return a.reshape(heads, width, -1)[order].reshape(heads * width, -1)


def lay_out(i):
    i = {n: np.asarray(a) for n, a in i.items()}
    w = {"x": i["x"], "ctxT": i["ctx_768"].reshape(TOKENS, CTX).T,
         "ident": np.eye(P, dtype=np.float32), "ones": np.ones((P, P), np.float32)}
    future = (np.arange(P)[None, :] > np.arange(P)[:, None]).astype(np.int32)
    w["future"] = np.repeat(future[:, None, :], 4, axis=1)
    n = "L0_attn_"
    for m in "qkv":
        w[n + "W" + m] = pad_heads(i[n + "W" + m], 1)
    w[n + "bq"], w[n + "bk"] = columns(pad_heads(i[n + "bq"], 0)), columns(pad_heads(i[n + "bk"], 0))
    w[n + "bv"], w[n + "bo"] = row(pad_heads(i[n + "bv"], 0)), row(i[n + "bo"])
    w[n + "Wo"] = wo_order(pad_heads(i[n + "Wo"], 0), 16, PAD)
    for n in ("L1_xattn_", "L2_xattn_", "L3_xattn_"):
        for m in ("Wq", "Wk", "Wv", "Wo", "Wout", "bo", "bout"):
            if n + m in i:
                w[n + m] = i[n + m] if m[0] == "W" else row(i[n + m])
            if n + m in i and m in ("Wo", "Wout"):
                w[n + m] = wo_order(i[n + m], len(i[n + m]) // 64, 64)
    lay_out_rest(i, w)
    return {n: np.ascontiguousarray(a) for n, a in w.items()}


def kernel(**inputs):
    import concourse.bacc as bacc
    from concourse.bass_utils import run_bass_kernel_spmd

    arrays = {f"in_{n}": a for n, a in lay_out(inputs).items()}
    nc = bacc.Bacc("TRN2", target_bir_lowering=False, num_devices=1)
    w = {n[3:]: nc.dram_tensor(n, a.shape, mybir.dt.from_np(a.dtype), kind="ExternalInput").ap() for n, a in arrays.items()}
    out = nc.dram_tensor("out_0_dram", (BATCH, SEQ, DIM), F32, kind="ExternalOutput").ap()
    build(nc, w, out)
    return run_bass_kernel_spmd(nc, [arrays], core_ids=[0]).results[0]["out_0_dram"]
```

```python
from contextlib import ExitStack, contextmanager
from itertools import count

import numpy as np

import concourse.bass as bass
from concourse import mybir

F32 = mybir.dt.float32
BF16 = mybir.dt.bfloat16
I32 = mybir.dt.int32
ALU = mybir.AluOpType
ACT = mybir.ActivationFunctionType
AX = mybir.AxisListType

P = 128
BATCH, SEQ, DIM = 16, 128, 256
KD = DIM // P
CTX = 192
GROUP = 4
GROUPS = BATCH // GROUP
GT = GROUP * SEQ
TOKENS = BATCH * SEQ
PAD = 32
LN_EPS = 1e-5
MAGIC = 12582912.0
CTX_ROWS = (P, CTX - P)
SIGNALS = 16


def sl(i, n=P):
    return slice(i * n, (i + 1) * n)


class Core:

    def __init__(self, nc, w):
        self.nc, self.w = nc, w
        self.turn = self.count = self.names = 0



@contextmanager
def phase(k, title, signals):
    nc = k.nc
    mine, other = k.banks[k.turn], k.banks[1 - k.turn]
    k.turn = 1 - k.turn
    k.count += 1
    with ExitStack() as stack:
        sems = {}
        for number, name in zip(mine, signals.split()):
            sems[name] = stack.enter_context(nc.semaphore(f"{title}{k.count}_{name}", num=number))
        with nc.Block() as block:
            @block.sync
            def _(sp):
                sp.sem_clear(range(other[0], other[-1] + 1))
            yield block, sems


class Part:

    def __init__(self, title, signals):
        self.title, self.signals, self.programs = title, signals, {}

    def tensor(self, program):
        self.programs["tensor"] = program

    def vector(self, program):
        self.programs["vector"] = program

    def scalar(self, program):
        self.programs["scalar"] = program

    def gpsimd(self, program):
        self.programs["gpsimd"] = program


def side_by_side(k, *parts):
    names = " ".join(f"{n}_{name}" for n, (part, _) in enumerate(parts) for name in part.signals.split())
    with phase(k, "_".join(part.title for part, _ in parts), names) as (block, s):
        signals = [{name: s[f"{n}_{name}"] for name in part.signals.split()} for n, (part, _) in enumerate(parts)]

        def merged(engine, name):
            running = [(part.programs[name](engine, own), pace) for (part, pace), own in zip(parts, signals)
                       if name in part.programs]
            for r in count():
                if not running:
                    break
                for steps, pace in list(running):
                    for _ in range(int((r + 1) * pace) - int(r * pace)):
                        if next(steps, "end") == "end":
                            running.remove((steps, pace))
                            break

        @block.tensor
        def _(pe):
            merged(pe, "tensor")

        @block.vector
        def _(dve):
            merged(dve, "vector")

        @block.scalar
        def _(act):
            merged(act, "scalar")

        @block.gpsimd
        def _(pool):
            merged(pool, "gpsimd")


class Link:

    def __init__(self, engine, sem):
        self.engine, self.sem, self.count = engine, sem, 0

    def __call__(self, instruction):
        instruction.then_inc(self.sem, 1)
        self.count += 1
        self.engine.wait_ge(self.sem, self.count)


def load_phase(k, pairs):
    with phase(k, "load", "loaded") as (block, s):
        @block.sync
        def _(sp):
            for dst, src in pairs:
                sp.dma_start(dst, src).then_inc(s["loaded"], 16)
            sp.wait_ge(s["loaded"], 16 * len(pairs))


def gemm_part(k, title, jobs, banks=range(8)):
    nc = k.nc
    B = len(banks)
    place, counts = [], {"act": 0, "dve": 0}
    for _, _, _, engine, _ in jobs:
        place.append((engine, counts[engine]))
        counts[engine] += 1
    part = Part(title, "product_ready act_took dve_took")

    def bank(n):
        rows, columns = jobs[n][:2]
        return k.ps[0:rows, banks[n % B], 0:columns]

    @part.tensor
    def _(pe, s):
        for n, job in enumerate(jobs):
            if n >= B:
                engine, at = place[n - B]
                pe.wait_ge(s[f"{engine}_took"], at + 1)
            job[2](nc, bank(n)).then_inc(s["product_ready"], 1)
            yield

    @part.scalar
    def _(act, s):
        for n, job in enumerate(jobs):
            yield
            if job[3] == "act":
                act.wait_ge(s["product_ready"], n + 1)
                job[4](nc, "act", bank(n)).then_inc(s["act_took"], 1)

    @part.vector
    def _(dve, s):
        for n, job in enumerate(jobs):
            yield
            if job[3] == "dve":
                dve.wait_ge(s["product_ready"], n + 1)
                job[4](nc, "dve", bank(n)).then_inc(s["dve_took"], 1)
    return part


def gemm_phase(k, title, jobs):
    side_by_side(k, (gemm_part(k, title, jobs), 1))


def products(pairs):
    def fill(nc, bank):
        for i, (stationary, moving) in enumerate(pairs):
            last = nc.tensor.matmul(bank, stationary, moving, start=i == 0, stop=i == len(pairs) - 1)
        return last
    return fill


def turned(blocks, ident):
    def fill(nc, bank):
        if blocks[0].dtype == BF16:
            bank = bank.bitcast(BF16)
        for i, block in enumerate(blocks):
            last = nc.tensor.transpose(bank[:, sl(i)], block, ident)
        return last
    return fill


def to_copy(dst):
    def evacuate(nc, engine, bank):
        if engine == "act":
            return nc.scalar.activation(dst, bank, ACT.Copy)
        return nc.vector.tensor_copy(dst, bank)
    return evacuate


def to_bias(dst, bias):
    def evacuate(nc, engine, bank):
        if engine == "act":
            return nc.scalar.activation(dst, bank, ACT.Identity, bias=bias)
        return nc.vector.tensor_scalar(dst, bank, bias, None, ALU.add)
    return evacuate


def to_sum(dst, other):
    def evacuate(nc, engine, bank):
        return nc.vector.tensor_tensor(dst, bank, other, ALU.add)
    return evacuate


def turns(n):
    return "act" if n % 2 == 0 else "dve"


def feature_jobs(dst, weights, source, rows, width, bias=None, n0=0):
    jobs = []
    for m in range(width // P):
        pairs = [(weights[0:r, i, sl(m)], source[0:r, i, :]) for i, r in enumerate(rows)]
        out = dst[:, m, :]
        jobs.append((P, GT, products(pairs), turns(n0 + m), to_copy(out) if bias is None else to_bias(out, bias[:, m:m + 1])))
    return jobs


def token_pairs(k, source, rows, j, weights, columns, bias=None):
    pairs = [(source[0:r, i, sl(j)], weights[0:r, i, columns]) for i, r in enumerate(rows)]
    if bias is not None:
        pairs.append((k.ones[0:1, 0:P], bias[0:1, columns]))
    return products(pairs)


def residual_jobs(k, g, source, tiles, weights, bias=None):
    jobs = []
    for j in range(GROUP):
        x = k.x[:, bass.ds(g * GROUP + j, 1), :]
        jobs.append((P, DIM, token_pairs(k, source, [P] * tiles, j, weights, slice(0, DIM), bias), "dve",
                     lambda nc, engine, bank, x=x: nc.vector.tensor_tensor(x, bank.rearrange("p (o d) -> p o d", o=1), x, ALU.add)))
    return jobs


def row_stats(k, dve, link, source, measured):
    nc = k.nc
    for j in range(GROUP):
        last = nc.vector.bn_stats(k.stats[:, j, :], source(j))
    link(last)
    for j in range(GROUP):
        last = nc.vector.bn_aggr(k.moments[:, j, :], k.stats[:, j, :])
    link(last)
    link(nc.vector.tensor_scalar(k.rstd[:, :], k.moments[:, :, 1], LN_EPS, None, ALU.add))
    nc.vector.reciprocal(k.rstd[:, :], k.rstd[:, :]).then_inc(measured, 1)


def row_rstd(k, act, measured, rooted):
    act.wait_ge(measured, 1)
    k.nc.scalar.activation(k.rstd[:, :], k.rstd[:, :], ACT.Sqrt).then_inc(rooted, 1)


def norm_part(k, g, dst, banks=(0, 1)):
    nc = k.nc
    part = Part("norm", "step measured rooted normed turned")

    def source(j):
        return k.x[:, bass.ds(g * GROUP + j, 1), :].rearrange("p o d -> p (o d)")

    @part.vector
    def _(dve, s):
        row_stats(k, dve, Link(dve, s["step"]), source, s["measured"])
        yield
        dve.wait_ge(s["rooted"], 1)
        for j in range(GROUP):
            nc.vector.tensor_scalar(k.normed[:, j, :], source(j), k.moments[:, j, 0:1], k.rstd[:, j:j + 1],
                                    ALU.subtract, ALU.mult).then_inc(s["normed"], 1)
        yield
        dve.wait_ge(s["turned"], GROUP)
        nc.vector.tensor_copy(dst(1), k.ps[:, banks[1], :])
        yield

    @part.tensor
    def _(pe, s):
        for j in range(GROUP):
            pe.wait_ge(s["normed"], j + 1)
            for kt in range(KD):
                last = nc.tensor.transpose(k.ps[:, banks[kt], sl(j)], k.normed[:, j, sl(kt)], k.ident[:, :])
            last.then_inc(s["turned"], 1)
            yield

    @part.scalar
    def _(act, s):
        row_rstd(k, act, s["measured"], s["rooted"])
        yield
        act.wait_ge(s["turned"], GROUP)
        nc.scalar.activation(dst(0), k.ps[:, banks[0], :], ACT.Copy)
        yield
    return part


def norm_phase(k, g, dst):
    side_by_side(k, (norm_part(k, g, dst), 1))


def attention_part(k, heads, width, q_of, k_of, v_of, out_of, scale, causal=False):
    nc = k.nc
    units = [(j, u) for j in range(GROUP) for u in range(heads // 4)]
    SB, WB, TB, OB = 2, 4, 2, 2
    per = P // width
    blocks = 4 * width // P

    def head(u, i):
        return (u // per * 4 + i) * per + u % per

    def scores(n):
        return k.ps[:, n % SB, :].rearrange("p (h t) -> p h t", h=4)

    def weights(n):
        return k.attn_w[:, n % WB, :, :]

    def turned(n):
        return k.ps[:, SB + n % TB, :]

    def output(n):
        return k.ps[:, SB + TB + n % OB, 0:blocks * P]

    part = Part("attention", "scored step read summed exped scaled turned copied mixed taken")

    @part.tensor
    def _(pe, s):
        def score(n):
            if n >= SB:
                pe.wait_ge(s["read"], n - SB + 1)
            j, u = units[n]
            for i in range(4):
                last = nc.tensor.matmul(scores(n)[:, i, :], q_of(j, head(u, i)), k_of(j, head(u, i)), start=True, stop=True)
            last.then_inc(s["scored"], 1)

        def turn(n):
            pe.wait_ge(s["scaled"], n + 1)
            if n >= TB:
                pe.wait_ge(s["copied"], n - TB + 1)
            for i in range(4):
                last = nc.tensor.transpose(turned(n)[:, sl(i)], weights(n)[:, i, :], k.ident[:, :])
            last.then_inc(s["turned"], 1)

        def mix(n):
            pe.wait_ge(s["copied"], n + 1)
            if n >= OB:
                pe.wait_ge(s["taken"], n - OB + 1)
            j, u = units[n]
            for i in range(4):
                at = i * width
                last = nc.tensor.matmul(output(n)[at % P:at % P + width, sl(at // P)], v_of(j, head(u, i)),
                                        k.attn_wT[:, n % TB, sl(i)], start=True, stop=True)
            last.then_inc(s["mixed"], 1)

        for n in range(len(units) + 3):
            if n < len(units):
                score(n)
            if 0 <= n - 2 < len(units):
                turn(n - 2)
            if 0 <= n - 3:
                mix(n - 3)
            yield

    @part.vector
    def _(dve, s):
        link = Link(dve, s["step"])

        def subtract_max(n):
            dve.wait_ge(s["scored"], n + 1)
            if causal:
                link(nc.vector.copy_predicated(scores(n), k.future[:, :, :], k.minus[:, :, :]))
            link(nc.vector.tensor_reduce(k.peak[:, n % WB, :], scores(n), AX.X, ALU.max))
            if n >= WB:
                dve.wait_ge(s["turned"], n - WB + 1)
            nc.vector.tensor_tensor(weights(n), scores(n), k.peak[:, n % WB, :].unsqueeze(2).broadcast_to([P, 4, P]),
                                    ALU.subtract).then_inc(s["read"], 1)

        def total(n):
            dve.wait_ge(s["exped"], n + 1)
            link(nc.vector.tensor_reduce(k.total[:, n % WB, :], weights(n), AX.X, ALU.add))
            nc.vector.reciprocal(k.share[:, n % WB, :], k.total[:, n % WB, :]).then_inc(s["summed"], 1)

        def take(n):
            dve.wait_ge(s["mixed"], n + 1)
            j, u = units[n]
            nc.vector.tensor_copy(out_of(j, u), output(n).rearrange("p (b t) -> p b t", b=blocks)).then_inc(s["taken"], 1)

        for n in range(len(units) + 3):
            if n < len(units):
                subtract_max(n)
            if 0 <= n - 1 < len(units):
                total(n - 1)
            if 0 <= n - 3:
                take(n - 3)
            yield

    @part.scalar
    def _(act, s):
        for n in range(len(units) + 2):
            if n < len(units):
                act.wait_ge(s["read"], n + 1)
                nc.scalar.activation(weights(n), weights(n), ACT.Exp, scale=scale).then_inc(s["exped"], 1)
            if n >= 2:
                m = n - 2
                act.wait_ge(s["turned"], m + 1)
                if m >= TB:
                    act.wait_ge(s["mixed"], m - TB + 1)
                nc.scalar.activation(k.attn_wT[:, m % TB, :], turned(m), ACT.Copy).then_inc(s["copied"], 1)
            yield

    @part.gpsimd
    def _(pool, s):
        for n in range(len(units)):
            pool.wait_ge(s["summed"], n + 1)
            nc.gpsimd.tensor_tensor(weights(n), weights(n), k.share[:, n % WB, :].unsqueeze(2).broadcast_to([P, 4, P]),
                                    ALU.mult).then_inc(s["scaled"], 1)
            yield
    return part


def attention_memory(k, stack):
    k.attn_w = sb(k, stack, "attn_w", [P, 4, 4, P])
    k.attn_wT = sb(k, stack, "attn_wT", [P, 2, 4 * P])
    k.peak, k.total, k.share = (sb(k, stack, f"attn_{name}", [P, 4, 4]) for name in ("peak", "total", "share"))


def sb(k, stack, name, shape, dtype=F32):
    k.names += 1
    return stack.enter_context(k.nc.sbuf_tensor(f"{name}_{k.names}", shape, dtype))


def rows_of(dram, tiles):
    return dram.rearrange("(t p) n -> p t n", p=P)


def ctx_weights(k, stack, name, width):
    w = sb(k, stack, name, [P, 2, width])
    dram = k.w[name]
    return w, [(w[0:P, 0, :], dram[0:P, :]), (w[0:CTX - P, 1, :], dram[P:CTX, :])]


def weights(k, stack, name, tiles, width):
    w = sb(k, stack, name, [P, tiles, width])
    return w, [(w[:, :, :], rows_of(k.w[name], tiles))]


def bias_row(k, stack, name, width):
    w = sb(k, stack, name, [1, width])
    return w, [(w[0:1, :], k.w[name])]


def bias_columns(k, stack, name, tiles):
    w = sb(k, stack, name, [P, tiles])
    return w, [(w[:, :], k.w[name])]


def l0_attn(k):
    nc = k.nc
    H, W = 16, 16 * PAD
    T = W // P
    with ExitStack() as stack:
        attention_memory(k, stack)
        wq, a = weights(k, stack, "L0_attn_Wq", KD, W)
        wk, b = weights(k, stack, "L0_attn_Wk", KD, W)
        wv, c = weights(k, stack, "L0_attn_Wv", KD, W)
        wo, d = weights(k, stack, "L0_attn_Wo", T, DIM)
        bq, e = bias_columns(k, stack, "L0_attn_bq", T)
        bk, f = bias_columns(k, stack, "L0_attn_bk", T)
        bv, g_ = bias_row(k, stack, "L0_attn_bv", W)
        bo, h_ = bias_row(k, stack, "L0_attn_bo", DIM)
        qT, kT = ([sb(k, stack, n, [P, T, GT]) for _ in range(2)] for n in ("qT", "kT"))
        v = [sb(k, stack, "v", [P, GROUP, W]) for _ in range(2)]
        oT = sb(k, stack, "oT", [P, T, GT])
        k.future = sb(k, stack, "future", [P, 4, P], I32)
        k.minus = sb(k, stack, "minus", [P, 4, P])
        load_phase(k, a + b + c + d + e + f + g_ + h_ + [(k.future[:, :, :], k.w["future"])])
        with phase(k, "fill", "step") as (block, s):
            @block.vector
            def _(dve):
                nc.vector.memset(k.minus[:, :, :], -10000.0 * 4.0)

        def qkv(i):
            jobs = feature_jobs(qT[i], wq, k.xT, [P] * KD, W, bq) + feature_jobs(kT[i], wk, k.xT, [P] * KD, W, bk)
            return jobs + [(P, W, token_pairs(k, k.xT, [P] * KD, j, wv, slice(0, W), bv), turns(j), to_copy(v[i][:, j, :]))
                           for j in range(GROUP)]

        def head(t):
            return lambda j, h: t[PAD * (h % 4):PAD * (h % 4) + PAD, h // 4, sl(j)]

        def attend(i):
            return attention_part(k, H, PAD, head(qT[i]), head(kT[i]), lambda j, h: v[i][:, j, sl(h, PAD)],
                                  lambda j, u: oT[:, u:u + 1, sl(j)], 0.25, causal=True)
        attention_loop(k, qkv, attend, lambda g: residual_jobs(k, g, oT, T, wo, bo), context=False)


def attention_loop(k, qkv, attend, project, context):
    def norm_beside(g, *others):
        parts = [(norm_part(k, g, lambda kt: k.xT[:, kt, :], (4, 5)), 1)]
        if context:
            parts.append((context_part(k, g), 1))
        side_by_side(k, *others, *parts)

    def attend_beside(i):
        jobs = qkv(1 - i)
        side_by_side(k, (attend(i), 1), (gemm_part(k, "qkv", jobs, (6, 7)), max(1, len(jobs) / 16)))

    norm_beside(0)
    gemm_phase(k, "qkv", qkv(0))
    norm_beside(1)
    with k.nc.Fori(0, 2) as i:
        attend_beside(0)
        norm_beside(2 - 2 * i, (gemm_part(k, "project", project(2 * i), range(4)), 1))
        attend_beside(1)
        norm_beside(3 - 2 * i, (gemm_part(k, "project", project(2 * i + 1), range(4)), 1))


def cross_attention(k, layer, heads, wo_name, bo_name):
    nc = k.nc
    W = heads * 64
    T = W // P
    with ExitStack() as stack:
        attention_memory(k, stack)
        wq, a = weights(k, stack, f"{layer}_Wq", KD, W)
        wk, b = ctx_weights(k, stack, f"{layer}_Wk", W)
        wv, c = ctx_weights(k, stack, f"{layer}_Wv", W)
        wo, d = weights(k, stack, wo_name, T, DIM)
        bo, e = bias_row(k, stack, bo_name, DIM)
        qT, kT = ([sb(k, stack, n, [P, T, GT]) for _ in range(2)] for n in ("qT", "kT"))
        v = [sb(k, stack, "v", [P, GROUP, W]) for _ in range(2)]
        oT = sb(k, stack, "oT", [P, T, GT])
        load_phase(k, a + b + c + d + e)

        def qkv(i):
            jobs = feature_jobs(qT[i], wq, k.xT, [P] * KD, W) + feature_jobs(kT[i], wk, k.ctxG, CTX_ROWS, W)
            for j in range(GROUP):
                for c0 in range(0, W, 512):
                    jobs.append((P, 512, token_pairs(k, k.ctxG, CTX_ROWS, j, wv, slice(c0, c0 + 512)), turns(len(jobs)),
                                 to_copy(v[i][:, j, c0:c0 + 512])))
            return jobs

        def head(t):
            return lambda j, h: t[64 * (h % 2):64 * (h % 2) + 64, h // 2, sl(j)]

        def attend(i):
            return attention_part(k, heads, 64, head(qT[i]), head(kT[i]), lambda j, h: v[i][:, j, sl(h, 64)],
                                  lambda j, u: oT[:, 2 * u:2 * u + 2, sl(j)], 0.125)
        attention_loop(k, qkv, attend, lambda g: residual_jobs(k, g, oT, T, wo, bo), context=True)


def empty_phase(k):
    with phase(k, "turn", "none") as (block, s):
        pass


def context_part(k, g):
    part = Part("context", "none")

    @part.gpsimd
    def _(pool, s):
        k.nc.gpsimd.tensor_copy(k.ctxG[:, 0, :], k.ctxT[:, 0, bass.ds(g * GT, GT)])
        k.nc.gpsimd.tensor_copy(k.ctxG[0:CTX - P, 1, :], k.ctxT[0:CTX - P, 1, bass.ds(g * GT, GT)])
        yield
    return part


def l0_xattn(k):
    nc = k.nc
    H, W = 16, 16 * PAD
    T = W // P
    n = "L0_xattn_"
    with ExitStack() as stack:
        attention_memory(k, stack)
        wq, a = weights(k, stack, n + "Wq", KD, DIM)
        wk, b = ctx_weights(k, stack, n + "Wk", DIM)
        wv, c = ctx_weights(k, stack, n + "Wv", W)
        wo, d = weights(k, stack, n + "Wo", T, DIM)
        loads = a + b + c + d
        bq, bk, bo = (sb(k, stack, m, [1, DIM]) for m in ("bq", "bk", "bo"))
        bv = sb(k, stack, "bv", [1, W])
        gamma, beta = sb(k, stack, "gamma", [P, DIM]), sb(k, stack, "beta", [P, DIM])
        loads += [(bq[:, :], k.w[n + "bq"]), (bk[:, :], k.w[n + "bk"]), (bo[:, :], k.w[n + "bo"]), (bv[:, :], k.w[n + "bv"]),
                  (gamma[:, :], k.w[n + "ln_gamma"]), (beta[:, :], k.w[n + "ln_beta"])]
        qT, kT, oT = (sb(k, stack, m, [P, T, GT]) for m in ("qT", "kT", "oT"))
        v = [sb(k, stack, "v", [P, GROUP, W]) for _ in range(2)]
        qp = [sb(k, stack, "qp", [P, GROUP, DIM]) for _ in range(2)]
        kp, square, y = (sb(k, stack, m, [P, GROUP, DIM]) for m in ("kp", "square", "y"))
        padded = sb(k, stack, "padded", [P, 2, GROUP, W])
        length = sb(k, stack, "length", [P, 2, GROUP])
        load_phase(k, loads)
        with phase(k, "fill", "none") as (block, s):
            @block.vector
            def _(dve):
                nc.vector.memset(padded[:, :, :, :], 0.0)

        def qkv(i):
            jobs = []
            for j in range(GROUP):
                jobs.append((P, DIM, token_pairs(k, k.xT, [P] * KD, j, wq, slice(0, DIM), bq), "act", to_copy(qp[i][:, j, :])))
                jobs.append((P, DIM, token_pairs(k, k.ctxG, CTX_ROWS, j, wk, slice(0, DIM), bk), "dve", to_copy(kp[:, j, :])))
                jobs.append((P, W, token_pairs(k, k.ctxG, CTX_ROWS, j, wv, slice(0, W), bv), "act", to_copy(v[i][:, j, :])))
            return jobs

        def norm_and_context(g):
            return (norm_part(k, g, lambda kt: k.xT[:, kt, :], (4, 5)), 1), (context_part(k, g), 1)

        def head(t):
            return lambda j, h: t[PAD * (h % 4):PAD * (h % 4) + PAD, h // 4, sl(j)]

        side_by_side(k, *norm_and_context(0))
        gemm_phase(k, "qkv", qkv(0))
        side_by_side(k, *norm_and_context(1))
        side_by_side(k, (unit_part(k, qp[0], kp, square, length, padded, qT, kT), 1))
        with nc.Fori(0, 2) as half:
            for i in range(2):
                side_by_side(k, (attention_part(k, H, PAD, head(qT), head(kT), lambda j, h: v[i][:, j, sl(h, PAD)],
                                                lambda j, u: oT[:, u:u + 1, sl(j)], 0.25), 1),
                             (gemm_part(k, "qkv", qkv(1 - i), (6, 7)), 1))
                project = [(P, DIM, token_pairs(k, oT, [P] * T, j, wo, slice(0, DIM), bo), "dve",
                            to_sum(y[:, j, :], qp[i][:, j, :])) for j in range(GROUP)]
                side_by_side(k, (gemm_part(k, "project", project, range(4)), 1), *norm_and_context(2 + i - 2 * half))
                side_by_side(k, (unit_part(k, qp[1 - i], kp, square, length, padded, qT, kT), 1),
                             (outer_part(k, 2 * half + i, y, gamma, beta), 1))


def unit_part(k, qp, kp, square, length, padded, qT, kT):
    nc = k.nc
    T = padded.shape[3] // P
    part = Part("unit", "step squared rooted unit turned")

    @part.vector
    def _(dve, s):
        link = Link(dve, s["step"])
        for i, rows in enumerate((qp, kp)):
            for j in range(GROUP):
                last = nc.vector.tensor_tensor_reduce(square[:, j, :], rows[:, j, :], rows[:, j, :], 1.0, 0.0,
                                                      ALU.mult, ALU.add, length[:, i, j:j + 1])
            if i == 0:
                link(last)
        last.then_inc(s["squared"], 1)
        yield
        dve.wait_ge(s["rooted"], 1)
        link(nc.vector.tensor_scalar(length[:, :, :], length[:, :, :], 1e-12, None, ALU.max))
        link(nc.vector.reciprocal(length[:, :, :], length[:, :, :]))
        for i, rows in enumerate((qp, kp)):
            for j in range(GROUP):
                nc.vector.tensor_scalar(padded[:, i, j, :].rearrange("p (h d) -> p h d", d=PAD)[:, :, 0:16],
                                        rows[:, j, :].rearrange("p (h d) -> p h d", d=16),
                                        length[:, i, j:j + 1], None, ALU.mult).then_inc(s["unit"], 1)
        yield
        for m in range(T):
            dve.wait_ge(s["turned"], T + m + 1)
            nc.vector.tensor_copy(kT[:, m, :], k.ps[:, T + m, :])
            yield

    @part.scalar
    def _(act, s):
        act.wait_ge(s["squared"], 1)
        nc.scalar.activation(length[:, :, :], length[:, :, :], ACT.Sqrt).then_inc(s["rooted"], 1)
        yield
        yield
        for m in range(T):
            act.wait_ge(s["turned"], m + 1)
            nc.scalar.activation(qT[:, m, :], k.ps[:, m, :], ACT.Copy)
            yield

    @part.tensor
    def _(pe, s):
        for i in range(2):
            pe.wait_ge(s["unit"], GROUP * (i + 1))
            for m in range(T):
                for j in range(GROUP):
                    last = nc.tensor.transpose(k.ps[:, T * i + m, sl(j)], padded[:, i, j, sl(m)], k.ident[:, :])
                last.then_inc(s["turned"], 1)
                yield
    return part


def outer_part(k, g, y, gamma, beta):
    nc = k.nc
    part = Part("outer", "step measured rooted normed scaled")

    @part.vector
    def _(dve, s):
        link = Link(dve, s["step"])
        row_stats(k, dve, link, lambda j: y[:, j, :], s["measured"])
        yield
        dve.wait_ge(s["rooted"], 1)
        for j in range(GROUP):
            nc.vector.tensor_scalar(y[:, j, :], y[:, j, :], k.moments[:, j, 0:1], k.rstd[:, j:j + 1],
                                    ALU.subtract, ALU.mult).then_inc(s["normed"], 1)
        yield

    @part.scalar
    def _(act, s):
        row_rstd(k, act, s["measured"], s["rooted"])
        yield

    @part.gpsimd
    def _(pool, s):
        yield
        yield
        pool.wait_ge(s["normed"], GROUP)
        nc.gpsimd.tensor_tensor(y[:, :, :], y[:, :, :], gamma[:, :].unsqueeze(1).broadcast_to([P, GROUP, DIM]),
                                ALU.mult).then_inc(s["scaled"], 1)
        pool.wait_ge(s["scaled"], 1)
        nc.gpsimd.tensor_tensor(y[:, :, :], y[:, :, :], beta[:, :].unsqueeze(1).broadcast_to([P, GROUP, DIM]),
                                ALU.add).then_inc(s["scaled"], 1)
        pool.wait_ge(s["scaled"], 2)
        x = k.x[:, bass.ds(g * GROUP, GROUP), :]
        nc.gpsimd.tensor_tensor(x, x, y[:, :, :], ALU.add)
        yield
    return part


def keep_turned_phase(k, g, all_tokens):
    nc = k.nc
    with phase(k, "keep", "none") as (block, s):
        @block.vector
        def _(dve):
            nc.vector.tensor_copy(all_tokens[:, 0, bass.ds(g * GT, GT)], k.xT[:, 0, :])

        @block.scalar
        def _(act):
            nc.scalar.activation(all_tokens[:, 1, bass.ds(g * GT, GT)], k.xT[:, 1, :], ACT.Copy)


def l0_ffn(k):
    nc = k.nc
    E, TOP, INNER, SET = 32, 8, 128, 3
    SETS = (E + 1) // SET
    COLS = 2 * KD * INNER + DIM + 2
    n = "L0_ffn_"
    with ExitStack() as stack:
        wr, a = weights(k, stack, n + "Wr", KD, E)
        br, b = bias_row(k, stack, n + "br", E)
        bd = sb(k, stack, "bd", [E + 1, DIM])
        xA = sb(k, stack, "xA", [P, KD, TOKENS])
        share = sb(k, stack, "share", [P, BATCH, E + 1])
        affinity, rest = sb(k, stack, "affinity", [P, GROUP, E]), sb(k, stack, "rest", [P, GROUP, E])
        chosen = sb(k, stack, "chosen", [P, GROUP, E + 1])
        top, total = sb(k, stack, "top", [P, GROUP, TOP]), sb(k, stack, "total", [P, GROUP])
        chosenT = sb(k, stack, "chosenT", [E + 1, GROUP, P])
        experts = [sb(k, stack, f"experts{i}", [P, SET, COLS]) for i in range(2)]
        load_phase(k, a + b + [(bd[:, :], k.w[n + "bd"]), (experts[0][:, :, :], k.w[n + "experts"][0])])
        with phase(k, "fill", "none") as (block, s):
            @block.vector
            def _(dve):
                nc.vector.memset(chosen[:, :, :], 1.0)

        with nc.Fori(0, GROUPS) as g:
            norm_phase(k, g, lambda kt: k.xT[:, kt, :])
            keep_turned_phase(k, g, xA)

            def to_sigmoid(dst):
                return lambda nc, engine, bank: nc.scalar.activation(dst, bank, ACT.Sigmoid)
            gemm_phase(k, "router", [(P, E, token_pairs(k, k.xT, [P] * KD, j, wr, slice(0, E), br), "act",
                                      to_sigmoid(affinity[:, j, :])) for j in range(GROUP)])

            with phase(k, "choose", "step chosen") as (block, s):
                @block.vector
                def _(dve):
                    link = Link(dve, s["step"])
                    for j in range(GROUP):
                        last = nc.vector.max(top[:, j, :], affinity[:, j, :])
                    link(last)
                    for j in range(GROUP):
                        last = nc.vector.match_replace(rest[:, j, :], top[:, j, :], affinity[:, j, :], -1.0)
                    link(last)
                    link(nc.vector.tensor_reduce(total[:, :], top[:, :, :], AX.X, ALU.add))
                    link(nc.vector.tensor_scalar(total[:, :], total[:, :], 1e-9, None, ALU.add))
                    link(nc.vector.reciprocal(total[:, :], total[:, :]))
                    link(nc.vector.scalar_tensor_tensor(chosen[:, :, 0:E], rest[:, :, :], 0.0, affinity[:, :, :], ALU.is_lt, ALU.mult))
                    link(nc.vector.tensor_tensor(chosen[:, :, 0:E], chosen[:, :, 0:E],
                                                 total[:, :].unsqueeze(2).broadcast_to([P, GROUP, E]), ALU.mult))
                    nc.vector.tensor_copy(share[:, bass.ds(g * GROUP, GROUP), :], chosen[:, :, :])

            def turn_chosen(j):
                return lambda nc, bank: nc.tensor.transpose(bank, chosen[:, j, :], k.ident[:, :])
            gemm_phase(k, "turn", [(E + 1, P, turn_chosen(j), turns(j), to_copy(chosenT[:, j, :])) for j in range(GROUP)])

            jobs = []
            for j in range(GROUP):
                x = k.x[:, bass.ds(g * GROUP + j, 1), :]
                jobs.append((P, DIM, products([(chosenT[:, j, :], bd[:, :])]), "dve",
                             lambda nc, engine, bank, x=x: nc.vector.tensor_tensor(x, bank.rearrange("p (o d) -> p o d", o=1), x, ALU.add)))
            gemm_phase(k, "biases", jobs)

        with ExitStack() as inner:
            silu_gate = sb(k, inner, "silu_gate", [P, 2, GT])
            hidden = sb(k, inner, "hidden", [P, 2, GT])
            share_now = sb(k, inner, "share_now", [P, BATCH, SET])

            def set_phase(now, first, later=None):
                units = [(e, c) for e in range(SET) for c in range(GROUPS)]
                up_at = KD * INNER
                down_at = 2 * KD * INNER
                with phase(k, "experts", "loaded gated upped silued multiplied downed fetched added") as (block, s):
                    @block.sync
                    def _(sp):
                        if later is not None:
                            dst, index = later
                            sp.dma_start(dst[:, :, :].rearrange("p e c -> p (e c)"),
                                         k.w[n + "experts"].rearrange("i p e c -> (i p) (e c)")[bass.ds(index * P, P), :]).then_inc(s["loaded"], 16)
                            sp.wait_ge(s["loaded"], 16)

                    @block.tensor
                    def _(pe):
                        def down(m):
                            e, c = units[m]
                            pe.wait_ge(s["multiplied"], m + 1)
                            if m >= 2:
                                pe.wait_ge(s["added"], m - 1)
                            for j in range(GROUP):
                                last = nc.tensor.matmul(k.ps[:, 4 + 2 * (m % 2) + j // 2, sl(j % 2, DIM)], hidden[:, m % 2, sl(j)],
                                                        now[:, e, down_at:down_at + DIM], start=True, stop=True)
                            last.then_inc(s["downed"], 1)

                        for m, (e, c) in enumerate(units):
                            if m >= 2:
                                pe.wait_ge(s["silued"], m - 1)
                                pe.wait_ge(s["multiplied"], m - 1)
                            for at, base, sem in ((0, 0, s["gated"]), (up_at, 2, s["upped"])):
                                for kt in range(KD):
                                    last = nc.tensor.matmul(k.ps[:, base + m % 2, :], now[:, e, at + kt * INNER:at + (kt + 1) * INNER],
                                                            xA[:, kt, sl(c, GT)], start=kt == 0, stop=kt == KD - 1)
                                last.then_inc(sem, 1)
                            if m >= 1:
                                down(m - 1)
                        down(len(units) - 1)

                    @block.scalar
                    def _(act):
                        for m, (e, c) in enumerate(units):
                            act.wait_ge(s["gated"], m + 1)
                            if m >= 2:
                                act.wait_ge(s["multiplied"], m - 1)
                            nc.scalar.activation(silu_gate[:, m % 2, :], k.ps[:, m % 2, :], ACT.Silu,
                                                 bias=now[:, e, COLS - 2:COLS - 1]).then_inc(s["silued"], 1)

                    @block.vector
                    def _(dve):
                        nc.vector.tensor_copy(share_now[:, :, :], share[:, :, bass.ds(first, SET)]).then_inc(s["fetched"], 1)

                        def add(m):
                            e, c = units[m]
                            dve.wait_ge(s["downed"], m + 1)
                            if m == 0:
                                dve.wait_ge(s["fetched"], 1)
                            if m >= GROUPS:
                                dve.wait_ge(s["added"], m - GROUPS + 1)
                            for j in range(GROUP):
                                t = GROUP * c + j
                                last = nc.vector.scalar_tensor_tensor(k.x[:, t, :], k.ps[:, 4 + 2 * (m % 2) + j // 2, sl(j % 2, DIM)],
                                                                      share_now[:, t, e:e + 1], k.x[:, t, :], ALU.mult, ALU.add)
                            last.then_inc(s["added"], 1)

                        for m, (e, c) in enumerate(units):
                            dve.wait_ge(s["upped"], m + 1)
                            dve.wait_ge(s["silued"], m + 1)
                            if m >= 2:
                                dve.wait_ge(s["downed"], m - 1)
                            nc.vector.scalar_tensor_tensor(hidden[:, m % 2, :], k.ps[:, 2 + m % 2, :], now[:, e, COLS - 1:COLS],
                                                           silu_gate[:, m % 2, :], ALU.add, ALU.mult).then_inc(s["multiplied"], 1)
                            if m >= 1:
                                add(m - 1)
                        add(len(units) - 1)

            with nc.Fori(0, SETS // 2) as i:
                set_phase(experts[0], i * 2 * SET, (experts[1], 2 * i + 1))
                set_phase(experts[1], (2 * i + 1) * SET, (experts[0], 2 * i + 2))
            set_phase(experts[0], (SETS - 1) * SET)


def l2_ffn(k):
    nc = k.nc
    E, INNER, TOP = 8, 512, TOKENS // 8
    M = INNER // P
    n = "L2_ffn_"
    COLS = KD * INNER + M * DIM
    with ExitStack() as stack:
        wg, a = weights(k, stack, n + "Wg", KD, E)
        xA = sb(k, stack, "xA", [P, KD, TOKENS])
        share = sb(k, stack, "share", [P, BATCH, E])
        experts = [sb(k, stack, f"expert{i}", [P, COLS]) for i in range(2)]
        order = sb(k, stack, "order", [P, BATCH, E])
        logits = sb(k, stack, "logits", [P, GROUP, E])
        probs = sb(k, stack, "probs", [P, BATCH, E])
        load_phase(k, a + [(experts[0][:, :], k.w[n + "experts"][0]), (order[:, :, :], k.w["order"])])
        with nc.Fori(0, GROUPS) as g:
            norm_phase(k, g, lambda kt: k.xT[:, kt, :])
            keep_turned_phase(k, g, xA)
            gemm_phase(k, "router", [(P, E, token_pairs(k, k.xT, [P] * KD, j, wg, slice(0, E)), "act",
                                      to_copy(logits[:, j, :])) for j in range(GROUP)])
            with phase(k, "keep", "none") as (block, s):
                @block.vector
                def _(dve):
                    nc.vector.tensor_copy(probs[:, bass.ds(g * GROUP, GROUP), :], logits[:, :, :])

        with ExitStack() as inner:
            peak = sb(k, inner, "peak", [P, BATCH])
            first, second = sb(k, inner, "first", [P, BATCH, E]), sb(k, inner, "second", [P, BATCH, E])
            probsT, restT = sb(k, inner, "probsT", [E, TOKENS]), sb(k, inner, "restT", [E, TOKENS])
            best = sb(k, inner, "best", [E, 2, 8])
            all_e = [P, BATCH, E]

            def spread(t):
                return t[:, :].unsqueeze(2).broadcast_to(all_e)

            with phase(k, "softmax", "step shifted exped") as (block, s):
                @block.vector
                def _(dve):
                    link = Link(dve, s["step"])
                    link(nc.vector.tensor_reduce(peak[:, :], probs[:, :, :], AX.X, ALU.max))
                    nc.vector.tensor_tensor(first[:, :, :], probs[:, :, :], spread(peak), ALU.subtract).then_inc(s["shifted"], 1)
                    dve.wait_ge(s["exped"], 1)
                    link(nc.vector.tensor_reduce(peak[:, :], first[:, :, :], AX.X, ALU.add))
                    link(nc.vector.reciprocal(peak[:, :], peak[:, :]))
                    nc.vector.tensor_tensor(probs[:, :, :], first[:, :, :], spread(peak), ALU.mult)

                @block.scalar
                def _(act):
                    act.wait_ge(s["shifted"], 1)
                    nc.scalar.activation(first[:, :, :], first[:, :, :], ACT.Exp).then_inc(s["exped"], 1)

            def turn4(i, source, rows, columns):
                def fill(nc, bank):
                    for j in range(4):
                        last = nc.tensor.transpose(bank[:, j * columns:(j + 1) * columns], source(4 * i + j), k.ident[0:rows, 0:rows])
                    return last
                return fill
            gemm_phase(k, "turn", [(E, GT, turn4(i, lambda t: probs[:, t, :], P, P), turns(i), to_copy(probsT[:, sl(i, GT)]))
                                   for i in range(GROUPS)])

            with phase(k, "top", "step") as (block, s):
                @block.vector
                def _(dve):
                    link = Link(dve, s["step"])
                    for r in range(TOP // 8):
                        source = probsT if r == 0 else restT
                        link(nc.vector.max(best[:, r % 2, :], source[:, :]))
                        link(nc.vector.match_replace(restT[:, :], best[:, r % 2, :], source[:, :], -1.0))
            gemm_phase(k, "turn", [(P, 4 * E, turn4(i, lambda t: restT[:, sl(t)], E, E), turns(i),
                                    to_copy(first[:, sl(i, 4), :].rearrange("p t e -> p (t e)"))) for i in range(GROUPS)])

            with phase(k, "assign", "step") as (block, s):
                @block.vector
                def _(dve):
                    link = Link(dve, s["step"])
                    v = nc.vector
                    link(v.tensor_scalar(first[:, :, :], first[:, :, :], 0.0, None, ALU.is_lt))
                    link(v.tensor_reduce(peak[:, :], first[:, :, :], AX.X, ALU.max))
                    link(v.tensor_tensor(second[:, :, :], first[:, :, :], spread(peak), ALU.is_ge))
                    link(v.scalar_tensor_tensor(first[:, :, :], probs[:, :, :], 1.0, second[:, :, :], ALU.add, ALU.mult))
                    link(v.tensor_reduce(peak[:, :], first[:, :, :], AX.X, ALU.max))
                    link(v.tensor_tensor(second[:, :, :], first[:, :, :], spread(peak), ALU.is_equal))
                    link(v.tensor_tensor(second[:, :, :], second[:, :, :], order[:, :, :], ALU.mult))
                    link(v.tensor_reduce(peak[:, :], second[:, :, :], AX.X, ALU.max))
                    link(v.tensor_tensor(second[:, :, :], second[:, :, :], spread(peak), ALU.is_equal))
                    v.tensor_tensor(share[:, :, :], second[:, :, :], probs[:, :, :], ALU.mult)

        with ExitStack() as inner:
            hidden = sb(k, inner, "hidden", [P, 2, M, GT])
            share_now = sb(k, inner, "share_now", [P, BATCH])

            def expert_phase(now, e, later=None):
                with phase(k, "expert", "loaded upped gelued downed fetched added") as (block, s):
                    @block.sync
                    def _(sp):
                        if later is not None:
                            dst, index = later
                            sp.dma_start(dst[:, :], k.w[n + "experts"].rearrange("i p c -> (i p) c")[bass.ds(index * P, P), :]).then_inc(s["loaded"], 16)
                            sp.wait_ge(s["loaded"], 16)

                    @block.tensor
                    def _(pe):
                        def down(c):
                            pe.wait_ge(s["gelued"], M * (c + 1))
                            if c >= 2:
                                pe.wait_ge(s["added"], c - 1)
                            for j in range(GROUP):
                                for m in range(M):
                                    at = KD * INNER + m * DIM
                                    last = nc.tensor.matmul(k.ps[:, 4 + 2 * (c % 2) + j // 2, sl(j % 2, DIM)], hidden[:, c % 2, m, sl(j)],
                                                            now[:, at:at + DIM], start=m == 0, stop=m == M - 1)
                            last.then_inc(s["downed"], 1)

                        for c in range(GROUPS):
                            for m in range(M):
                                if c >= 1:
                                    pe.wait_ge(s["gelued"], M * (c - 1) + m + 1)
                                for kt in range(KD):
                                    at = kt * INNER + m * P
                                    last = nc.tensor.matmul(k.ps[:, m, :], now[:, at:at + P], xA[:, kt, sl(c, GT)],
                                                            start=kt == 0, stop=kt == KD - 1)
                                last.then_inc(s["upped"], 1)
                            if c >= 1:
                                down(c - 1)
                        down(GROUPS - 1)

                    @block.scalar
                    def _(act):
                        for c in range(GROUPS):
                            if c >= 2:
                                act.wait_ge(s["downed"], c - 1)
                            for m in range(M):
                                act.wait_ge(s["upped"], M * c + m + 1)
                                nc.scalar.activation(hidden[:, c % 2, m, :], k.ps[:, m, :], ACT.Gelu).then_inc(s["gelued"], 1)

                    @block.vector
                    def _(dve):
                        nc.vector.tensor_copy(share_now[:, :].unsqueeze(2), share[:, :, bass.ds(e, 1)]).then_inc(s["fetched"], 1)
                        dve.wait_ge(s["fetched"], 1)
                        for c in range(GROUPS):
                            dve.wait_ge(s["downed"], c + 1)
                            for j in range(GROUP):
                                t = GROUP * c + j
                                last = nc.vector.scalar_tensor_tensor(k.x[:, t, :], k.ps[:, 4 + 2 * (c % 2) + j // 2, sl(j % 2, DIM)],
                                                                      share_now[:, t:t + 1], k.x[:, t, :], ALU.mult, ALU.add)
                            last.then_inc(s["added"], 1)

            with nc.Fori(0, E // 2 - 1) as i:
                expert_phase(experts[0], 2 * i, (experts[1], 2 * i + 1))
                expert_phase(experts[1], 2 * i + 1, (experts[0], 2 * i + 2))
            expert_phase(experts[0], E - 2, (experts[1], E - 1))
            expert_phase(experts[1], E - 1)


def l3_ffn(k):
    nc = k.nc
    INNER, RANK = 1024, 16
    M = INNER // P
    n = "L3_ffn_"
    with ExitStack() as stack:
        wf, a = weights(k, stack, n + "W_fc", KD, INNER)
        wp, b = weights(k, stack, n + "W_proj", M, DIM)
        bf, c = bias_columns(k, stack, n + "b_fc", M)
        bp, d = bias_row(k, stack, n + "b_proj", DIM)
        af, bfT = sb(k, stack, "af", [RANK, DIM]), sb(k, stack, "bfT", [RANK, INNER])
        ap, bpT = sb(k, stack, "ap", [RANK, INNER]), sb(k, stack, "bpT", [RANK, DIM])
        load_phase(k, a + b + c + d + [(af[:, :], k.w[n + "A_fc"]), (bfT[:, :], k.w[n + "B_fc"]),
                                       (ap[:, :], k.w[n + "A_proj"]), (bpT[:, :], k.w[n + "B_proj"])])
        hT = sb(k, stack, "hT", [P, M, GT])
        size = sb(k, stack, "size", [P, 2, 4])
        row_ = sb(k, stack, "row", [1, 4])

        for which, w in enumerate((wf, wp)):
            flat = w[:, :, :]
            peak, step, inverse = size[:, which, 0:1], size[:, which, 1:2], size[:, which, 2:3]
            with phase(k, "round", "step peaked turned maxed spread") as (block, s):
                @block.vector
                def _(dve):
                    link = Link(dve, s["step"])
                    v = nc.vector
                    v.tensor_reduce(peak, w[:, :, :], AX.XY, ALU.max, apply_absolute_value=True).then_inc(s["peaked"], 1)
                    dve.wait_ge(s["turned"], 1)
                    link(v.tensor_reduce(row_[:, 0:1], k.ps[0:1, 0, 0:P], AX.X, ALU.max))
                    v.tensor_scalar(row_[:, 1:2], row_[:, 0:1], 1.0 / 127.0, None, ALU.mult).then_inc(s["maxed"], 1)
                    dve.wait_ge(s["spread"], 1)
                    link(v.tensor_copy(step, k.ps[:, 1, 0:1]))
                    link(v.reciprocal(inverse, step))
                    link(v.tensor_scalar(flat, flat, inverse, MAGIC, ALU.mult, ALU.add))
                    link(v.tensor_scalar(flat, flat, MAGIC, 127.0, ALU.subtract, ALU.min))
                    v.tensor_scalar(flat, flat, -128.0, step, ALU.max, ALU.mult)

                @block.tensor
                def _(pe):
                    pe.wait_ge(s["peaked"], 1)
                    nc.tensor.transpose(k.ps[0:1, 0, 0:P], peak, k.ident[:, :]).then_inc(s["turned"], 1)
                    pe.wait_ge(s["maxed"], 1)
                    nc.tensor.matmul(k.ps[:, 1, 0:1], k.ones[0:1, 0:P], row_[:, 1:2], start=True, stop=True).then_inc(s["spread"], 1)

        def to_twice(dst):
            return lambda nc, engine, bank: nc.vector.scalar_tensor_tensor(dst, bank, 2.0, dst, ALU.mult, ALU.add)
        jobs = [(P, 512, products([(af[:, sl(kt)], bfT[:, sl(c, 512)])]), "dve", to_twice(wf[:, kt, sl(c, 512)]))
                for kt in range(KD) for c in range(INNER // 512)]
        jobs += [(P, DIM, products([(ap[:, sl(m)], bpT[:, :])]), "dve", to_twice(wp[:, m, :])) for m in range(M)]
        gemm_phase(k, "lora", jobs)

        def to_gelu(m):
            return lambda nc, engine, bank: nc.scalar.activation(hT[:, m, :], bank, ACT.Gelu, bias=bf[:, m:m + 1])
        with nc.Fori(0, GROUPS) as g:
            norm_phase(k, g, lambda kt: k.xT[:, kt, :])
            gemm_phase(k, "up", [(P, GT, products([(wf[:, kt, sl(m)], k.xT[:, kt, :]) for kt in range(KD)]), "act", to_gelu(m))
                                 for m in range(M)])
            gemm_phase(k, "down", residual_jobs(k, g, hT, M, wp, bp))
            empty_phase(k)


def l1_attn(k):
    nc = k.nc
    H, D, C = 16, 16, 64
    PAIRS, T = H // 2, H * PAD // P
    VW = D + 1
    n = "L1_attn_"
    with ExitStack() as stack:
        wq, a = weights(k, stack, n + "W_q", KD, H * PAD)
        wk, b = weights(k, stack, n + "W_k", KD, H * PAD)
        wv, c = weights(k, stack, n + "W_v", KD, DIM)
        wo, d = weights(k, stack, n + "W_o", KD, DIM)
        centers, e = sb(k, stack, "centers", [P, PAIRS, P]), None
        where = sb(k, stack, "where", [P, PAIRS, P])
        scales, amplitude = sb(k, stack, "scales", [P, PAIRS]), sb(k, stack, "amplitude", [P, PAIRS])
        center2 = sb(k, stack, "center2", [P, PAIRS])
        qT, kT = (sb(k, stack, m, [P, T, GT]) for m in ("qT", "kT"))
        square = [sb(k, stack, f"square{i}", [P, T, GT]) for i in range(2)]
        near = [sb(k, stack, f"near{i}", [P, PAIRS, GT]) for i in range(2)]
        keysT = sb(k, stack, "keysT", [P, GROUP, PAIRS, P])
        values = sb(k, stack, "values", [P, GROUP, H, VW])
        pooled = sb(k, stack, "pooled", [P, GROUP, PAIRS, 2 * VW])
        share = sb(k, stack, "share", [P, GROUP, H])
        mixed = sb(k, stack, "mixed", [P, GROUP, DIM])
        oT = sb(k, stack, "oT", [P, KD, GT])
        load_phase(k, a + b + c + d + [(centers[:, :, :], k.w[n + "centers"]), (where[:, :, :], k.w[n + "where"]),
                                       (scales[:, :], k.w[n + "log_scales"]), (amplitude[:, :], k.w[n + "amplitudes"])])
        with phase(k, "centers", "step exped squared summed") as (block, s):
            @block.vector
            def _(dve):
                link = Link(dve, s["step"])
                v = nc.vector
                v.tensor_tensor(near[0][:, :, 0:P], centers[:, :, :], centers[:, :, :], ALU.mult).then_inc(s["squared"], 1)
                v.memset(values[:, :, :, :], 1.0)
                v.memset(pooled[:, :, :, :], 0.0)
                dve.wait_ge(s["exped"], 1)
                link(v.tensor_scalar(scales[:, :], scales[:, :], 1e-3, None, ALU.max))
                link(v.tensor_tensor(scales[:, :], scales[:, :], scales[:, :], ALU.mult))
                link(v.reciprocal(scales[:, :], scales[:, :]))
                v.tensor_scalar(scales[:, :], scales[:, :], -0.5, None, ALU.mult)
                v.tensor_tensor(amplitude[:, :], amplitude[:, :], amplitude[:, :], ALU.mult)
                dve.wait_ge(s["summed"], 1)
                v.tensor_copy(center2[:, :], k.ps[:, 0, 0:PAIRS])
                v.tensor_scalar(centers[:, :, :], centers[:, :, :], -2.0, None, ALU.mult)

            @block.scalar
            def _(act):
                nc.scalar.activation(scales[:, :], scales[:, :], ACT.Exp).then_inc(s["exped"], 1)

            @block.tensor
            def _(pe):
                pe.wait_ge(s["squared"], 1)
                for p in range(PAIRS):
                    last = nc.tensor.matmul(k.ps[:, 0, p:p + 1], near[0][:, p, 0:P], k.ones[:, 0:1], start=True, stop=True)
                last.then_inc(s["summed"], 1)

        with nc.Fori(0, GROUPS) as g:
            norm_phase(k, g, lambda kt: k.xT[:, kt, :])
            jobs = feature_jobs(qT, wq, k.xT, [P] * KD, H * PAD) + feature_jobs(kT, wk, k.xT, [P] * KD, H * PAD)

            def to_values(j):
                def evacuate(nc, engine, bank):
                    source, dst = bank.rearrange("p (h d) -> p h d", d=D), values[:, j, :, 0:D]
                    if engine == "act":
                        return nc.scalar.activation(dst, source, ACT.Copy)
                    return nc.vector.tensor_copy(dst, source)
                return evacuate
            jobs += [(P, DIM, token_pairs(k, k.xT, [P] * KD, j, wv, slice(0, DIM)), turns(j), to_values(j)) for j in range(GROUP)]
            gemm_phase(k, "qkv", jobs)

            with phase(k, "affinity", "squared keys_squared measured bounded") as (block, s):
                jobs = [(side, p) for side in range(2) for p in range(PAIRS)]

                @block.scalar
                def _(act):
                    nc.scalar.activation(square[0][:, :, :], qT[:, :, :], ACT.Square).then_inc(s["squared"], 1)
                    for m, (side, p) in enumerate(jobs):
                        act.wait_ge(s["bounded"], m + 1)
                        nc.scalar.activation(near[side][:, p, :], near[side][:, p, :], ACT.Exp, scale=scales[:, p:p + 1])

                @block.gpsimd
                def _(pool):
                    nc.gpsimd.tensor_tensor(square[1][:, :, :], kT[:, :, :], kT[:, :, :], ALU.mult).then_inc(s["keys_squared"], 1)

                @block.tensor
                def _(pe):
                    for m, (side, p) in enumerate(jobs):
                        if p == 0:
                            pe.wait_ge((s["squared"], s["keys_squared"])[side], 1)
                        if m >= 8:
                            pe.wait_ge(s["bounded"], m - 7)
                        source = (qT, kT)[side]
                        nc.tensor.matmul(k.ps[:, m % 8, :], centers[:, p, :], source[:, p // 2, :], start=True, stop=False)
                        nc.tensor.matmul(k.ps[:, m % 8, :], where[:, p, :], square[side][:, p // 2, :],
                                         start=False, stop=True).then_inc(s["measured"], 1)

                @block.vector
                def _(dve):
                    for m, (side, p) in enumerate(jobs):
                        dve.wait_ge(s["measured"], m + 1)
                        nc.vector.tensor_scalar(near[side][:, p, :], k.ps[:, m % 8, :], center2[:, p:p + 1], 0.0,
                                                ALU.add, ALU.max).then_inc(s["bounded"], 1)

            gemm_phase(k, "turn", [(P, GT, turned([near[1][:, 4 * i + p, sl(j)] for p in range(4)], k.ident[:, :]),
                                    turns(i), to_copy(keysT[:, j, sl(i, 4), :].rearrange("p a b -> p (a b)")))
                                   for j in range(GROUP) for i in range(PAIRS // 4)])

            def pool_values(j):
                def fill(nc, bank):
                    for p in range(PAIRS):
                        last = nc.tensor.matmul(bank[:, sl(p, 2 * VW)], keysT[:, j, p, :],
                                                values[:, j, sl(p, 2), :].rearrange("p h d -> p (h d)"), start=True, stop=True)
                    return last
                return fill

            def to_pooled(j):
                def evacuate(nc, engine, bank):
                    for i in range(2):
                        rows = slice(C * i, C * i + C)
                        source = bank[rows, :].rearrange("p (a d) -> p a d", d=2 * VW)[:, :, sl(i, VW)]
                        last = nc.vector.tensor_tensor(pooled[rows, j, :, sl(i, VW)], source,
                                                       amplitude[rows, :].unsqueeze(2).broadcast_to([C, PAIRS, VW]), ALU.mult)
                    return last
                return evacuate
            gemm_phase(k, "pool", [(P, H * VW, pool_values(j), "dve", to_pooled(j)) for j in range(GROUP)])

            with phase(k, "mix", "step mixed divided turned") as (block, s):
                @block.tensor
                def _(pe):
                    for j in range(GROUP):
                        for p in range(PAIRS):
                            last = nc.tensor.matmul(k.ps[:, j, sl(p, 2 * VW)], near[0][:, p, sl(j)], pooled[:, j, p, :], start=True, stop=True)
                        last.then_inc(s["mixed"], 1)
                    for j in range(GROUP):
                        pe.wait_ge(s["divided"], j + 1)
                        for kt in range(KD):
                            last = nc.tensor.transpose(k.ps[:, 4 + kt, sl(j)], mixed[:, j, sl(kt)], k.ident[:, :])
                        last.then_inc(s["turned"], 1)

                @block.vector
                def _(dve):
                    link = Link(dve, s["step"])
                    for j in range(GROUP):
                        dve.wait_ge(s["mixed"], j + 1)
                        bank = k.ps[:, j, 0:H * VW].rearrange("p (h d) -> p h d", d=VW)
                        link(nc.vector.tensor_scalar(share[:, j, :].unsqueeze(2), bank[:, :, D:VW], 1e-6, None, ALU.add))
                        link(nc.vector.reciprocal(share[:, j, :], share[:, j, :]))
                        nc.vector.tensor_tensor(mixed[:, j, :].rearrange("p (h d) -> p h d", d=D), bank[:, :, 0:D],
                                                share[:, j, :].unsqueeze(2).broadcast_to([P, H, D]), ALU.mult).then_inc(s["divided"], 1)
                    dve.wait_ge(s["turned"], GROUP)
                    nc.vector.tensor_copy(oT[:, 1, :], k.ps[:, 5, :])

                @block.scalar
                def _(act):
                    act.wait_ge(s["turned"], GROUP)
                    nc.scalar.activation(oT[:, 0, :], k.ps[:, 4, :], ACT.Copy)
            gemm_phase(k, "project", residual_jobs(k, g, oT, KD, wo))
            empty_phase(k)


def l1_ffn(k):
    nc = k.nc
    INNER = 1024
    M = INNER // P
    n = "L1_ffn_"
    with ExitStack() as stack:
        wg, a = weights(k, stack, n + "w_gate", KD, INNER)
        wu, b = weights(k, stack, n + "w_up", KD, INNER)
        wd, c = weights(k, stack, n + "w_down", M, DIM)
        ternary = [sb(k, stack, f"ternary{i}", [P, 2 * INNER], BF16) for i in range(3)]
        size = sb(k, stack, "size", [P, 3, 3])
        identb = sb(k, stack, "identb", [P, P], BF16)
        rows = sb(k, stack, "rows", [P, GROUP, INNER])
        gate = sb(k, stack, "gate", [P, GROUP, INNER])
        rounded = sb(k, stack, "rounded", [P, GROUP, INNER], BF16)
        roundedT = sb(k, stack, "roundedT", [P, M, GT], BF16)
        peak, inverse = sb(k, stack, "peak", [P, GROUP]), sb(k, stack, "inverse", [P, GROUP])
        factor = sb(k, stack, "factor", [P, 3, GROUP])
        load_phase(k, a + b + c)
        flat = [w[:, :, :].rearrange("p a b -> p (a b)") for w in (wg, wu, wd)]
        with phase(k, "ternary", "step summed spread") as (block, s):
            @block.vector
            def _(dve):
                link = Link(dve, s["step"])
                v = nc.vector
                v.tensor_copy(identb[:, :], k.ident[:, :])
                for i in range(3):
                    last = v.tensor_reduce(size[:, i, 0:1], flat[i], AX.X, ALU.add, apply_absolute_value=True)
                last.then_inc(s["summed"], 1)
                dve.wait_ge(s["spread"], 1)
                link(v.tensor_scalar(size[:, :, 1], k.ps[:, 0, 0:3], 1.0 / (DIM * INNER), 1e-5, ALU.mult, ALU.max))
                link(v.reciprocal(size[:, :, 2], size[:, :, 1]))
                for i in range(3):
                    link(v.tensor_scalar(flat[i], flat[i], size[:, i, 2:3], MAGIC, ALU.mult, ALU.add))
                    link(v.tensor_scalar(flat[i], flat[i], MAGIC, 1.0, ALU.subtract, ALU.min))
                    v.tensor_scalar(ternary[i][:, :], flat[i], -1.0, None, ALU.max)

            @block.tensor
            def _(pe):
                pe.wait_ge(s["summed"], 1)
                nc.tensor.matmul(k.ps[:, 0, 0:3], k.ones[:, :], size[:, :, 0], start=True, stop=True).then_inc(s["spread"], 1)

        def round_rows(dve, link, source, width):
            v = nc.vector
            rows_ = source[:, :, 0:width]
            link(v.tensor_reduce(peak[:, :], rows_, AX.X, ALU.max, apply_absolute_value=True))
            link(v.tensor_scalar(peak[:, :], peak[:, :], 1e-5, None, ALU.max))
            link(v.reciprocal(inverse[:, :], peak[:, :]))
            link(v.tensor_scalar(inverse[:, :], inverse[:, :], 127.0, None, ALU.mult))
            for j in range(GROUP):
                last = v.tensor_scalar(source[:, j, 0:width], source[:, j, 0:width], inverse[:, j:j + 1], MAGIC, ALU.mult, ALU.add)
            link(last)
            link(v.tensor_scalar(rounded[:, :, 0:width], rows_, MAGIC, 127.0, ALU.subtract, ALU.min))
            for i in range(3):
                last = v.tensor_scalar(factor[:, i, :], peak[:, :], 1.0 / 127.0, size[:, i, 1:2], ALU.mult, ALU.mult)
            link(last)

        def turn_jobs(width):
            return [(P, GT // 2, turned([rounded[:, j, sl(m)] for j in range(GROUP)], identb[:, :]), turns(m),
                     lambda nc, engine, bank, m=m: to_copy(roundedT[:, m, :])(nc, engine, bank.bitcast(BF16)))
                    for m in range(width // P)]

        with nc.Fori(0, GROUPS) as g:
            with phase(k, "norm", "step measured rooted") as (block, s):
                def source(j):
                    return k.x[:, bass.ds(g * GROUP + j, 1), :].rearrange("p o d -> p (o d)")

                @block.vector
                def _(dve):
                    link = Link(dve, s["step"])
                    row_stats(k, dve, link, source, s["measured"])
                    dve.wait_ge(s["rooted"], 1)
                    for j in range(GROUP):
                        last = nc.vector.tensor_scalar(k.normed[:, j, :], source(j), k.moments[:, j, 0:1], k.rstd[:, j:j + 1],
                                                       ALU.subtract, ALU.mult)
                    link(last)
                    round_rows(dve, link, k.normed, DIM)

                @block.scalar
                def _(act):
                    row_rstd(k, act, s["measured"], s["rooted"])
            gemm_phase(k, "turn", turn_jobs(DIM))

            with phase(k, "up", "gated upped silued multiplied") as (block, s):
                units = [(j, c) for j in range(GROUP) for c in range(INNER // 512)]

                @block.tensor
                def _(pe):
                    for m, (j, c) in enumerate(units):
                        if m >= 4:
                            pe.wait_ge(s["silued"], m - 3)
                            pe.wait_ge(s["multiplied"], m - 3)
                        for i, sem in enumerate((s["gated"], s["upped"])):
                            for kt in range(KD):
                                last = nc.tensor.matmul(k.ps[:, 4 * i + m % 4, :], roundedT[:, kt, sl(j)],
                                                        ternary[i][:, kt * INNER + c * 512:kt * INNER + (c + 1) * 512],
                                                        start=kt == 0, stop=kt == KD - 1)
                            last.then_inc(sem, 1)

                @block.scalar
                def _(act):
                    for m, (j, c) in enumerate(units):
                        act.wait_ge(s["gated"], m + 1)
                        nc.scalar.activation(gate[:, j, sl(c, 512)], k.ps[:, m % 4, :], ACT.Silu,
                                             scale=factor[:, 0, j:j + 1]).then_inc(s["silued"], 1)

                @block.vector
                def _(dve):
                    for m, (j, c) in enumerate(units):
                        dve.wait_ge(s["upped"], m + 1)
                        dve.wait_ge(s["silued"], m + 1)
                        nc.vector.scalar_tensor_tensor(rows[:, j, sl(c, 512)], k.ps[:, 4 + m % 4, :], factor[:, 1, j:j + 1],
                                                       gate[:, j, sl(c, 512)], ALU.mult, ALU.mult).then_inc(s["multiplied"], 1)

            with phase(k, "round", "step") as (block, s):
                @block.vector
                def _(dve):
                    round_rows(dve, Link(dve, s["step"]), rows, INNER)
            gemm_phase(k, "turn", turn_jobs(INNER))

            jobs = []
            for j in range(GROUP):
                x = k.x[:, bass.ds(g * GROUP + j, 1), :]
                jobs.append((P, DIM, products([(roundedT[:, m, sl(j)], ternary[2][:, sl(m, DIM)]) for m in range(M)]), "dve",
                             lambda nc, engine, bank, x=x, j=j: nc.vector.scalar_tensor_tensor(
                                 x, bank.rearrange("p (o d) -> p o d", o=1), factor[:, 2, j:j + 1], x, ALU.mult, ALU.add)))
            gemm_phase(k, "down", jobs)


def l2_attn(k):
    nc = k.nc
    INNER, STATE, HEADS, WIDTH, TAPS = 512, 128, 8, 64, 4
    M, CH = INNER // P, (INNER + 2 * STATE) // P
    COLS = 2 * INNER + 2 * STATE + HEADS
    LONG = SEQ + TAPS - 1
    n = "L2_attn_"
    ways = "fb"
    with ExitStack() as stack:
        in_w = {d: weights(k, stack, f"{n}{d}_in_w", KD, COLS) for d in ways}
        folded = {d: sb(k, stack, f"folded_{d}", [P, M, DIM]) for d in ways}
        small = {}
        loads = []
        for d in ways:
            loads += in_w[d][1]
            for name, shape in (("conv_w", [P, CH, TAPS]), ("conv_b", [P, CH]), ("A", [P, HEADS]), ("D", [P, HEADS]),
                                ("dt_bias", [1, HEADS]), ("mask", [P, P])):
                small[d, name] = sb(k, stack, f"{name}_{d}", shape)
                loads.append((small[d, name][tuple(slice(None) for _ in shape)], k.w[f"{n}{d}_{name}"]))
        norm_w, a = bias_columns(k, stack, n + "norm_w", KD)
        out_b, b = bias_row(k, stack, n + "out_b", DIM)
        select = sb(k, stack, "select", [HEADS, HEADS, P])
        loads += a + b + [(select[:, :, :], k.w[n + "select"])]
        with ExitStack() as inner:
            out_w = {d: weights(k, inner, f"{n}{d}_out_w", KD, INNER) for d in ways}
            block_w = {d: weights(k, inner, f"{n}{d}_block_w", KD, DIM) for d in ways}
            gnorm = {d: bias_columns(k, inner, f"{n}{d}_gnorm_w", M) for d in ways}
            for d in ways:
                loads += out_w[d][1] + block_w[d][1] + gnorm[d][1]
            load_phase(k, loads)

            def to_scaled(dst, scale):
                return lambda nc, engine, bank: nc.vector.tensor_scalar(dst, bank, scale, None, ALU.mult)
            gemm_phase(k, "fold", [(P, DIM, products([(out_w[d][0][:, kt, sl(m)], block_w[d][0][:, kt, :]) for kt in range(KD)]),
                                    "dve", to_scaled(folded[d][:, m, :], gnorm[d][0][:, m:m + 1])) for d in ways for m in range(M)])

        square = sb(k, stack, "square", [P, DIM])
        around = {d: sb(k, stack, f"around_{d}", [P, CH, GROUP, LONG]) for d in ways}
        conved = sb(k, stack, "conved", [P, CH, GT])
        gate = sb(k, stack, "gate", [P, GROUP, INNER])
        raw, dt, decay, e, u, miss, late, total = (sb(k, stack, m, [P, GROUP, HEADS])
                                                   for m in ("raw", "dt", "decay", "e", "u", "miss", "late", "total"))
        totalT = sb(k, stack, "totalT", [HEADS, GT])
        pairs = sb(k, stack, "pairs", [P, GROUP, P])
        inputs, skipped = sb(k, stack, "inputs", [P, GROUP, INNER]), sb(k, stack, "skipped", [P, GROUP, INNER])
        LB = 4
        lasting = sb(k, stack, "lasting", [P, LB, GROUP, P])
        y = sb(k, stack, "y", [P, GROUP, INNER])
        yT = {d: sb(k, stack, f"yT_{d}", [P, M, GT]) for d in ways}
        with phase(k, "rates", "exped") as (block, s):
            @block.scalar
            def _(act):
                for d in ways:
                    last = nc.scalar.activation(small[d, "A"][:, :], small[d, "A"][:, :], ACT.Exp)
                last.then_inc(s["exped"], 1)

            @block.vector
            def _(dve):
                for d in ways:
                    nc.vector.memset(around[d][:, :, :, :], 0.0)
                dve.wait_ge(s["exped"], 1)
                for d in ways:
                    nc.vector.tensor_scalar(small[d, "A"][:, :], small[d, "A"][:, :], -1.0, None, ALU.mult)

        with nc.Fori(0, GROUPS) as g:
            with phase(k, "norm", "step measured rooted squared rooted2 normed turned") as (block, s):
                x4 = k.x[:, bass.ds(g * GROUP, GROUP), :]

                def source(j):
                    return k.x[:, bass.ds(g * GROUP + j, 1), :].rearrange("p o d -> p (o d)")

                @block.vector
                def _(dve):
                    link = Link(dve, s["step"])
                    row_stats(k, dve, link, source, s["measured"])
                    dve.wait_ge(s["rooted"], 1)
                    for j in range(GROUP):
                        last = nc.vector.tensor_scalar(k.normed[:, j, :], source(j), k.moments[:, j, 0:1], k.rstd[:, j:j + 1],
                                                       ALU.subtract, ALU.mult)
                    link(last)
                    nc.vector.tensor_tensor(x4, x4, k.normed[:, :, :], ALU.add)
                    for j in range(GROUP):
                        last = nc.vector.tensor_tensor_reduce(y[:, j, 0:DIM], k.normed[:, j, :], k.normed[:, j, :], 1.0, 0.0,
                                                              ALU.mult, ALU.add, k.rstd[:, j:j + 1])
                    link(last)
                    link(nc.vector.tensor_scalar(k.rstd[:, :], k.rstd[:, :], 1.0 / DIM, LN_EPS, ALU.mult, ALU.add))
                    nc.vector.reciprocal(k.rstd[:, :], k.rstd[:, :]).then_inc(s["squared"], 1)
                    dve.wait_ge(s["rooted2"], 1)
                    for j in range(GROUP):
                        nc.vector.tensor_scalar(k.normed[:, j, :], k.normed[:, j, :], k.rstd[:, j:j + 1], None, ALU.mult).then_inc(s["normed"], 1)
                    dve.wait_ge(s["turned"], GROUP)
                    nc.vector.tensor_scalar(k.xT[:, 1, :], k.ps[:, 1, :], norm_w[:, 1:2], None, ALU.mult)

                @block.scalar
                def _(act):
                    row_rstd(k, act, s["measured"], s["rooted"])
                    row_rstd(k, act, s["squared"], s["rooted2"])
                    act.wait_ge(s["turned"], GROUP)
                    nc.scalar.activation(k.xT[:, 0, :], k.ps[:, 0, :], ACT.Copy, scale=norm_w[:, 0:1])

                @block.tensor
                def _(pe):
                    for j in range(GROUP):
                        pe.wait_ge(s["normed"], j + 1)
                        for kt in range(KD):
                            last = nc.tensor.transpose(k.ps[:, kt, sl(j)], k.normed[:, j, sl(kt)], k.ident[:, :])
                        last.then_inc(s["turned"], 1)

            for d in ways:
                w = in_w[d][0]
                lead = TAPS - 1 if d == "f" else 0

                def to_silu(dst):
                    return lambda nc, engine, bank: nc.scalar.activation(dst, bank, ACT.Silu)

                def to_around(m):
                    return lambda nc, engine, bank: nc.vector.tensor_copy(around[d][:, m, :, lead:lead + SEQ],
                                                                          bank.rearrange("p (j t) -> p j t", j=GROUP))
                jobs = []
                for j in range(GROUP):
                    jobs.append((P, INNER, token_pairs(k, k.xT, [P] * KD, j, w, slice(0, INNER)), "act", to_silu(gate[:, j, :])))
                    pairs_dt = [(k.xT[:, kt, sl(j)], w[:, kt, COLS - HEADS:COLS]) for kt in range(KD)]
                    pairs_dt.append((k.ones[0:1, 0:P], small[d, "dt_bias"][0:1, :]))
                    jobs.append((P, HEADS, products(pairs_dt), "dve", to_copy(raw[:, j, :])))
                for m in range(CH):
                    jobs.append((P, GT, products([(w[:, kt, INNER + m * P:INNER + (m + 1) * P], k.xT[:, kt, :]) for kt in range(KD)]),
                                 "dve", to_around(m)))
                gemm_phase(k, "in", jobs)

                with phase(k, "conv", "step sized exped plussed logged conved") as (block, s):
                    @block.vector
                    def _(dve):
                        link = Link(dve, s["step"])
                        v = nc.vector
                        for m in range(CH):
                            out = conved[:, m, :].rearrange("p (j t) -> p j t", j=GROUP)
                            for tap in range(TAPS):
                                at = tap if d == "f" else TAPS - 1 - tap
                                window, weight = around[d][:, m, :, at:at + SEQ], small[d, "conv_w"][:, m, tap:tap + 1]
                                if tap == 0:
                                    last = v.tensor_scalar(out, window, weight, None, ALU.mult)
                                else:
                                    last = v.scalar_tensor_tensor(out, window, weight, out, ALU.mult, ALU.add)
                                if tap < TAPS - 1:
                                    link(last)
                            last.then_inc(s["conved"], 1)
                        dve.wait_ge(s["exped"], 1)
                        v.tensor_scalar(u[:, :, :], e[:, :, :], 1.0, None, ALU.add).then_inc(s["plussed"], 1)
                        dve.wait_ge(s["plussed"], 1)
                        link(v.tensor_scalar(late[:, :, :], u[:, :, :], 1.0, None, ALU.subtract))
                        link(v.tensor_scalar(miss[:, :, :], late[:, :, :], 0.0, None, ALU.is_equal))
                        link(v.tensor_tensor(late[:, :, :], late[:, :, :], miss[:, :, :], ALU.add))
                        link(v.reciprocal(late[:, :, :], late[:, :, :]))
                        link(v.tensor_tensor(late[:, :, :], late[:, :, :], e[:, :, :], ALU.mult))
                        link(v.tensor_tensor(miss[:, :, :], miss[:, :, :], e[:, :, :], ALU.mult))
                        dve.wait_ge(s["logged"], 1)
                        link(v.tensor_tensor(u[:, :, :], u[:, :, :], late[:, :, :], ALU.mult))
                        link(v.tensor_tensor(u[:, :, :], u[:, :, :], miss[:, :, :], ALU.add))
                        link(v.scalar_tensor_tensor(dt[:, :, :], raw[:, :, :], 0.0, u[:, :, :], ALU.max, ALU.add))
                        v.tensor_tensor(decay[:, :, :], dt[:, :, :], small[d, "A"][:, :].unsqueeze(1).broadcast_to([P, GROUP, HEADS]),
                                        ALU.mult)

                    @block.scalar
                    def _(act):
                        nc.scalar.activation(e[:, :, :], raw[:, :, :], ACT.Abs).then_inc(s["sized"], 1)
                        act.wait_ge(s["sized"], 1)
                        nc.scalar.activation(e[:, :, :], e[:, :, :], ACT.Exp, scale=-1.0).then_inc(s["exped"], 1)
                        for m in range(CH):
                            act.wait_ge(s["conved"], m + 1)
                            nc.scalar.activation(conved[:, m, :], conved[:, m, :], ACT.Silu, bias=small[d, "conv_b"][:, m:m + 1])
                        act.wait_ge(s["plussed"], 1)
                        act.wait_ge(s["step"], CH * (TAPS - 1) + 1)
                        nc.scalar.activation(u[:, :, :], u[:, :, :], ACT.Ln).then_inc(s["logged"], 1)

                with phase(k, "sum", "summed copied turned paired") as (block, s):
                    @block.tensor
                    def _(pe):
                        nc.tensor.matmul(k.ps[:, 0, 0:GROUP * HEADS], small[d, "mask"][:, :],
                                         decay[:, :, :].rearrange("p j h -> p (j h)"), start=True, stop=True).then_inc(s["summed"], 1)
                        for j in range(GROUP):
                            last = nc.tensor.matmul(k.ps[:, 2, sl(j)], conved[:, M, sl(j)], conved[:, M + 1, sl(j)], start=True, stop=True)
                        last.then_inc(s["paired"], 1)
                        pe.wait_ge(s["copied"], 1)
                        for j in range(GROUP):
                            last = nc.tensor.transpose(k.ps[0:HEADS, 1, sl(j)], total[:, j, :], k.ident[:, :])
                        last.then_inc(s["turned"], 1)

                    @block.vector
                    def _(dve):
                        dve.wait_ge(s["summed"], 1)
                        nc.vector.tensor_copy(total[:, :, :].rearrange("p j h -> p (j h)"), k.ps[:, 0, 0:GROUP * HEADS]).then_inc(s["copied"], 1)
                        dve.wait_ge(s["paired"], 1)
                        nc.vector.tensor_tensor(pairs[:, :, :], k.ps[:, 2, :].rearrange("p (j t) -> p j t", j=GROUP),
                                                small[d, "mask"][:, :].unsqueeze(1).broadcast_to([P, GROUP, P]), ALU.mult)

                    @block.scalar
                    def _(act):
                        act.wait_ge(s["turned"], 1)
                        nc.scalar.activation(totalT[:, :], k.ps[0:HEADS, 1, :], ACT.Copy)

                def to_inputs(j):
                    def evacuate(nc, engine, bank):
                        heads = bank.rearrange("p (h d) -> p h d", d=WIDTH)
                        nc.vector.tensor_tensor(inputs[:, j, :].rearrange("p (h d) -> p h d", d=WIDTH), heads,
                                                dt[:, j, :].unsqueeze(2).broadcast_to([P, HEADS, WIDTH]), ALU.mult)
                        return nc.vector.tensor_tensor(skipped[:, j, :].rearrange("p (h d) -> p h d", d=WIDTH), heads,
                                                       small[d, "D"][:, :].unsqueeze(2).broadcast_to([P, HEADS, WIDTH]), ALU.mult)
                    return evacuate
                gemm_phase(k, "turn", [(P, INNER, turned([conved[:, m, sl(j)] for m in range(M)], k.ident[:, :]), "dve", to_inputs(j))
                                       for j in range(GROUP)])

                with phase(k, "scan", "spread read capped exped weighted mixed") as (block, s):
                    @block.tensor
                    def _(pe):
                        def mix(h):
                            pe.wait_ge(s["weighted"], h + 1)
                            for j in range(GROUP):
                                last = nc.tensor.matmul(k.ps[:, 4 + j, sl(h, WIDTH)], lasting[:, h % LB, j, :],
                                                        inputs[:, j, sl(h, WIDTH)], start=True, stop=True)
                            last.then_inc(s["mixed"], 1)

                        for h in range(HEADS):
                            if h >= 4:
                                pe.wait_ge(s["read"], h - 3)
                            nc.tensor.matmul(k.ps[:, h % 4, :], select[:, h, :], totalT[:, :], start=True, stop=True).then_inc(s["spread"], 1)
                            if h >= 3:
                                mix(h - 3)
                        for h in range(HEADS - 3, HEADS):
                            mix(h)

                    @block.vector
                    def _(dve):
                        def weight(h):
                            dve.wait_ge(s["exped"], h + 1)
                            nc.vector.tensor_tensor(lasting[:, h % LB, :, :], lasting[:, h % LB, :, :], pairs[:, :, :],
                                                    ALU.mult).then_inc(s["weighted"], 1)

                        for h in range(HEADS):
                            dve.wait_ge(s["spread"], h + 1)
                            if h >= LB:
                                dve.wait_ge(s["mixed"], h - LB + 1)
                            nc.vector.tensor_tensor(lasting[:, h % LB, :, :], k.ps[:, h % 4, :].rearrange("p (j t) -> p j t", j=GROUP),
                                                    total[:, :, h].unsqueeze(2).broadcast_to([P, GROUP, P]), ALU.subtract).then_inc(s["read"], 1)
                            if h >= 2:
                                weight(h - 2)
                        weight(HEADS - 2)
                        weight(HEADS - 1)

                    @block.gpsimd
                    def _(pool):
                        for h in range(HEADS):
                            pool.wait_ge(s["read"], h + 1)
                            nc.gpsimd.tensor_scalar(lasting[:, h % LB, :, :], lasting[:, h % LB, :, :], 0.0, None, ALU.min).then_inc(s["capped"], 1)

                    @block.scalar
                    def _(act):
                        for h in range(HEADS):
                            act.wait_ge(s["capped"], h + 1)
                            nc.scalar.activation(lasting[:, h % LB, :, :], lasting[:, h % LB, :, :], ACT.Exp).then_inc(s["exped"], 1)

                with phase(k, "gate", "step squared rooted") as (block, s):
                    @block.vector
                    def _(dve):
                        link = Link(dve, s["step"])
                        v = nc.vector
                        for j in range(GROUP):
                            last = v.tensor_tensor(y[:, j, :], k.ps[:, 4 + j, :], skipped[:, j, :], ALU.add)
                        link(last)
                        link(v.tensor_tensor(y[:, :, :], y[:, :, :], gate[:, :, :], ALU.mult))
                        for j in range(GROUP):
                            last = v.tensor_tensor_reduce(skipped[:, j, :], y[:, j, :], y[:, j, :], 1.0, 0.0, ALU.mult, ALU.add,
                                                          k.rstd[:, j:j + 1])
                        link(last)
                        link(v.tensor_scalar(k.rstd[:, :], k.rstd[:, :], 1.0 / INNER, LN_EPS, ALU.mult, ALU.add))
                        v.reciprocal(k.rstd[:, :], k.rstd[:, :]).then_inc(s["squared"], 1)
                        dve.wait_ge(s["rooted"], 1)
                        for j in range(GROUP):
                            v.tensor_scalar(y[:, j, :], y[:, j, :], k.rstd[:, j:j + 1], None, ALU.mult)

                    @block.scalar
                    def _(act):
                        row_rstd(k, act, s["squared"], s["rooted"])
                gemm_phase(k, "turn", [(P, GT, turned([y[:, j, sl(m)] for j in range(GROUP)], k.ident[:, :]), turns(m),
                                        to_copy(yT[d][:, m, :])) for m in range(M)])

            jobs = []
            for j in range(GROUP):
                x = k.x[:, bass.ds(g * GROUP + j, 1), :]
                both = [(yT[d][:, m, sl(j)], folded[d][:, m, :]) for d in ways for m in range(M)]
                both.append((k.ones[0:1, 0:P], out_b[0:1, :]))
                jobs.append((P, DIM, products(both), "dve",
                             lambda nc, engine, bank, x=x: nc.vector.tensor_tensor(x, bank.rearrange("p (o d) -> p o d", o=1), x, ALU.add)))
            gemm_phase(k, "out", jobs)


def l3_attn(k):
    nc = k.nc
    H, D = 16, 16
    QT = TOKENS // P
    Q_PARTS, K_PARTS = (0, 0, 1, 0, 2, 1), (0, 1, 0, 2, 0, 1)
    ROWS = len(Q_PARTS) * D
    DEEP = ROWS + 3
    VW = D + 1
    CHUNK = 512
    n = "L3_attn_"
    parts_dram = nc.dram_tensor("parts", (6 * DIM, TOKENS), BF16, kind="Internal").ap()
    with ExitStack() as stack:
        wp, a = weights(k, stack, n + "proj_w", KD, DIM)
        wq, b = weights(k, stack, n + "wq", KD, P)
        wk, c = weights(k, stack, n + "wk", KD, P)
        bp, d = bias_columns(k, stack, n + "proj_b", KD)
        bp_row, e = bias_row(k, stack, n + "proj_b_row", DIM)
        values = sb(k, stack, "values", [P, QT, H, VW])
        load_phase(k, a + b + c + d + e)
        with ExitStack() as inner:
            flat = sb(k, inner, "flat", [P, KD, GT])
            whole, left = sb(k, inner, "whole", [P, 2 * KD, GT]), sb(k, inner, "left", [P, 2 * KD, GT])
            parts = sb(k, inner, "parts", [P, 3, 2 * KD, GT], BF16)
            with phase(k, "fill", "none") as (block, s):
                @block.vector
                def _(dve):
                    nc.vector.memset(values[:, :, :, :], 1.0)
            with nc.Fori(0, GROUPS) as g:
                norm_phase(k, g, lambda kt: k.xT[:, kt, :])

                def to_values(j):
                    def evacuate(nc, engine, bank):
                        return nc.vector.tensor_copy(values[:, bass.ds(g * GROUP + j, 1), :, 0:D],
                                                     bank.rearrange("p (o h d) -> p o h d", o=1, d=D))
                    return evacuate
                jobs = feature_jobs(flat, wp, k.xT, [P] * KD, DIM, bp)
                jobs += [(P, DIM, token_pairs(k, k.xT, [P] * KD, j, wp, slice(0, DIM), bp_row), "dve", to_values(j))
                         for j in range(GROUP)]
                gemm_phase(k, "flat", jobs)
                gemm_phase(k, "qk", [(P, GT, products([(w[:, m, :], flat[:, m, :])]), turns(m), to_copy(whole[:, KD * i + m, :]))
                                     for i, w in enumerate((wq, wk)) for m in range(KD)])
                with phase(k, "split", "step stored") as (block, s):
                    @block.vector
                    def _(dve):
                        link = Link(dve, s["step"])
                        v = nc.vector
                        link(v.tensor_copy(parts[:, 0], whole[:, :, :]))
                        link(v.tensor_tensor(left[:, :, :], whole[:, :, :], parts[:, 0], ALU.subtract))
                        link(v.tensor_copy(parts[:, 1], left[:, :, :]))
                        link(v.tensor_tensor(parts[:, 2], left[:, :, :], parts[:, 1], ALU.subtract))

                    @block.sync
                    def _(sp):
                        for part, ready in enumerate((1, 3, 4)):
                            sp.wait_ge(s["step"], ready)
                            for i in range(2 * KD):
                                row0 = ((i // KD) * 3 + part) * DIM + (i % KD) * P
                                sp.dma_start(parts_dram[row0:row0 + P, bass.ds(g * GT, GT)], parts[:, part, i, :]).then_inc(s["stored"], 16)
                        sp.wait_ge(s["stored"], 16 * 3 * 2 * KD)

        queries = [sb(k, stack, f"queries{i}", [P, TOKENS], BF16) for i in range(3)]
        keys = [sb(k, stack, f"keys{i}", [P, TOKENS], BF16) for i in range(3)]
        attn = sb(k, stack, "attn", [P, 2, TOKENS])
        head_values = sb(k, stack, "head_values", [P, QT, PAD])
        peaks = sb(k, stack, "peaks", [P, QT, TOKENS // CHUNK])
        minus, left = sb(k, stack, "minus", [P, QT]), sb(k, stack, "left", [P, QT])
        minus_b = sb(k, stack, "minus_b", [P, QT], BF16)
        minus_parts = sb(k, stack, "minus_parts", [P, 3, QT])
        minus_rows = sb(k, stack, "minus_rows", [3 * QT, P], BF16)
        output = sb(k, stack, "output", [P, CHUNK])
        share, fresh = sb(k, stack, "share", [P, QT]), sb(k, stack, "fresh", [P, 4, 4, D])

        def load_head(sp, loaded, i, head):
            for side, (dst, order) in enumerate(((queries[i], Q_PARTS), (keys[i], K_PARTS))):
                for block_, part in enumerate(order):
                    sp.dma_start(dst[sl(block_, D), :], parts_dram[bass.ds(head * D + (side * 3 + part) * DIM, D), :]).then_inc(loaded, 16)

        with phase(k, "start", "loaded") as (block, s):
            @block.vector
            def _(dve):
                nc.vector.memset(head_values[:, :, :], 0.0)
                for i in range(3):
                    nc.vector.memset(keys[i][ROWS:P, :], 1.0)

            @block.sync
            def _(sp):
                for i in range(2):
                    load_head(sp, s["loaded"], i, i)
                sp.wait_ge(s["loaded"], 16 * 24)

        PROBES = QT * TOKENS // CHUNK
        PER_STEP = 5

        def head_phase(here, ahead, later, head, before=None):
            with phase(k, "head", "step loaded scored exped mixed probed maxed parted turned rowed moved fetched unturned emptied") as (block, s):
                @block.sync
                def _(sp):
                    if later is not None:
                        load_head(sp, s["loaded"], *later)
                        sp.wait_ge(s["loaded"], 16 * 12)
                    if ahead is not None:
                        sp.wait_ge(s["rowed"], 1)
                        for part in range(3):
                            sp.dma_start(queries[ahead][ROWS + part:ROWS + part + 1, :].rearrange("o (t q) -> o t q", q=P),
                                         minus_rows[sl(part, QT), :]).then_inc(s["moved"], 16)
                        sp.wait_ge(s["moved"], 48)

                @block.gpsimd
                def _(pool):
                    if here is not None:
                        nc.gpsimd.tensor_copy(head_values[:, :, 0:VW].unsqueeze(2), values[:, :, bass.ds(head, 1), :]).then_inc(s["fetched"], 1)

                @block.tensor
                def _(pe):
                    def score(kt, half):
                        if here is None:
                            return
                        if kt >= 1:
                            pe.wait_ge(s["exped"], 2 * (kt - 1) + half + 1)
                        for c in range(2 * half, 2 * half + 2):
                            last = nc.tensor.matmul(k.ps[:, c, :], keys[here][0:DEEP, sl(kt)], queries[here][0:DEEP, sl(c, CHUNK)],
                                                    start=True, stop=True)
                        last.then_inc(s["scored"], 1)

                    def probe(u):
                        if ahead is None or u >= PROBES:
                            return
                        if u == 2 and before is not None:
                            pe.wait_ge(s["emptied"], 1)
                        if u >= 3:
                            pe.wait_ge(s["maxed"], u - 2)
                        nc.tensor.matmul(k.ps[:, 5 + u % 3, :], queries[ahead][0:ROWS, sl(u // 4)], keys[ahead][0:ROWS, sl(u % 4, CHUNK)],
                                         start=True, stop=True).then_inc(s["probed"], 1)

                    def mix(kt):
                        if here is None or kt < 0:
                            return
                        pe.wait_ge(s["exped"], 2 * kt + 2)
                        if kt == 0:
                            pe.wait_ge(s["fetched"], 1)
                        for c in range(4):
                            last = nc.tensor.matmul(k.ps[sl(c, PAD), 4, :], head_values[:, kt, :], attn[:, kt % 2, sl(c, CHUNK)],
                                                    start=kt == 0, stop=kt == QT - 1)
                        last.then_inc(s["mixed"], 1)

                    if before is not None:
                        for b_ in range(4):
                            last = nc.tensor.transpose(k.ps[:, 7, sl(b_)], output[:, sl(b_)], k.ident[:, :])
                        last.then_inc(s["unturned"], 1)
                    for kt in range(QT):
                        u = PER_STEP * kt
                        score(kt, 0)
                        probe(u)
                        probe(u + 1)
                        score(kt, 1)
                        probe(u + 2)
                        probe(u + 3)
                        mix(kt - 1)
                        probe(u + 4)
                    if ahead is not None:
                        pe.wait_ge(s["parted"], 1)
                        nc.tensor.transpose(k.ps[0:3 * QT, 7, 0:P], minus_parts[:, :, :].rearrange("p a b -> p (a b)"),
                                            k.ident[:, :]).then_inc(s["turned"], 1)
                    mix(QT - 1)

                @block.scalar
                def _(act):
                    if here is not None:
                        for kt in range(QT):
                            for half in range(2):
                                act.wait_ge(s["scored"], 2 * kt + half + 1)
                                if kt >= 2:
                                    act.wait_ge(s["mixed"], kt - 1)
                                nc.scalar.activation(attn[:, kt % 2, sl(half, 2 * CHUNK)].rearrange("p (c q) -> p c q", c=2),
                                                     k.ps[:, 2 * half:2 * half + 2, :], ACT.Exp, scale=1.0 / 16.0).then_inc(s["exped"], 1)
                    if ahead is not None:
                        act.wait_ge(s["turned"], 1)
                        nc.scalar.activation(minus_rows[:, :], k.ps[0:3 * QT, 7, 0:P], ACT.Copy).then_inc(s["rowed"], 1)
                    if here is not None:
                        if before is not None:
                            act.wait_ge(s["unturned"], 1)
                        act.wait_ge(s["mixed"], QT)
                        nc.scalar.activation(output[:, :], k.ps[:, 4, :], ACT.Copy)

                @block.vector
                def _(dve):
                    link = Link(dve, s["step"])
                    v = nc.vector
                    if before is not None:
                        dve.wait_ge(s["unturned"], 1)
                        turned_ = k.ps[:, 7, :].rearrange("p (b c w) -> p b c w", b=4, c=4)
                        share_ = share[:, :].rearrange("p (b c) -> p b c", b=4)
                        link(v.reciprocal(share_.unsqueeze(3), turned_[:, :, :, D:VW]))
                        v.tensor_tensor(fresh[:, :, :, :], turned_[:, :, :, 0:D], share_.unsqueeze(3).broadcast_to([P, 4, 4, D]),
                                        ALU.mult).then_inc(s["emptied"], 1)
                        dve.wait_ge(s["emptied"], 1)
                        for b_ in range(4):
                            x = k.x[:, :, bass.ds(before * D, D)].rearrange("p (c b) d -> p c b d", b=4)[:, :, b_, :]
                            v.tensor_tensor(x, x, fresh[:, b_, :, :], ALU.add)
                    if ahead is not None:
                        for u in range(PROBES):
                            dve.wait_ge(s["probed"], u + 1)
                            v.tensor_reduce(peaks[:, u // 4, u % 4:u % 4 + 1], k.ps[:, 5 + u % 3, :], AX.X, ALU.max).then_inc(s["maxed"], 1)
                        dve.wait_ge(s["maxed"], PROBES)
                        link(v.tensor_reduce(minus[:, :], peaks[:, :, :], AX.X, ALU.max))
                        link(v.tensor_scalar(minus[:, :], minus[:, :], -1.0, None, ALU.mult))
                        link(v.tensor_copy(minus_b[:, :], minus[:, :]))
                        link(v.tensor_copy(minus_parts[:, 0, :], minus_b[:, :]))
                        link(v.tensor_tensor(left[:, :], minus[:, :], minus_parts[:, 0, :], ALU.subtract))
                        link(v.tensor_copy(minus_b[:, :], left[:, :]))
                        link(v.tensor_copy(minus_parts[:, 1, :], minus_b[:, :]))
                        v.tensor_tensor(minus_parts[:, 2, :], left[:, :], minus_parts[:, 1, :], ALU.subtract).then_inc(s["parted"], 1)

        def one_head(m, h):
            head_phase(m, (m + 1) % 3, ((m + 2) % 3, h + 2), h, h - 1)

        head_phase(None, 0, None, None)
        head_phase(0, 1, (2, 2), 0)
        with nc.Fori(0, 4) as i:
            for m in range(3):
                one_head((m + 1) % 3, 3 * i + m + 1)
            empty_phase(k)
        one_head(1, 13)
        head_phase(2, 0, None, 14, 13)
        head_phase(0, None, None, 15, 14)
        head_phase(None, None, None, None, 15)


def lay_out_rest(i, w):
    n = "L0_xattn_"
    w[n + "Wq"], w[n + "Wk"], w[n + "Wv"] = i[n + "Wq"], i[n + "Wk"], pad_heads(i[n + "Wv"], 1)
    w[n + "Wo"] = wo_order(pad_heads(i[n + "Wo"], 0), 16, PAD)
    w[n + "bv"] = row(pad_heads(i[n + "bv"], 0))
    for m in ("bq", "bk", "bo"):
        w[n + m] = row(i[n + m])
    for m in ("ln_gamma", "ln_beta"):
        w[n + m] = np.repeat(row(i[n + m]), P, axis=0)

    n = "L0_ffn_"
    w[n + "Wr"], w[n + "br"] = i[n + "Wr"], row(i[n + "br"])
    w[n + "bd"] = np.concatenate([i[n + "bd"], row(i[n + "bd_s"])])

    def expert_parts(name):
        return np.concatenate([i[n + name], i[n + name + "_s"][None]])

    def by_partition(a, tiles):
        return a.reshape(len(a), tiles, P, -1).transpose(0, 2, 1, 3).reshape(len(a), P, -1)
    packed = np.concatenate([by_partition(expert_parts("Wg"), 2), by_partition(expert_parts("Wu"), 2), expert_parts("Wd"),
                             expert_parts("bg")[:, :, None], expert_parts("bu")[:, :, None]], axis=2)
    w[n + "experts"] = packed.reshape(11, 3, P, -1).transpose(0, 2, 1, 3)

    n = "L2_ffn_"
    w[n + "Wg"] = i[n + "Wg"]
    w[n + "experts"] = np.concatenate([by_partition(i[n + "W1"], 2), by_partition(i[n + "W2"], 4)], axis=2)
    w["order"] = np.broadcast_to(np.arange(8, 0, -1, dtype=np.float32), (P, BATCH, 8))

    n = "L3_ffn_"
    for m in ("W_fc", "W_proj", "B_fc", "B_proj"):
        w[n + m] = i[n + m].T
    w[n + "A_fc"], w[n + "A_proj"] = i[n + "A_fc"], i[n + "A_proj"]
    w[n + "b_fc"], w[n + "b_proj"] = columns(i[n + "b_fc"]), row(i[n + "b_proj"])

    n = "L1_attn_"
    w[n + "W_q"], w[n + "W_k"] = pad_heads(i[n + "W_q"], 1), pad_heads(i[n + "W_k"], 1)
    w[n + "W_v"], w[n + "W_o"] = i[n + "W_v"], i[n + "W_o"]
    blocks, where = np.zeros((P, 8, P), np.float32), np.zeros((P, 8, P), np.float32)
    for h in range(16):
        at = PAD * (h % 4)
        blocks[at:at + 16, h // 2, sl(h % 2, 64)] = i[n + "centers"][h].T
        where[at:at + 16, h // 2, sl(h % 2, 64)] = 1
    w[n + "centers"], w[n + "where"] = blocks, where
    for m in ("log_scales", "amplitudes"):
        w[n + m] = columns(i[n + m].reshape(-1))

    n = "L1_ffn_"
    for m in ("w_gate", "w_up", "w_down"):
        w[n + m] = i[n + m].T

    n = "L2_attn_"
    w[n + "norm_w"], w[n + "out_b"] = columns(i[n + "norm_w"]), row(i[n + "out_b_blk"])
    w[n + "select"] = np.repeat(np.eye(8, dtype=np.float32)[:, :, None], P, axis=2)
    for number, d in enumerate("fb"):
        m = n + d + "_"
        w[m + "in_w"], w[m + "out_w"] = i[m + "in_w"].T, i[m + "out_w"]
        w[m + "block_w"] = i[n + "out_w_blk"][:, sl(number, DIM)].T
        w[m + "gnorm_w"], w[m + "conv_b"] = columns(i[m + "gnorm_w"]), columns(i[m + "conv_b"])
        w[m + "conv_w"] = i[m + "conv_w"].reshape(6, P, 4).transpose(1, 0, 2)
        w[m + "A"], w[m + "D"] = np.repeat(row(i[m + "A_log"]), P, axis=0), np.repeat(row(i[m + "D"]), P, axis=0)
        w[m + "dt_bias"] = row(i[m + "dt_bias"])
        w[m + "mask"] = np.tri(P, dtype=np.float32).T if d == "f" else np.tri(P, dtype=np.float32)

    n = "L3_attn_"
    w[n + "proj_w"] = i[n + "proj_w"].T
    w[n + "proj_b"], w[n + "proj_b_row"] = columns(i[n + "proj_b"]), row(i[n + "proj_b"])
    for m in ("wq", "wk"):
        blocks = np.zeros((2, P, P), np.float32)
        for h in range(16):
            blocks[h // 8, sl(h % 8, 16), sl(h % 8, 16)] = i[n + m][h]
        w[n + m] = blocks.reshape(2 * P, P)


def layers(k):
    l0_attn(k)
    l0_xattn(k)
    l0_ffn(k)
    l1_attn(k)
    cross_attention(k, "L1_xattn", 16, "L1_xattn_Wo", "L1_xattn_bo")
    l1_ffn(k)
    l2_attn(k)
    cross_attention(k, "L2_xattn", 8, "L2_xattn_Wout", "L2_xattn_bout")
    l2_ffn(k)
    l3_attn(k)
    cross_attention(k, "L3_xattn", 8, "L3_xattn_Wo", "L3_xattn_bo")
    l3_ffn(k)


def build(nc, w, out):
    with ExitStack() as stack:
        k = Core(nc, w)
        free = sorted(nc.free_semaphores)[-2 * SIGNALS:]
        k.banks = (free[:SIGNALS], free[SIGNALS:])
        k.ps = stack.enter_context(nc.psum_tensor("ps", [P, 8, 512], F32))
        k.x = sb(k, stack, "x", [P, BATCH, DIM])
        k.ctxT = sb(k, stack, "ctxT", [P, 2, TOKENS])
        k.ctxG = sb(k, stack, "ctxG", [P, 2, GT])
        k.xT = sb(k, stack, "xT", [P, KD, GT])
        k.normed = sb(k, stack, "normed", [P, GROUP, DIM])
        k.ident = sb(k, stack, "ident", [P, P])
        k.ones = sb(k, stack, "ones", [P, P])
        k.stats = sb(k, stack, "stats", [P, GROUP, 6])
        k.moments = sb(k, stack, "moments", [P, GROUP, 2])
        k.rstd = sb(k, stack, "rstd", [P, GROUP])
        load_phase(k, [(k.x[:, :, :], w["x"].rearrange("b t d -> t b d")), (k.ident[:, :], w["ident"]),
                       (k.ones[:, :], w["ones"]),
                       (k.ctxT[:, 0, :], w["ctxT"][0:P, :]), (k.ctxT[0:CTX - P, 1, :], w["ctxT"][P:CTX, :])])
        layers(k)
        with phase(k, "store", "stored") as (block, s):
            @block.sync
            def _(sp):
                sp.dma_start(out.rearrange("b t d -> t b d"), k.x[:, :, :]).then_inc(s["stored"], 16)
                sp.wait_ge(s["stored"], 16)


def pad_heads(a, axis):
    a = np.moveaxis(a, axis, -1)
    b = np.zeros(a.shape[:-1] + (16, PAD), a.dtype)
    b[..., :16] = a.reshape(a.shape[:-1] + (16, 16))
    return np.ascontiguousarray(np.moveaxis(b.reshape(a.shape[:-1] + (16 * PAD,)), -1, axis))


def columns(b):
    return np.ascontiguousarray(b.reshape(-1, P).T)


def row(b):
    return b.reshape(1, -1)


def wo_order(a, heads, width):
    per = P // width
    order = [(u // per * 4 + i) * per + u % per for u in range(heads // 4) for i in range(4)]
    return a.reshape(heads, width, -1)[order].reshape(heads * width, -1)


def lay_out(i):
    i = {n: np.asarray(a) for n, a in i.items()}
    w = {"x": i["x"], "ctxT": i["ctx_768"].reshape(TOKENS, CTX).T,
         "ident": np.eye(P, dtype=np.float32), "ones": np.ones((P, P), np.float32)}
    future = (np.arange(P)[None, :] > np.arange(P)[:, None]).astype(np.int32)
    w["future"] = np.repeat(future[:, None, :], 4, axis=1)
    n = "L0_attn_"
    for m in "qkv":
        w[n + "W" + m] = pad_heads(i[n + "W" + m], 1)
    w[n + "bq"], w[n + "bk"] = columns(pad_heads(i[n + "bq"], 0)), columns(pad_heads(i[n + "bk"], 0))
    w[n + "bv"], w[n + "bo"] = row(pad_heads(i[n + "bv"], 0)), row(i[n + "bo"])
    w[n + "Wo"] = wo_order(pad_heads(i[n + "Wo"], 0), 16, PAD)
    for n in ("L1_xattn_", "L2_xattn_", "L3_xattn_"):
        for m in ("Wq", "Wk", "Wv", "Wo", "Wout", "bo", "bout"):
            if n + m in i:
                w[n + m] = i[n + m] if m[0] == "W" else row(i[n + m])
            if n + m in i and m in ("Wo", "Wout"):
                w[n + m] = wo_order(i[n + m], len(i[n + m]) // 64, 64)
    lay_out_rest(i, w)
    return {n: np.ascontiguousarray(a) for n, a in w.items()}


def kernel(**inputs):
    import concourse.bacc as bacc
    from concourse.bass_utils import run_bass_kernel_spmd

    arrays = {f"in_{n}": a for n, a in lay_out(inputs).items()}
    nc = bacc.Bacc("TRN2", target_bir_lowering=False, num_devices=1)
    w = {n[3:]: nc.dram_tensor(n, a.shape, mybir.dt.from_np(a.dtype), kind="ExternalInput").ap() for n, a in arrays.items()}
    out = nc.dram_tensor("out_0_dram", (BATCH, SEQ, DIM), F32, kind="ExternalOutput").ap()
    build(nc, w, out)
    return run_bass_kernel_spmd(nc, [arrays], core_ids=[0]).results[0]["out_0_dram"]
```

```python
from contextlib import ExitStack, contextmanager
from itertools import count

import numpy as np

import concourse.bass as bass
from concourse import mybir

F32 = mybir.dt.float32
BF16 = mybir.dt.bfloat16
I32 = mybir.dt.int32
ALU = mybir.AluOpType
ACT = mybir.ActivationFunctionType
AX = mybir.AxisListType

P = 128
BATCH, SEQ, DIM = 16, 128, 256
KD = DIM // P
CTX = 192
GROUP = 4
GROUPS = BATCH // GROUP
GT = GROUP * SEQ
TOKENS = BATCH * SEQ
PAD = 32
LN_EPS = 1e-5
MAGIC = 12582912.0
CTX_ROWS = (P, CTX - P)
SIGNALS = 16


def sl(i, n=P):
    return slice(i * n, (i + 1) * n)


class Core:

    def __init__(self, nc, w):
        self.nc, self.w = nc, w
        self.turn = self.count = self.names = 0



@contextmanager
def phase(k, title, signals):
    nc = k.nc
    mine, other = k.banks[k.turn], k.banks[1 - k.turn]
    k.turn = 1 - k.turn
    k.count += 1
    with ExitStack() as stack:
        sems = {}
        for number, name in zip(mine, signals.split()):
            sems[name] = stack.enter_context(nc.semaphore(f"{title}{k.count}_{name}", num=number))
        with nc.Block() as block:
            @block.sync
            def _(sp):
                sp.sem_clear(range(other[0], other[-1] + 1))
            yield block, sems


class Part:

    def __init__(self, title, signals):
        self.title, self.signals, self.programs = title, signals, {}

    def tensor(self, program):
        self.programs["tensor"] = program

    def vector(self, program):
        self.programs["vector"] = program

    def scalar(self, program):
        self.programs["scalar"] = program

    def gpsimd(self, program):
        self.programs["gpsimd"] = program

    def sync(self, program):
        self.programs["sync"] = program


def side_by_side(k, *parts):
    names = " ".join(f"{n}_{name}" for n, (part, _) in enumerate(parts) for name in part.signals.split())
    with phase(k, "_".join(part.title for part, _ in parts), names) as (block, s):
        signals = [{name: s[f"{n}_{name}"] for name in part.signals.split()} for n, (part, _) in enumerate(parts)]

        def merged(engine, name):
            running = [(part.programs[name](engine, own), pace) for (part, pace), own in zip(parts, signals)
                       if name in part.programs]
            for r in count():
                if not running:
                    break
                for steps, pace in list(running):
                    for _ in range(int((r + 1) * pace) - int(r * pace)):
                        if next(steps, "end") == "end":
                            running.remove((steps, pace))
                            break

        @block.tensor
        def _(pe):
            merged(pe, "tensor")

        @block.vector
        def _(dve):
            merged(dve, "vector")

        @block.scalar
        def _(act):
            merged(act, "scalar")

        @block.gpsimd
        def _(pool):
            merged(pool, "gpsimd")

        @block.sync
        def _(sp):
            merged(sp, "sync")


class Link:

    def __init__(self, engine, sem):
        self.engine, self.sem, self.count = engine, sem, 0

    def __call__(self, instruction):
        instruction.then_inc(self.sem, 1)
        self.count += 1
        self.engine.wait_ge(self.sem, self.count)


def load_part(pairs):
    part = Part("load", "loaded")

    @part.sync
    def _(sp, s):
        for dst, src in pairs:
            sp.dma_start(dst, src).then_inc(s["loaded"], 16)
        sp.wait_ge(s["loaded"], 16 * len(pairs))
        yield
    return part


def load_phase(k, pairs):
    side_by_side(k, (load_part(pairs), 1))


def gemm_part(k, title, jobs, banks=range(8)):
    nc = k.nc
    B = len(banks)
    place, counts = [], {"act": 0, "dve": 0}
    for _, _, _, engine, _ in jobs:
        place.append((engine, counts[engine]))
        counts[engine] += 1
    part = Part(title, "product_ready act_took dve_took")

    def bank(n):
        rows, columns = jobs[n][:2]
        return k.ps[0:rows, banks[n % B], 0:columns]

    @part.tensor
    def _(pe, s):
        for n, job in enumerate(jobs):
            if n >= B:
                engine, at = place[n - B]
                pe.wait_ge(s[f"{engine}_took"], at + 1)
            job[2](nc, bank(n)).then_inc(s["product_ready"], 1)
            yield

    @part.scalar
    def _(act, s):
        for n, job in enumerate(jobs):
            yield
            if job[3] == "act":
                act.wait_ge(s["product_ready"], n + 1)
                job[4](nc, "act", bank(n)).then_inc(s["act_took"], 1)

    @part.vector
    def _(dve, s):
        for n, job in enumerate(jobs):
            yield
            if job[3] == "dve":
                dve.wait_ge(s["product_ready"], n + 1)
                job[4](nc, "dve", bank(n)).then_inc(s["dve_took"], 1)
    return part


def gemm_phase(k, title, jobs):
    side_by_side(k, (gemm_part(k, title, jobs), 1))


def products(pairs):
    def fill(nc, bank):
        for i, (stationary, moving) in enumerate(pairs):
            last = nc.tensor.matmul(bank, stationary, moving, start=i == 0, stop=i == len(pairs) - 1)
        return last
    return fill


def turned(blocks, ident):
    def fill(nc, bank):
        if blocks[0].dtype == BF16:
            bank = bank.bitcast(BF16)
        for i, block in enumerate(blocks):
            last = nc.tensor.transpose(bank[:, sl(i)], block, ident)
        return last
    return fill


def to_copy(dst):
    def evacuate(nc, engine, bank):
        if engine == "act":
            return nc.scalar.activation(dst, bank, ACT.Copy)
        return nc.vector.tensor_copy(dst, bank)
    return evacuate


def to_bias(dst, bias):
    def evacuate(nc, engine, bank):
        if engine == "act":
            return nc.scalar.activation(dst, bank, ACT.Identity, bias=bias)
        return nc.vector.tensor_scalar(dst, bank, bias, None, ALU.add)
    return evacuate


def to_sum(dst, other):
    def evacuate(nc, engine, bank):
        return nc.vector.tensor_tensor(dst, bank, other, ALU.add)
    return evacuate


def turns(n):
    return "act" if n % 2 == 0 else "dve"


def feature_jobs(dst, weights, source, rows, width, bias=None, n0=0):
    jobs = []
    for m in range(width // P):
        pairs = [(weights[0:r, i, sl(m)], source[0:r, i, :]) for i, r in enumerate(rows)]
        out = dst[:, m, :]
        jobs.append((P, GT, products(pairs), turns(n0 + m), to_copy(out) if bias is None else to_bias(out, bias[:, m:m + 1])))
    return jobs


def token_pairs(k, source, rows, j, weights, columns, bias=None):
    pairs = [(source[0:r, i, sl(j)], weights[0:r, i, columns]) for i, r in enumerate(rows)]
    if bias is not None:
        pairs.append((k.ones[0:1, 0:P], bias[0:1, columns]))
    return products(pairs)


def residual_jobs(k, g, source, tiles, weights, bias=None):
    jobs = []
    for j in range(GROUP):
        x = k.x[:, bass.ds(g * GROUP + j, 1), :]
        jobs.append((P, DIM, token_pairs(k, source, [P] * tiles, j, weights, slice(0, DIM), bias), "dve",
                     lambda nc, engine, bank, x=x: nc.vector.tensor_tensor(x, bank.rearrange("p (o d) -> p o d", o=1), x, ALU.add)))
    return jobs


def row_stats(k, dve, link, source, measured):
    nc = k.nc
    for j in range(GROUP):
        last = nc.vector.bn_stats(k.stats[:, j, :], source(j))
    link(last)
    for j in range(GROUP):
        last = nc.vector.bn_aggr(k.moments[:, j, :], k.stats[:, j, :])
    link(last)
    link(nc.vector.tensor_scalar(k.rstd[:, :], k.moments[:, :, 1], LN_EPS, None, ALU.add))
    nc.vector.reciprocal(k.rstd[:, :], k.rstd[:, :]).then_inc(measured, 1)


def row_rstd(k, act, measured, rooted):
    act.wait_ge(measured, 1)
    k.nc.scalar.activation(k.rstd[:, :], k.rstd[:, :], ACT.Sqrt).then_inc(rooted, 1)


def norm_part(k, g, dst, banks=(0, 1), all_tokens=None):
    nc = k.nc
    part = Part("norm", "step measured rooted normed turned")

    def source(j):
        return k.x[:, bass.ds(g * GROUP + j, 1), :].rearrange("p o d -> p (o d)")

    @part.vector
    def _(dve, s):
        row_stats(k, dve, Link(dve, s["step"]), source, s["measured"])
        yield
        dve.wait_ge(s["rooted"], 1)
        for j in range(GROUP):
            nc.vector.tensor_scalar(k.normed[:, j, :], source(j), k.moments[:, j, 0:1], k.rstd[:, j:j + 1],
                                    ALU.subtract, ALU.mult).then_inc(s["normed"], 1)
        yield
        dve.wait_ge(s["turned"], GROUP)
        nc.vector.tensor_copy(dst(1), k.ps[:, banks[1], :])
        if all_tokens is not None:
            nc.vector.tensor_copy(all_tokens[:, 1, bass.ds(g * GT, GT)], k.ps[:, banks[1], :])
        yield

    @part.tensor
    def _(pe, s):
        for j in range(GROUP):
            pe.wait_ge(s["normed"], j + 1)
            for kt in range(KD):
                last = nc.tensor.transpose(k.ps[:, banks[kt], sl(j)], k.normed[:, j, sl(kt)], k.ident[:, :])
            last.then_inc(s["turned"], 1)
            yield

    @part.scalar
    def _(act, s):
        row_rstd(k, act, s["measured"], s["rooted"])
        yield
        act.wait_ge(s["turned"], GROUP)
        nc.scalar.activation(dst(0), k.ps[:, banks[0], :], ACT.Copy)
        if all_tokens is not None:
            nc.scalar.activation(all_tokens[:, 0, bass.ds(g * GT, GT)], k.ps[:, banks[0], :], ACT.Copy)
        yield
    return part


def each_group(k, body):
    with k.nc.Fori(0, GROUPS - 1) as g:
        body(g, True)
    body(GROUPS - 1, False)


def norm_phase(k, g, dst, all_tokens=None):
    side_by_side(k, (norm_part(k, g, dst, all_tokens=all_tokens), 1))


def attention_part(k, heads, width, q_of, k_of, v_of, out_of, scale, causal=False):
    nc = k.nc
    units = [(j, u) for j in range(GROUP) for u in range(heads // 4)]
    SB, WB, TB, OB = 2, 4, 2, 2
    per = P // width
    blocks = 4 * width // P

    def head(u, i):
        return (u // per * 4 + i) * per + u % per

    def scores(n):
        return k.ps[:, n % SB, :].rearrange("p (h t) -> p h t", h=4)

    def weights(n):
        return k.attn_w[:, n % WB, :, :]

    def turned(n):
        return k.ps[:, SB + n % TB, :]

    def output(n):
        return k.ps[:, SB + TB + n % OB, 0:blocks * P]

    part = Part("attention", "scored step read summed exped scaled turned copied mixed taken")

    @part.tensor
    def _(pe, s):
        def score(n):
            if n >= SB:
                pe.wait_ge(s["read"], n - SB + 1)
            j, u = units[n]
            for i in range(4):
                last = nc.tensor.matmul(scores(n)[:, i, :], q_of(j, head(u, i)), k_of(j, head(u, i)), start=True, stop=True)
            last.then_inc(s["scored"], 1)

        def turn(n):
            pe.wait_ge(s["scaled"], n + 1)
            if n >= TB:
                pe.wait_ge(s["copied"], n - TB + 1)
            for i in range(4):
                last = nc.tensor.transpose(turned(n)[:, sl(i)], weights(n)[:, i, :], k.ident[:, :])
            last.then_inc(s["turned"], 1)

        def mix(n):
            pe.wait_ge(s["copied"], n + 1)
            if n >= OB:
                pe.wait_ge(s["taken"], n - OB + 1)
            j, u = units[n]
            for i in range(4):
                at = i * width
                last = nc.tensor.matmul(output(n)[at % P:at % P + width, sl(at // P)], v_of(j, head(u, i)),
                                        k.attn_wT[:, n % TB, sl(i)], start=True, stop=True)
            last.then_inc(s["mixed"], 1)

        for n in range(len(units) + 3):
            if n < len(units):
                score(n)
            if 0 <= n - 2 < len(units):
                turn(n - 2)
            if 0 <= n - 3:
                mix(n - 3)
            yield

    @part.vector
    def _(dve, s):
        link = Link(dve, s["step"])

        def subtract_max(n):
            dve.wait_ge(s["scored"], n + 1)
            if causal:
                link(nc.vector.copy_predicated(scores(n), k.future[:, :, :], k.minus[:, :, :]))
            link(nc.vector.tensor_reduce(k.peak[:, n % WB, :], scores(n), AX.X, ALU.max))
            if n >= WB:
                dve.wait_ge(s["turned"], n - WB + 1)
            nc.vector.tensor_tensor(weights(n), scores(n), k.peak[:, n % WB, :].unsqueeze(2).broadcast_to([P, 4, P]),
                                    ALU.subtract).then_inc(s["read"], 1)

        def total(n):
            dve.wait_ge(s["exped"], n + 1)
            link(nc.vector.tensor_reduce(k.total[:, n % WB, :], weights(n), AX.X, ALU.add))
            nc.vector.reciprocal(k.share[:, n % WB, :], k.total[:, n % WB, :]).then_inc(s["summed"], 1)

        def take(n):
            dve.wait_ge(s["mixed"], n + 1)
            j, u = units[n]
            nc.vector.tensor_copy(out_of(j, u), output(n).rearrange("p (b t) -> p b t", b=blocks)).then_inc(s["taken"], 1)

        for n in range(len(units) + 3):
            if n < len(units):
                subtract_max(n)
            if 0 <= n - 1 < len(units):
                total(n - 1)
            if 0 <= n - 3:
                take(n - 3)
            yield

    @part.scalar
    def _(act, s):
        for n in range(len(units) + 2):
            if n < len(units):
                act.wait_ge(s["read"], n + 1)
                nc.scalar.activation(weights(n), weights(n), ACT.Exp, scale=scale).then_inc(s["exped"], 1)
            if n >= 2:
                m = n - 2
                act.wait_ge(s["turned"], m + 1)
                if m >= TB:
                    act.wait_ge(s["mixed"], m - TB + 1)
                nc.scalar.activation(k.attn_wT[:, m % TB, :], turned(m), ACT.Copy).then_inc(s["copied"], 1)
            yield

    @part.gpsimd
    def _(pool, s):
        for n in range(len(units)):
            pool.wait_ge(s["summed"], n + 1)
            nc.gpsimd.tensor_tensor(weights(n), weights(n), k.share[:, n % WB, :].unsqueeze(2).broadcast_to([P, 4, P]),
                                    ALU.mult).then_inc(s["scaled"], 1)
            yield
    return part


def attention_memory(k, stack):
    k.attn_w = sb(k, stack, "attn_w", [P, 4, 4, P])
    k.attn_wT = sb(k, stack, "attn_wT", [P, 2, 4 * P])
    k.peak, k.total, k.share = (sb(k, stack, f"attn_{name}", [P, 4, 4]) for name in ("peak", "total", "share"))


def sb(k, stack, name, shape, dtype=F32):
    k.names += 1
    return stack.enter_context(k.nc.sbuf_tensor(f"{name}_{k.names}", shape, dtype))


def rows_of(dram, tiles):
    return dram.rearrange("(t p) n -> p t n", p=P)


def ctx_weights(k, stack, name, width):
    w = sb(k, stack, name, [P, 2, width])
    dram = k.w[name]
    return w, [(w[0:P, 0, :], dram[0:P, :]), (w[0:CTX - P, 1, :], dram[P:CTX, :])]


def weights(k, stack, name, tiles, width):
    w = sb(k, stack, name, [P, tiles, width])
    return w, [(w[:, :, :], rows_of(k.w[name], tiles))]


def bias_row(k, stack, name, width):
    w = sb(k, stack, name, [1, width])
    return w, [(w[0:1, :], k.w[name])]


def bias_columns(k, stack, name, tiles):
    w = sb(k, stack, name, [P, tiles])
    return w, [(w[:, :], k.w[name])]


def l0_attn(k):
    nc = k.nc
    H, W = 16, 16 * PAD
    T = W // P
    with ExitStack() as stack:
        attention_memory(k, stack)
        wq, a = weights(k, stack, "L0_attn_Wq", KD, W)
        wk, b = weights(k, stack, "L0_attn_Wk", KD, W)
        wv, c = weights(k, stack, "L0_attn_Wv", KD, W)
        wo, d = weights(k, stack, "L0_attn_Wo", T, DIM)
        bq, e = bias_columns(k, stack, "L0_attn_bq", T)
        bk, f = bias_columns(k, stack, "L0_attn_bk", T)
        bv, g_ = bias_row(k, stack, "L0_attn_bv", W)
        bo, h_ = bias_row(k, stack, "L0_attn_bo", DIM)
        qT, kT = ([sb(k, stack, n, [P, T, GT]) for _ in range(2)] for n in ("qT", "kT"))
        v = [sb(k, stack, "v", [P, GROUP, W]) for _ in range(2)]
        oT = sb(k, stack, "oT", [P, T, GT])
        k.future = sb(k, stack, "future", [P, 4, P], I32)
        k.minus = sb(k, stack, "minus", [P, 4, P])
        loads = a + b + c + d + e + f + g_ + h_ + [(k.future[:, :, :], k.w["future"])]
        with phase(k, "fill", "step") as (block, s):
            @block.vector
            def _(dve):
                nc.vector.memset(k.minus[:, :, :], -10000.0 * 4.0)

        def qkv(i):
            jobs = feature_jobs(qT[i], wq, k.xT, [P] * KD, W, bq) + feature_jobs(kT[i], wk, k.xT, [P] * KD, W, bk)
            return jobs + [(P, W, token_pairs(k, k.xT, [P] * KD, j, wv, slice(0, W), bv), turns(j), to_copy(v[i][:, j, :]))
                           for j in range(GROUP)]

        def head(t):
            return lambda j, h: t[PAD * (h % 4):PAD * (h % 4) + PAD, h // 4, sl(j)]

        def attend(i):
            return attention_part(k, H, PAD, head(qT[i]), head(kT[i]), lambda j, h: v[i][:, j, sl(h, PAD)],
                                  lambda j, u: oT[:, u:u + 1, sl(j)], 0.25, causal=True)
        attention_loop(k, loads, qkv, attend, lambda g: residual_jobs(k, g, oT, T, wo, bo), context=False)


def attention_loop(k, loads, qkv, attend, project, context):
    def norm_beside(g, *others):
        parts = []
        if g < GROUPS:
            parts.append((norm_part(k, g, lambda kt: k.xT[:, kt, :], (4, 5)), 1))
            if context:
                parts.append((context_part(k, g), 1))
        side_by_side(k, *others, *parts)

    norm_beside(0, (load_part(loads), 1))
    gemm_phase(k, "qkv", qkv(0))
    norm_beside(1)
    for g in range(GROUPS):
        beside = []
        if g + 1 < GROUPS:
            jobs = qkv((g + 1) % 2)
            beside.append((gemm_part(k, "qkv", jobs, (6, 7)), max(1, len(jobs) / 16)))
        side_by_side(k, (attend(g % 2), 1), *beside)
        norm_beside(g + 2, (gemm_part(k, "project", project(g), range(4)), 1))


def cross_attention(k, layer, heads, wo_name, bo_name):
    nc = k.nc
    W = heads * 64
    T = W // P
    with ExitStack() as stack:
        attention_memory(k, stack)
        wq, a = weights(k, stack, f"{layer}_Wq", KD, W)
        wk, b = ctx_weights(k, stack, f"{layer}_Wk", W)
        wv, c = ctx_weights(k, stack, f"{layer}_Wv", W)
        wo, d = weights(k, stack, wo_name, T, DIM)
        bo, e = bias_row(k, stack, bo_name, DIM)
        qT, kT = ([sb(k, stack, n, [P, T, GT]) for _ in range(2)] for n in ("qT", "kT"))
        v = [sb(k, stack, "v", [P, GROUP, W]) for _ in range(2)]
        oT = sb(k, stack, "oT", [P, T, GT])
        loads = a + b + c + d + e

        def qkv(i):
            jobs = feature_jobs(qT[i], wq, k.xT, [P] * KD, W) + feature_jobs(kT[i], wk, k.ctxG, CTX_ROWS, W)
            for j in range(GROUP):
                for c0 in range(0, W, 512):
                    jobs.append((P, 512, token_pairs(k, k.ctxG, CTX_ROWS, j, wv, slice(c0, c0 + 512)), turns(len(jobs)),
                                 to_copy(v[i][:, j, c0:c0 + 512])))
            return jobs

        def head(t):
            return lambda j, h: t[64 * (h % 2):64 * (h % 2) + 64, h // 2, sl(j)]

        def attend(i):
            return attention_part(k, heads, 64, head(qT[i]), head(kT[i]), lambda j, h: v[i][:, j, sl(h, 64)],
                                  lambda j, u: oT[:, 2 * u:2 * u + 2, sl(j)], 0.125)
        attention_loop(k, loads, qkv, attend, lambda g: residual_jobs(k, g, oT, T, wo, bo), context=True)


def empty_phase(k):
    with phase(k, "turn", "none") as (block, s):
        pass


def context_part(k, g):
    part = Part("context", "none")

    @part.gpsimd
    def _(pool, s):
        k.nc.gpsimd.tensor_copy(k.ctxG[:, 0, :], k.ctxT[:, 0, bass.ds(g * GT, GT)])
        k.nc.gpsimd.tensor_copy(k.ctxG[0:CTX - P, 1, :], k.ctxT[0:CTX - P, 1, bass.ds(g * GT, GT)])
        yield
    return part


def l0_xattn(k):
    nc = k.nc
    H, W = 16, 16 * PAD
    T = W // P
    n = "L0_xattn_"
    with ExitStack() as stack:
        attention_memory(k, stack)
        wq, a = weights(k, stack, n + "Wq", KD, DIM)
        wk, b = ctx_weights(k, stack, n + "Wk", DIM)
        wv, c = ctx_weights(k, stack, n + "Wv", W)
        wo, d = weights(k, stack, n + "Wo", T, DIM)
        loads = a + b + c + d
        bq, bk, bo = (sb(k, stack, m, [1, DIM]) for m in ("bq", "bk", "bo"))
        bv = sb(k, stack, "bv", [1, W])
        gamma, beta = sb(k, stack, "gamma", [P, DIM]), sb(k, stack, "beta", [P, DIM])
        loads += [(bq[:, :], k.w[n + "bq"]), (bk[:, :], k.w[n + "bk"]), (bo[:, :], k.w[n + "bo"]), (bv[:, :], k.w[n + "bv"]),
                  (gamma[:, :], k.w[n + "ln_gamma"]), (beta[:, :], k.w[n + "ln_beta"])]
        qT, kT, oT = (sb(k, stack, m, [P, T, GT]) for m in ("qT", "kT", "oT"))
        v = [sb(k, stack, "v", [P, GROUP, W]) for _ in range(2)]
        qp = [sb(k, stack, "qp", [P, GROUP, DIM]) for _ in range(2)]
        kp, square, y = (sb(k, stack, m, [P, GROUP, DIM]) for m in ("kp", "square", "y"))
        padded = sb(k, stack, "padded", [P, 2, GROUP, W])
        length = sb(k, stack, "length", [P, 2, GROUP])
        fill = Part("fill", "none")

        @fill.vector
        def _(dve, s):
            nc.vector.memset(padded[:, :, :, :], 0.0)
            yield

        def qkv(i):
            jobs = []
            for j in range(GROUP):
                jobs.append((P, DIM, token_pairs(k, k.xT, [P] * KD, j, wq, slice(0, DIM), bq), "act", to_copy(qp[i][:, j, :])))
                jobs.append((P, DIM, token_pairs(k, k.ctxG, CTX_ROWS, j, wk, slice(0, DIM), bk), "dve", to_copy(kp[:, j, :])))
                jobs.append((P, W, token_pairs(k, k.ctxG, CTX_ROWS, j, wv, slice(0, W), bv), "act", to_copy(v[i][:, j, :])))
            return jobs

        def norm_and_context(g):
            return (norm_part(k, g, lambda kt: k.xT[:, kt, :], (4, 5)), 1), (context_part(k, g), 1)

        def head(t):
            return lambda j, h: t[PAD * (h % 4):PAD * (h % 4) + PAD, h // 4, sl(j)]

        side_by_side(k, (load_part(loads), 1), *norm_and_context(0), (fill, 1))
        gemm_phase(k, "qkv", qkv(0))
        side_by_side(k, *norm_and_context(1))
        side_by_side(k, (unit_part(k, qp[0], kp, square, length, padded, qT, kT), 1))
        for g in range(GROUPS):
            i = g % 2
            coming, after = g + 1 < GROUPS, g + 2 < GROUPS
            side_by_side(k, (attention_part(k, H, PAD, head(qT), head(kT), lambda j, h: v[i][:, j, sl(h, PAD)],
                                            lambda j, u: oT[:, u:u + 1, sl(j)], 0.25), 1),
                         *([(gemm_part(k, "qkv", qkv(1 - i), (6, 7)), 1)] if coming else []))
            project = [(P, DIM, token_pairs(k, oT, [P] * T, j, wo, slice(0, DIM), bo), "dve",
                        to_sum(y[:, j, :], qp[i][:, j, :])) for j in range(GROUP)]
            side_by_side(k, (gemm_part(k, "project", project, range(4)), 1), *(norm_and_context(g + 2) if after else []))
            side_by_side(k, *([(unit_part(k, qp[1 - i], kp, square, length, padded, qT, kT), 1)] if coming else []),
                         (outer_part(k, g, y, gamma, beta), 1))


def unit_part(k, qp, kp, square, length, padded, qT, kT):
    nc = k.nc
    T = padded.shape[3] // P
    part = Part("unit", "step squared rooted unit turned")

    @part.vector
    def _(dve, s):
        link = Link(dve, s["step"])
        for i, rows in enumerate((qp, kp)):
            for j in range(GROUP):
                last = nc.vector.tensor_tensor_reduce(square[:, j, :], rows[:, j, :], rows[:, j, :], 1.0, 0.0,
                                                      ALU.mult, ALU.add, length[:, i, j:j + 1])
            if i == 0:
                link(last)
        last.then_inc(s["squared"], 1)
        yield
        dve.wait_ge(s["rooted"], 1)
        link(nc.vector.tensor_scalar(length[:, :, :], length[:, :, :], 1e-12, None, ALU.max))
        link(nc.vector.reciprocal(length[:, :, :], length[:, :, :]))
        for i, rows in enumerate((qp, kp)):
            for j in range(GROUP):
                nc.vector.tensor_scalar(padded[:, i, j, :].rearrange("p (h d) -> p h d", d=PAD)[:, :, 0:16],
                                        rows[:, j, :].rearrange("p (h d) -> p h d", d=16),
                                        length[:, i, j:j + 1], None, ALU.mult).then_inc(s["unit"], 1)
        yield
        for m in range(T):
            dve.wait_ge(s["turned"], T + m + 1)
            nc.vector.tensor_copy(kT[:, m, :], k.ps[:, T + m, :])
            yield

    @part.scalar
    def _(act, s):
        act.wait_ge(s["squared"], 1)
        nc.scalar.activation(length[:, :, :], length[:, :, :], ACT.Sqrt).then_inc(s["rooted"], 1)
        yield
        yield
        for m in range(T):
            act.wait_ge(s["turned"], m + 1)
            nc.scalar.activation(qT[:, m, :], k.ps[:, m, :], ACT.Copy)
            yield

    @part.tensor
    def _(pe, s):
        for i in range(2):
            pe.wait_ge(s["unit"], GROUP * (i + 1))
            for m in range(T):
                for j in range(GROUP):
                    last = nc.tensor.transpose(k.ps[:, T * i + m, sl(j)], padded[:, i, j, sl(m)], k.ident[:, :])
                last.then_inc(s["turned"], 1)
                yield
    return part


def outer_part(k, g, y, gamma, beta):
    nc = k.nc
    part = Part("outer", "step measured rooted normed scaled")

    @part.vector
    def _(dve, s):
        link = Link(dve, s["step"])
        row_stats(k, dve, link, lambda j: y[:, j, :], s["measured"])
        yield
        dve.wait_ge(s["rooted"], 1)
        for j in range(GROUP):
            nc.vector.tensor_scalar(y[:, j, :], y[:, j, :], k.moments[:, j, 0:1], k.rstd[:, j:j + 1],
                                    ALU.subtract, ALU.mult).then_inc(s["normed"], 1)
        yield

    @part.scalar
    def _(act, s):
        row_rstd(k, act, s["measured"], s["rooted"])
        yield

    @part.gpsimd
    def _(pool, s):
        yield
        yield
        pool.wait_ge(s["normed"], GROUP)
        nc.gpsimd.tensor_tensor(y[:, :, :], y[:, :, :], gamma[:, :].unsqueeze(1).broadcast_to([P, GROUP, DIM]),
                                ALU.mult).then_inc(s["scaled"], 1)
        pool.wait_ge(s["scaled"], 1)
        nc.gpsimd.tensor_tensor(y[:, :, :], y[:, :, :], beta[:, :].unsqueeze(1).broadcast_to([P, GROUP, DIM]),
                                ALU.add).then_inc(s["scaled"], 1)
        pool.wait_ge(s["scaled"], 2)
        x = k.x[:, bass.ds(g * GROUP, GROUP), :]
        nc.gpsimd.tensor_tensor(x, x, y[:, :, :], ALU.add)
        yield
    return part


def l0_ffn(k):
    nc = k.nc
    E, TOP, INNER, SET = 32, 8, 128, 3
    SETS = (E + 1) // SET
    COLS = 2 * KD * INNER + DIM + 2
    n = "L0_ffn_"
    with ExitStack() as stack:
        wr, a = weights(k, stack, n + "Wr", KD, E)
        br, b = bias_row(k, stack, n + "br", E)
        bd = sb(k, stack, "bd", [E + 1, DIM])
        xA = sb(k, stack, "xA", [P, KD, TOKENS])
        share = sb(k, stack, "share", [P, BATCH, E + 1])
        affinity, rest = sb(k, stack, "affinity", [P, GROUP, E]), sb(k, stack, "rest", [P, GROUP, E])
        chosen = sb(k, stack, "chosen", [P, GROUP, E + 1])
        top, total = sb(k, stack, "top", [P, GROUP, TOP]), sb(k, stack, "total", [P, GROUP])
        chosenT = sb(k, stack, "chosenT", [E + 1, GROUP, P])
        experts = [sb(k, stack, f"experts{i}", [P, SET, COLS]) for i in range(2)]
        load_phase(k, a + b + [(bd[:, :], k.w[n + "bd"]), (experts[0][:, :, :], k.w[n + "experts"][0])])
        with phase(k, "fill", "none") as (block, s):
            @block.vector
            def _(dve):
                nc.vector.memset(chosen[:, :, :], 1.0)

        def route(g, more):
            def to_sigmoid(dst):
                return lambda nc, engine, bank: nc.scalar.activation(dst, bank, ACT.Sigmoid)
            gemm_phase(k, "router", [(P, E, token_pairs(k, k.xT, [P] * KD, j, wr, slice(0, E), br), "act",
                                      to_sigmoid(affinity[:, j, :])) for j in range(GROUP)])

            with phase(k, "choose", "step chosen") as (block, s):
                @block.vector
                def _(dve):
                    link = Link(dve, s["step"])
                    for j in range(GROUP):
                        last = nc.vector.max(top[:, j, :], affinity[:, j, :])
                    link(last)
                    for j in range(GROUP):
                        last = nc.vector.match_replace(rest[:, j, :], top[:, j, :], affinity[:, j, :], -1.0)
                    link(last)
                    link(nc.vector.tensor_reduce(total[:, :], top[:, :, :], AX.X, ALU.add))
                    link(nc.vector.tensor_scalar(total[:, :], total[:, :], 1e-9, None, ALU.add))
                    link(nc.vector.reciprocal(total[:, :], total[:, :]))
                    link(nc.vector.scalar_tensor_tensor(chosen[:, :, 0:E], rest[:, :, :], 0.0, affinity[:, :, :], ALU.is_lt, ALU.mult))
                    link(nc.vector.tensor_tensor(chosen[:, :, 0:E], chosen[:, :, 0:E],
                                                 total[:, :].unsqueeze(2).broadcast_to([P, GROUP, E]), ALU.mult))
                    nc.vector.tensor_copy(share[:, bass.ds(g * GROUP, GROUP), :], chosen[:, :, :])

            def turn_chosen(j):
                return lambda nc, bank: nc.tensor.transpose(bank, chosen[:, j, :], k.ident[:, :])
            gemm_phase(k, "turn", [(E + 1, P, turn_chosen(j), turns(j), to_copy(chosenT[:, j, :])) for j in range(GROUP)])

            jobs = []
            for j in range(GROUP):
                x = k.x[:, bass.ds(g * GROUP + j, 1), :]
                jobs.append((P, DIM, products([(chosenT[:, j, :], bd[:, :])]), "dve",
                             lambda nc, engine, bank, x=x: nc.vector.tensor_tensor(x, bank.rearrange("p (o d) -> p o d", o=1), x, ALU.add)))
            side_by_side(k, (gemm_part(k, "biases", jobs, range(4)), 1),
                         *([(norm_part(k, g + 1, lambda kt: k.xT[:, kt, :], (4, 5), xA), 1)] if more else []))

        norm_phase(k, 0, lambda kt: k.xT[:, kt, :], xA)
        each_group(k, route)

        with ExitStack() as inner:
            silu_gate = sb(k, inner, "silu_gate", [P, 2, GT])
            hidden = sb(k, inner, "hidden", [P, 2, GT])
            share_now = sb(k, inner, "share_now", [P, BATCH, SET])

            def set_phase(now, first, later=None):
                units = [(e, c) for e in range(SET) for c in range(GROUPS)]
                up_at = KD * INNER
                down_at = 2 * KD * INNER
                with phase(k, "experts", "loaded gated upped silued multiplied downed fetched added") as (block, s):
                    @block.sync
                    def _(sp):
                        if later is not None:
                            dst, index = later
                            sp.dma_start(dst[:, :, :].rearrange("p e c -> p (e c)"),
                                         k.w[n + "experts"].rearrange("i p e c -> (i p) (e c)")[bass.ds(index * P, P), :]).then_inc(s["loaded"], 16)
                            sp.wait_ge(s["loaded"], 16)

                    @block.tensor
                    def _(pe):
                        def down(m):
                            e, c = units[m]
                            pe.wait_ge(s["multiplied"], m + 1)
                            if m >= 2:
                                pe.wait_ge(s["added"], m - 1)
                            for j in range(GROUP):
                                last = nc.tensor.matmul(k.ps[:, 4 + 2 * (m % 2) + j // 2, sl(j % 2, DIM)], hidden[:, m % 2, sl(j)],
                                                        now[:, e, down_at:down_at + DIM], start=True, stop=True)
                            last.then_inc(s["downed"], 1)

                        for m, (e, c) in enumerate(units):
                            if m >= 2:
                                pe.wait_ge(s["silued"], m - 1)
                                pe.wait_ge(s["multiplied"], m - 1)
                            for at, base, sem in ((0, 0, s["gated"]), (up_at, 2, s["upped"])):
                                for kt in range(KD):
                                    last = nc.tensor.matmul(k.ps[:, base + m % 2, :], now[:, e, at + kt * INNER:at + (kt + 1) * INNER],
                                                            xA[:, kt, sl(c, GT)], start=kt == 0, stop=kt == KD - 1)
                                last.then_inc(sem, 1)
                            if m >= 1:
                                down(m - 1)
                        down(len(units) - 1)

                    @block.scalar
                    def _(act):
                        for m, (e, c) in enumerate(units):
                            act.wait_ge(s["gated"], m + 1)
                            if m >= 2:
                                act.wait_ge(s["multiplied"], m - 1)
                            nc.scalar.activation(silu_gate[:, m % 2, :], k.ps[:, m % 2, :], ACT.Silu,
                                                 bias=now[:, e, COLS - 2:COLS - 1]).then_inc(s["silued"], 1)

                    @block.vector
                    def _(dve):
                        nc.vector.tensor_copy(share_now[:, :, :], share[:, :, bass.ds(first, SET)]).then_inc(s["fetched"], 1)

                        def add(m):
                            e, c = units[m]
                            dve.wait_ge(s["downed"], m + 1)
                            if m == 0:
                                dve.wait_ge(s["fetched"], 1)
                            if m >= GROUPS:
                                dve.wait_ge(s["added"], m - GROUPS + 1)
                            for j in range(GROUP):
                                t = GROUP * c + j
                                last = nc.vector.scalar_tensor_tensor(k.x[:, t, :], k.ps[:, 4 + 2 * (m % 2) + j // 2, sl(j % 2, DIM)],
                                                                      share_now[:, t, e:e + 1], k.x[:, t, :], ALU.mult, ALU.add)
                            last.then_inc(s["added"], 1)

                        for m, (e, c) in enumerate(units):
                            dve.wait_ge(s["upped"], m + 1)
                            dve.wait_ge(s["silued"], m + 1)
                            if m >= 2:
                                dve.wait_ge(s["downed"], m - 1)
                            nc.vector.scalar_tensor_tensor(hidden[:, m % 2, :], k.ps[:, 2 + m % 2, :], now[:, e, COLS - 1:COLS],
                                                           silu_gate[:, m % 2, :], ALU.add, ALU.mult).then_inc(s["multiplied"], 1)
                            if m >= 1:
                                add(m - 1)
                        add(len(units) - 1)

            with nc.Fori(0, SETS // 2) as i:
                set_phase(experts[0], i * 2 * SET, (experts[1], 2 * i + 1))
                set_phase(experts[1], (2 * i + 1) * SET, (experts[0], 2 * i + 2))
            set_phase(experts[0], (SETS - 1) * SET)


def l2_ffn(k):
    nc = k.nc
    E, INNER, TOP = 8, 512, TOKENS // 8
    M = INNER // P
    n = "L2_ffn_"
    COLS = KD * INNER + M * DIM
    with ExitStack() as stack:
        wg, a = weights(k, stack, n + "Wg", KD, E)
        xA = sb(k, stack, "xA", [P, KD, TOKENS])
        share = sb(k, stack, "share", [P, BATCH, E])
        experts = [sb(k, stack, f"expert{i}", [P, COLS]) for i in range(2)]
        order = sb(k, stack, "order", [P, BATCH, E])
        early = [sb(k, stack, "early", [P, BATCH, DIM]) for _ in range(2)]
        hidden = sb(k, stack, "hidden", [P, 2, M, GT])
        share_now = sb(k, stack, "share_now", [P, BATCH])
        probs = sb(k, stack, "probs", [P, BATCH, E])
        load_phase(k, a + [(experts[0][:, :], k.w[n + "experts"][0]), (order[:, :, :], k.w["order"])])
        with nc.Fori(0, GROUPS) as g:
            norm_phase(k, g, lambda kt: k.xT[:, kt, :], xA)

            def to_probs(j):
                return lambda nc, engine, bank: to_copy(probs[:, bass.ds(g * GROUP + j, 1), :])(
                    nc, engine, bank.rearrange("p (o e) -> p o e", o=1))
            gemm_phase(k, "router", [(P, E, token_pairs(k, k.xT, [P] * KD, j, wg, slice(0, E)), "act", to_probs(j))
                                     for j in range(GROUP)])

        def expert(now, e, later=None, keep=None, late=None):
            part = Part("expert", "loaded upped gelued downed fetched added")

            @part.sync
            def _(sp, s):
                if later is not None:
                    dst, index = later
                    sp.dma_start(dst[:, :], k.w[n + "experts"].rearrange("i p c -> (i p) c")[bass.ds(index * P, P), :]).then_inc(s["loaded"], 16)
                    sp.wait_ge(s["loaded"], 16)
                yield

            def downs(c, half):
                return k.ps[:, 4 + 2 * (c % 2) + half, :]

            @part.tensor
            def _(pe, s):
                def down(c):
                    pe.wait_ge(s["gelued"], M * (c + 1))
                    if c >= 2:
                        pe.wait_ge(s["added"], c - 1)
                    for j in range(GROUP):
                        for m in range(M):
                            at = KD * INNER + m * DIM
                            last = nc.tensor.matmul(downs(c, j // 2)[:, sl(j % 2, DIM)], hidden[:, c % 2, m, sl(j)],
                                                    now[:, at:at + DIM], start=m == 0, stop=m == M - 1)
                    last.then_inc(s["downed"], 1)

                for c in range(GROUPS):
                    for m in range(M):
                        if c >= 1:
                            pe.wait_ge(s["gelued"], M * (c - 1) + m + 1)
                        for kt in range(KD):
                            at = kt * INNER + m * P
                            last = nc.tensor.matmul(k.ps[:, m, :], now[:, at:at + P], xA[:, kt, sl(c, GT)],
                                                    start=kt == 0, stop=kt == KD - 1)
                        last.then_inc(s["upped"], 1)
                    if c >= 1:
                        down(c - 1)
                    yield
                down(GROUPS - 1)
                yield

            @part.scalar
            def _(act, s):
                def take(c):
                    act.wait_ge(s["downed"], c + 1)
                    for half in range(2):
                        at = GROUP * c + 2 * half
                        last = nc.scalar.activation(early[keep][:, at:at + 2, :].rearrange("p t d -> p (t d)"), downs(c, half), ACT.Copy)
                    last.then_inc(s["added"], 1)

                for c in range(GROUPS):
                    if c >= 2:
                        act.wait_ge(s["downed"], c - 1)
                    for m in range(M):
                        act.wait_ge(s["upped"], M * c + m + 1)
                        nc.scalar.activation(hidden[:, c % 2, m, :], k.ps[:, m, :], ACT.Gelu).then_inc(s["gelued"], 1)
                    if keep is not None and c >= 1:
                        take(c - 1)
                    yield
                if keep is not None:
                    take(GROUPS - 1)
                yield

            @part.vector
            def _(dve, s):
                if keep is not None:
                    return
                nc.vector.tensor_copy(share_now[:, :].unsqueeze(2), share[:, :, bass.ds(e, 1)]).then_inc(s["fetched"], 1)
                dve.wait_ge(s["fetched"], 1)
                if late is not None:
                    for t in range(BATCH):
                        last = nc.vector.scalar_tensor_tensor(k.x[:, t, :], early[late][:, t, :], share[:, t, late:late + 1],
                                                              k.x[:, t, :], ALU.mult, ALU.add)
                    last.then_inc(s["fetched"], 1)
                    dve.wait_ge(s["fetched"], 2)
                for c in range(GROUPS):
                    dve.wait_ge(s["downed"], c + 1)
                    for j in range(GROUP):
                        t = GROUP * c + j
                        last = nc.vector.scalar_tensor_tensor(k.x[:, t, :], downs(c, j // 2)[:, sl(j % 2, DIM)],
                                                              share_now[:, t:t + 1], k.x[:, t, :], ALU.mult, ALU.add)
                    last.then_inc(s["added"], 1)
                    yield
            return part

        with ExitStack() as inner:
            peak = sb(k, inner, "peak", [P, BATCH])
            first, second = sb(k, inner, "first", [P, BATCH, E]), sb(k, inner, "second", [P, BATCH, E])
            probsT, restT = sb(k, inner, "probsT", [E, TOKENS]), sb(k, inner, "restT", [E, TOKENS])
            best = sb(k, inner, "best", [E, 2, 8])
            all_e = [P, BATCH, E]

            def spread(t):
                return t[:, :].unsqueeze(2).broadcast_to(all_e)

            with phase(k, "softmax", "step shifted exped") as (block, s):
                @block.vector
                def _(dve):
                    link = Link(dve, s["step"])
                    link(nc.vector.tensor_reduce(peak[:, :], probs[:, :, :], AX.X, ALU.max))
                    nc.vector.tensor_tensor(first[:, :, :], probs[:, :, :], spread(peak), ALU.subtract).then_inc(s["shifted"], 1)
                    dve.wait_ge(s["exped"], 1)
                    link(nc.vector.tensor_reduce(peak[:, :], first[:, :, :], AX.X, ALU.add))
                    link(nc.vector.reciprocal(peak[:, :], peak[:, :]))
                    nc.vector.tensor_tensor(probs[:, :, :], first[:, :, :], spread(peak), ALU.mult)

                @block.scalar
                def _(act):
                    act.wait_ge(s["shifted"], 1)
                    nc.scalar.activation(first[:, :, :], first[:, :, :], ACT.Exp).then_inc(s["exped"], 1)

            def turn4(i, source, rows, columns):
                def fill(nc, bank):
                    for j in range(4):
                        last = nc.tensor.transpose(bank[:, j * columns:(j + 1) * columns], source(4 * i + j), k.ident[0:rows, 0:rows])
                    return last
                return fill
            gemm_phase(k, "turn", [(E, GT, turn4(i, lambda t: probs[:, t, :], P, P), turns(i), to_copy(probsT[:, sl(i, GT)]))
                                   for i in range(GROUPS)])

            def take_top(rounds):
                part = Part("top", "step")

                @part.vector
                def _(dve, s):
                    link = Link(dve, s["step"])
                    for r in rounds:
                        source = probsT if r == 0 else restT
                        link(nc.vector.max(best[:, r % 2, :], source[:, :]))
                        link(nc.vector.match_replace(restT[:, :], best[:, r % 2, :], source[:, :], -1.0))
                        yield
                return part

            side_by_side(k, (take_top(range(0, TOP // 16)), 1), (expert(experts[0], 0, (experts[1], 1), keep=0), 1))
            side_by_side(k, (take_top(range(TOP // 16, TOP // 8)), 1), (expert(experts[1], 1, (experts[0], 2), keep=1), 1))
            gemm_phase(k, "turn", [(P, 4 * E, turn4(i, lambda t: restT[:, sl(t)], E, E), turns(i),
                                    to_copy(first[:, sl(i, 4), :].rearrange("p t e -> p (t e)"))) for i in range(GROUPS)])

            with phase(k, "assign", "step") as (block, s):
                @block.vector
                def _(dve):
                    link = Link(dve, s["step"])
                    v = nc.vector
                    link(v.tensor_scalar(first[:, :, :], first[:, :, :], 0.0, None, ALU.is_lt))
                    link(v.tensor_reduce(peak[:, :], first[:, :, :], AX.X, ALU.max))
                    link(v.tensor_tensor(second[:, :, :], first[:, :, :], spread(peak), ALU.is_ge))
                    link(v.scalar_tensor_tensor(first[:, :, :], probs[:, :, :], 1.0, second[:, :, :], ALU.add, ALU.mult))
                    link(v.tensor_reduce(peak[:, :], first[:, :, :], AX.X, ALU.max))
                    link(v.tensor_tensor(second[:, :, :], first[:, :, :], spread(peak), ALU.is_equal))
                    link(v.tensor_tensor(second[:, :, :], second[:, :, :], order[:, :, :], ALU.mult))
                    link(v.tensor_reduce(peak[:, :], second[:, :, :], AX.X, ALU.max))
                    link(v.tensor_tensor(second[:, :, :], second[:, :, :], spread(peak), ALU.is_equal))
                    v.tensor_tensor(share[:, :, :], second[:, :, :], probs[:, :, :], ALU.mult)

        with nc.Fori(0, E // 2 - 2) as i:
            side_by_side(k, (expert(experts[0], 2 * i + 2, (experts[1], 2 * i + 3)), 1))
            side_by_side(k, (expert(experts[1], 2 * i + 3, (experts[0], 2 * i + 4)), 1))
        side_by_side(k, (expert(experts[0], E - 2, (experts[1], E - 1), late=0), 1))
        side_by_side(k, (expert(experts[1], E - 1, late=1), 1))


def l3_ffn(k):
    nc = k.nc
    INNER, RANK = 1024, 16
    M = INNER // P
    n = "L3_ffn_"
    with ExitStack() as stack:
        wf, a = weights(k, stack, n + "W_fc", KD, INNER)
        wp, b = weights(k, stack, n + "W_proj", M, DIM)
        bf, c = bias_columns(k, stack, n + "b_fc", M)
        bp, d = bias_row(k, stack, n + "b_proj", DIM)
        af, bfT = sb(k, stack, "af", [RANK, DIM]), sb(k, stack, "bfT", [RANK, INNER])
        ap, bpT = sb(k, stack, "ap", [RANK, INNER]), sb(k, stack, "bpT", [RANK, DIM])
        load_phase(k, a + b + c + d + [(af[:, :], k.w[n + "A_fc"]), (bfT[:, :], k.w[n + "B_fc"]),
                                       (ap[:, :], k.w[n + "A_proj"]), (bpT[:, :], k.w[n + "B_proj"])])
        hT = sb(k, stack, "hT", [P, M, GT])
        size = sb(k, stack, "size", [P, 2, 4])
        row_ = sb(k, stack, "row", [1, 4])

        for which, w in enumerate((wf, wp)):
            flat = w[:, :, :]
            peak, step, inverse = size[:, which, 0:1], size[:, which, 1:2], size[:, which, 2:3]
            with phase(k, "round", "step peaked turned maxed spread") as (block, s):
                @block.vector
                def _(dve):
                    link = Link(dve, s["step"])
                    v = nc.vector
                    v.tensor_reduce(peak, w[:, :, :], AX.XY, ALU.max, apply_absolute_value=True).then_inc(s["peaked"], 1)
                    dve.wait_ge(s["turned"], 1)
                    link(v.tensor_reduce(row_[:, 0:1], k.ps[0:1, 0, 0:P], AX.X, ALU.max))
                    v.tensor_scalar(row_[:, 1:2], row_[:, 0:1], 1.0 / 127.0, None, ALU.mult).then_inc(s["maxed"], 1)
                    dve.wait_ge(s["spread"], 1)
                    link(v.tensor_copy(step, k.ps[:, 1, 0:1]))
                    link(v.reciprocal(inverse, step))
                    link(v.tensor_scalar(flat, flat, inverse, MAGIC, ALU.mult, ALU.add))
                    link(v.tensor_scalar(flat, flat, MAGIC, 127.0, ALU.subtract, ALU.min))
                    v.tensor_scalar(flat, flat, -128.0, step, ALU.max, ALU.mult)

                @block.tensor
                def _(pe):
                    pe.wait_ge(s["peaked"], 1)
                    nc.tensor.transpose(k.ps[0:1, 0, 0:P], peak, k.ident[:, :]).then_inc(s["turned"], 1)
                    pe.wait_ge(s["maxed"], 1)
                    nc.tensor.matmul(k.ps[:, 1, 0:1], k.ones[0:1, 0:P], row_[:, 1:2], start=True, stop=True).then_inc(s["spread"], 1)

        def to_twice(dst):
            return lambda nc, engine, bank: nc.vector.scalar_tensor_tensor(dst, bank, 2.0, dst, ALU.mult, ALU.add)
        jobs = [(P, 512, products([(af[:, sl(kt)], bfT[:, sl(c, 512)])]), "dve", to_twice(wf[:, kt, sl(c, 512)]))
                for kt in range(KD) for c in range(INNER // 512)]
        jobs += [(P, DIM, products([(ap[:, sl(m)], bpT[:, :])]), "dve", to_twice(wp[:, m, :])) for m in range(M)]
        gemm_phase(k, "lora", jobs)

        def to_gelu(m):
            return lambda nc, engine, bank: nc.scalar.activation(hT[:, m, :], bank, ACT.Gelu, bias=bf[:, m:m + 1])
        def group(g, more):
            gemm_phase(k, "up", [(P, GT, products([(wf[:, kt, sl(m)], k.xT[:, kt, :]) for kt in range(KD)]), "act", to_gelu(m))
                                 for m in range(M)])
            side_by_side(k, (gemm_part(k, "down", residual_jobs(k, g, hT, M, wp, bp), range(4)), 1),
                         *([(norm_part(k, g + 1, lambda kt: k.xT[:, kt, :], (4, 5)), 1)] if more else []))

        norm_phase(k, 0, lambda kt: k.xT[:, kt, :])
        each_group(k, group)


def l1_attn(k):
    nc = k.nc
    H, D, C = 16, 16, 64
    PAIRS, T = H // 2, H * PAD // P
    VW = D + 1
    n = "L1_attn_"
    with ExitStack() as stack:
        wq, a = weights(k, stack, n + "W_q", KD, H * PAD)
        wk, b = weights(k, stack, n + "W_k", KD, H * PAD)
        wv, c = weights(k, stack, n + "W_v", KD, DIM)
        wo, d = weights(k, stack, n + "W_o", KD, DIM)
        centers, e = sb(k, stack, "centers", [P, PAIRS, P]), None
        where = sb(k, stack, "where", [P, PAIRS, P])
        scales, amplitude = sb(k, stack, "scales", [P, PAIRS]), sb(k, stack, "amplitude", [P, PAIRS])
        center2 = sb(k, stack, "center2", [P, PAIRS])
        qT, kT = (sb(k, stack, m, [P, T, GT]) for m in ("qT", "kT"))
        square = [sb(k, stack, f"square{i}", [P, T, GT]) for i in range(2)]
        near = [sb(k, stack, f"near{i}", [P, PAIRS, GT]) for i in range(2)]
        keysT = sb(k, stack, "keysT", [P, GROUP, PAIRS, P])
        values = sb(k, stack, "values", [P, GROUP, H, VW])
        pooled = sb(k, stack, "pooled", [P, GROUP, PAIRS, 2 * VW])
        share = sb(k, stack, "share", [P, GROUP, H])
        mixed = sb(k, stack, "mixed", [P, GROUP, DIM])
        oT = sb(k, stack, "oT", [P, KD, GT])
        load_phase(k, a + b + c + d + [(centers[:, :, :], k.w[n + "centers"]), (where[:, :, :], k.w[n + "where"]),
                                       (scales[:, :], k.w[n + "log_scales"]), (amplitude[:, :], k.w[n + "amplitudes"])])
        with phase(k, "centers", "step exped squared summed") as (block, s):
            @block.vector
            def _(dve):
                link = Link(dve, s["step"])
                v = nc.vector
                v.tensor_tensor(near[0][:, :, 0:P], centers[:, :, :], centers[:, :, :], ALU.mult).then_inc(s["squared"], 1)
                v.memset(values[:, :, :, :], 1.0)
                v.memset(pooled[:, :, :, :], 0.0)
                dve.wait_ge(s["exped"], 1)
                link(v.tensor_scalar(scales[:, :], scales[:, :], 1e-3, None, ALU.max))
                link(v.tensor_tensor(scales[:, :], scales[:, :], scales[:, :], ALU.mult))
                link(v.reciprocal(scales[:, :], scales[:, :]))
                v.tensor_scalar(scales[:, :], scales[:, :], -0.5, None, ALU.mult)
                v.tensor_tensor(amplitude[:, :], amplitude[:, :], amplitude[:, :], ALU.mult)
                dve.wait_ge(s["summed"], 1)
                v.tensor_copy(center2[:, :], k.ps[:, 0, 0:PAIRS])
                v.tensor_scalar(centers[:, :, :], centers[:, :, :], -2.0, None, ALU.mult)

            @block.scalar
            def _(act):
                nc.scalar.activation(scales[:, :], scales[:, :], ACT.Exp).then_inc(s["exped"], 1)

            @block.tensor
            def _(pe):
                pe.wait_ge(s["squared"], 1)
                for p in range(PAIRS):
                    last = nc.tensor.matmul(k.ps[:, 0, p:p + 1], near[0][:, p, 0:P], k.ones[:, 0:1], start=True, stop=True)
                last.then_inc(s["summed"], 1)

        query_jobs = feature_jobs(qT, wq, k.xT, [P] * KD, H * PAD) + feature_jobs(kT, wk, k.xT, [P] * KD, H * PAD)

        def to_values(j):
            def evacuate(nc, engine, bank):
                return to_copy(values[:, j, :, 0:D])(nc, engine, bank.rearrange("p (h d) -> p h d", d=D))
            return evacuate
        value_jobs = [(P, DIM, token_pairs(k, k.xT, [P] * KD, j, wv, slice(0, DIM)), turns(j), to_values(j)) for j in range(GROUP)]

        def group(g, more):
            def beside(part):
                return [(part, 1)] if more else []

            with phase(k, "affinity", "squared keys_squared measured bounded") as (block, s):
                jobs = [(side, p) for side in range(2) for p in range(PAIRS)]

                @block.scalar
                def _(act):
                    nc.scalar.activation(square[0][:, :, :], qT[:, :, :], ACT.Square).then_inc(s["squared"], 1)
                    for m, (side, p) in enumerate(jobs):
                        act.wait_ge(s["bounded"], m + 1)
                        nc.scalar.activation(near[side][:, p, :], near[side][:, p, :], ACT.Exp, scale=scales[:, p:p + 1])

                @block.gpsimd
                def _(pool):
                    nc.gpsimd.tensor_tensor(square[1][:, :, :], kT[:, :, :], kT[:, :, :], ALU.mult).then_inc(s["keys_squared"], 1)

                @block.tensor
                def _(pe):
                    for m, (side, p) in enumerate(jobs):
                        if p == 0:
                            pe.wait_ge((s["squared"], s["keys_squared"])[side], 1)
                        if m >= 8:
                            pe.wait_ge(s["bounded"], m - 7)
                        source = (qT, kT)[side]
                        nc.tensor.matmul(k.ps[:, m % 8, :], centers[:, p, :], source[:, p // 2, :], start=True, stop=False)
                        nc.tensor.matmul(k.ps[:, m % 8, :], where[:, p, :], square[side][:, p // 2, :],
                                         start=False, stop=True).then_inc(s["measured"], 1)

                @block.vector
                def _(dve):
                    for m, (side, p) in enumerate(jobs):
                        dve.wait_ge(s["measured"], m + 1)
                        nc.vector.tensor_scalar(near[side][:, p, :], k.ps[:, m % 8, :], center2[:, p:p + 1], 0.0,
                                                ALU.add, ALU.max).then_inc(s["bounded"], 1)

            turn = gemm_part(k, "turn", [(P, GT, turned([near[1][:, 4 * i + p, sl(j)] for p in range(4)], k.ident[:, :]),
                                    turns(i), to_copy(keysT[:, j, sl(i, 4), :].rearrange("p a b -> p (a b)")))
                                         for j in range(GROUP) for i in range(PAIRS // 4)], range(4))
            side_by_side(k, (turn, 2), *beside(norm_part(k, g + 1, lambda kt: k.xT[:, kt, :], (4, 5))))

            def pool_values(j):
                def fill(nc, bank):
                    for p in range(PAIRS):
                        last = nc.tensor.matmul(bank[:, sl(p, 2 * VW)], keysT[:, j, p, :],
                                                values[:, j, sl(p, 2), :].rearrange("p h d -> p (h d)"), start=True, stop=True)
                    return last
                return fill

            def to_pooled(j):
                def evacuate(nc, engine, bank):
                    for i in range(2):
                        rows = slice(C * i, C * i + C)
                        source = bank[rows, :].rearrange("p (a d) -> p a d", d=2 * VW)[:, :, sl(i, VW)]
                        last = nc.vector.tensor_tensor(pooled[rows, j, :, sl(i, VW)], source,
                                                       amplitude[rows, :].unsqueeze(2).broadcast_to([C, PAIRS, VW]), ALU.mult)
                    return last
                return evacuate
            side_by_side(k, (gemm_part(k, "pool", [(P, H * VW, pool_values(j), "dve", to_pooled(j)) for j in range(GROUP)], range(4)), 1),
                         *beside(gemm_part(k, "queries", query_jobs, range(4, 8))))
            side_by_side(k, (mix_part(), 1), *beside(gemm_part(k, "values", value_jobs, (6, 7))))
            gemm_phase(k, "project", residual_jobs(k, g, oT, KD, wo))
            empty_phase(k)

        def mix_part():
            part = Part("mix", "step mixed divided turned")

            @part.tensor
            def _(pe, s):
                for j in range(GROUP):
                    for p in range(PAIRS):
                        last = nc.tensor.matmul(k.ps[:, j, sl(p, 2 * VW)], near[0][:, p, sl(j)], pooled[:, j, p, :], start=True, stop=True)
                    last.then_inc(s["mixed"], 1)
                    yield
                for j in range(GROUP):
                    pe.wait_ge(s["divided"], j + 1)
                    for kt in range(KD):
                        last = nc.tensor.transpose(k.ps[:, 4 + kt, sl(j)], mixed[:, j, sl(kt)], k.ident[:, :])
                    last.then_inc(s["turned"], 1)
                yield

            @part.vector
            def _(dve, s):
                link = Link(dve, s["step"])
                for j in range(GROUP):
                    dve.wait_ge(s["mixed"], j + 1)
                    bank = k.ps[:, j, 0:H * VW].rearrange("p (h d) -> p h d", d=VW)
                    link(nc.vector.tensor_scalar(share[:, j, :].unsqueeze(2), bank[:, :, D:VW], 1e-6, None, ALU.add))
                    link(nc.vector.reciprocal(share[:, j, :], share[:, j, :]))
                    nc.vector.tensor_tensor(mixed[:, j, :].rearrange("p (h d) -> p h d", d=D), bank[:, :, 0:D],
                                            share[:, j, :].unsqueeze(2).broadcast_to([P, H, D]), ALU.mult).then_inc(s["divided"], 1)
                    yield
                yield
                dve.wait_ge(s["turned"], GROUP)
                nc.vector.tensor_copy(oT[:, 1, :], k.ps[:, 5, :])
                yield

            @part.scalar
            def _(act, s):
                for _ in range(GROUP + 1):
                    yield
                act.wait_ge(s["turned"], GROUP)
                nc.scalar.activation(oT[:, 0, :], k.ps[:, 4, :], ACT.Copy)
                yield
            return part

        norm_phase(k, 0, lambda kt: k.xT[:, kt, :])
        gemm_phase(k, "qkv", query_jobs + value_jobs)
        each_group(k, group)


def l1_ffn(k):
    nc = k.nc
    INNER = 1024
    M = INNER // P
    n = "L1_ffn_"
    with ExitStack() as stack:
        wg, a = weights(k, stack, n + "w_gate", KD, INNER)
        wu, b = weights(k, stack, n + "w_up", KD, INNER)
        wd, c = weights(k, stack, n + "w_down", M, DIM)
        ternary = [sb(k, stack, f"ternary{i}", [P, 2 * INNER], BF16) for i in range(3)]
        size = sb(k, stack, "size", [P, 3, 3])
        identb = sb(k, stack, "identb", [P, P], BF16)
        rows = sb(k, stack, "rows", [P, GROUP, INNER])
        gate = sb(k, stack, "gate", [P, GROUP, INNER])
        rounded = sb(k, stack, "rounded", [P, GROUP, INNER], BF16)
        roundedT = sb(k, stack, "roundedT", [P, M, GT], BF16)
        peak, inverse = sb(k, stack, "peak", [P, GROUP]), sb(k, stack, "inverse", [P, GROUP])
        factor, down_factor = (sb(k, stack, m, [P, 3, GROUP]) for m in ("factor", "down_factor"))
        load_phase(k, a + b + c)
        flat = [w[:, :, :].rearrange("p a b -> p (a b)") for w in (wg, wu, wd)]
        with phase(k, "ternary", "step summed spread") as (block, s):
            @block.vector
            def _(dve):
                link = Link(dve, s["step"])
                v = nc.vector
                v.tensor_copy(identb[:, :], k.ident[:, :])
                for i in range(3):
                    last = v.tensor_reduce(size[:, i, 0:1], flat[i], AX.X, ALU.add, apply_absolute_value=True)
                last.then_inc(s["summed"], 1)
                dve.wait_ge(s["spread"], 1)
                link(v.tensor_scalar(size[:, :, 1], k.ps[:, 0, 0:3], 1.0 / (DIM * INNER), 1e-5, ALU.mult, ALU.max))
                link(v.reciprocal(size[:, :, 2], size[:, :, 1]))
                for i in range(3):
                    link(v.tensor_scalar(flat[i], flat[i], size[:, i, 2:3], MAGIC, ALU.mult, ALU.add))
                    link(v.tensor_scalar(flat[i], flat[i], MAGIC, 1.0, ALU.subtract, ALU.min))
                    v.tensor_scalar(ternary[i][:, :], flat[i], -1.0, None, ALU.max)

            @block.tensor
            def _(pe):
                pe.wait_ge(s["summed"], 1)
                nc.tensor.matmul(k.ps[:, 0, 0:3], k.ones[:, :], size[:, :, 0], start=True, stop=True).then_inc(s["spread"], 1)

        def round_rows(dve, link, source, width, factor):
            v = nc.vector
            rows_ = source[:, :, 0:width]
            link(v.tensor_reduce(peak[:, :], rows_, AX.X, ALU.max, apply_absolute_value=True))
            link(v.tensor_scalar(peak[:, :], peak[:, :], 1e-5, None, ALU.max))
            link(v.reciprocal(inverse[:, :], peak[:, :]))
            link(v.tensor_scalar(inverse[:, :], inverse[:, :], 127.0, None, ALU.mult))
            for j in range(GROUP):
                last = v.tensor_scalar(source[:, j, 0:width], source[:, j, 0:width], inverse[:, j:j + 1], MAGIC, ALU.mult, ALU.add)
            link(last)
            link(v.tensor_scalar(rounded[:, :, 0:width], rows_, MAGIC, 127.0, ALU.subtract, ALU.min))
            for i in range(3):
                last = v.tensor_scalar(factor[:, i, :], peak[:, :], 1.0 / 127.0, size[:, i, 1:2], ALU.mult, ALU.mult)
            link(last)

        def turn_jobs(width):
            return [(P, GT // 2, turned([rounded[:, j, sl(m)] for j in range(GROUP)], identb[:, :]), turns(m),
                     lambda nc, engine, bank, m=m: to_copy(roundedT[:, m, :])(nc, engine, bank.bitcast(BF16)))
                    for m in range(width // P)]

        def norm(g):
            part = Part("norm", "step measured rooted")

            def source(j):
                return k.x[:, bass.ds(g * GROUP + j, 1), :].rearrange("p o d -> p (o d)")

            @part.vector
            def _(dve, s):
                link = Link(dve, s["step"])
                row_stats(k, dve, link, source, s["measured"])
                yield
                dve.wait_ge(s["rooted"], 1)
                for j in range(GROUP):
                    last = nc.vector.tensor_scalar(k.normed[:, j, :], source(j), k.moments[:, j, 0:1], k.rstd[:, j:j + 1],
                                                   ALU.subtract, ALU.mult)
                link(last)
                round_rows(dve, link, k.normed, DIM, factor)
                yield

            @part.scalar
            def _(act, s):
                row_rstd(k, act, s["measured"], s["rooted"])
                yield
            return part

        def group(g, more):
            gemm_phase(k, "turn", turn_jobs(DIM))

            with phase(k, "up", "gated upped silued multiplied") as (block, s):
                units = [(j, c) for j in range(GROUP) for c in range(INNER // 512)]

                @block.tensor
                def _(pe):
                    for m, (j, c) in enumerate(units):
                        if m >= 4:
                            pe.wait_ge(s["silued"], m - 3)
                            pe.wait_ge(s["multiplied"], m - 3)
                        for i, sem in enumerate((s["gated"], s["upped"])):
                            for kt in range(KD):
                                last = nc.tensor.matmul(k.ps[:, 4 * i + m % 4, :], roundedT[:, kt, sl(j)],
                                                        ternary[i][:, kt * INNER + c * 512:kt * INNER + (c + 1) * 512],
                                                        start=kt == 0, stop=kt == KD - 1)
                            last.then_inc(sem, 1)

                @block.scalar
                def _(act):
                    for m, (j, c) in enumerate(units):
                        act.wait_ge(s["gated"], m + 1)
                        nc.scalar.activation(gate[:, j, sl(c, 512)], k.ps[:, m % 4, :], ACT.Silu,
                                             scale=factor[:, 0, j:j + 1]).then_inc(s["silued"], 1)

                @block.vector
                def _(dve):
                    for m, (j, c) in enumerate(units):
                        dve.wait_ge(s["upped"], m + 1)
                        dve.wait_ge(s["silued"], m + 1)
                        nc.vector.scalar_tensor_tensor(rows[:, j, sl(c, 512)], k.ps[:, 4 + m % 4, :], factor[:, 1, j:j + 1],
                                                       gate[:, j, sl(c, 512)], ALU.mult, ALU.mult).then_inc(s["multiplied"], 1)

            with phase(k, "round", "step") as (block, s):
                @block.vector
                def _(dve):
                    round_rows(dve, Link(dve, s["step"]), rows, INNER, down_factor)
            gemm_phase(k, "turn", turn_jobs(INNER))

            jobs = []
            for j in range(GROUP):
                x = k.x[:, bass.ds(g * GROUP + j, 1), :]
                jobs.append((P, DIM, products([(roundedT[:, m, sl(j)], ternary[2][:, sl(m, DIM)]) for m in range(M)]), "dve",
                             lambda nc, engine, bank, x=x, j=j: nc.vector.scalar_tensor_tensor(
                                 x, bank.rearrange("p (o d) -> p o d", o=1), down_factor[:, 2, j:j + 1], x, ALU.mult, ALU.add)))
            side_by_side(k, (gemm_part(k, "down", jobs), 1), *([(norm(g + 1), 1)] if more else []))
            empty_phase(k)

        side_by_side(k, (norm(0), 1))
        each_group(k, group)



def l2_attn(k):
    nc = k.nc
    INNER, STATE, HEADS, WIDTH, TAPS = 512, 128, 8, 64, 4
    M, CH = INNER // P, (INNER + 2 * STATE) // P
    COLS = 2 * INNER + 2 * STATE + HEADS
    LONG = SEQ + TAPS - 1
    n = "L2_attn_"
    ways = "fb"
    with ExitStack() as stack:
        in_w = {d: weights(k, stack, f"{n}{d}_in_w", KD, COLS) for d in ways}
        folded = {d: sb(k, stack, f"folded_{d}", [P, M, DIM]) for d in ways}
        small = {}
        loads = []
        for d in ways:
            loads += in_w[d][1]
            for name, shape in (("conv_w", [P, CH, TAPS]), ("conv_b", [P, CH]), ("A", [P, HEADS]), ("D", [P, HEADS]),
                                ("dt_bias", [1, HEADS]), ("mask", [P, P])):
                small[d, name] = sb(k, stack, f"{name}_{d}", shape)
                loads.append((small[d, name][tuple(slice(None) for _ in shape)], k.w[f"{n}{d}_{name}"]))
        norm_w, a = bias_columns(k, stack, n + "norm_w", KD)
        out_b, b = bias_row(k, stack, n + "out_b", DIM)
        select32 = sb(k, stack, "select32", [3 * HEADS, HEADS, P])
        select, ident = sb(k, stack, "select", [3 * HEADS, HEADS, P], BF16), sb(k, stack, "ident", [P, P], BF16)
        loads += a + b + [(select32[:, :, :], k.w[n + "select"])]
        with ExitStack() as inner:
            out_w = {d: weights(k, inner, f"{n}{d}_out_w", KD, INNER) for d in ways}
            block_w = {d: weights(k, inner, f"{n}{d}_block_w", KD, DIM) for d in ways}
            gnorm = {d: bias_columns(k, inner, f"{n}{d}_gnorm_w", M) for d in ways}
            for d in ways:
                loads += out_w[d][1] + block_w[d][1] + gnorm[d][1]
            load_phase(k, loads)

            def to_scaled(dst, scale):
                return lambda nc, engine, bank: nc.vector.tensor_scalar(dst, bank, scale, None, ALU.mult)
            gemm_phase(k, "fold", [(P, DIM, products([(out_w[d][0][:, kt, sl(m)], block_w[d][0][:, kt, :]) for kt in range(KD)]),
                                    "dve", to_scaled(folded[d][:, m, :], gnorm[d][0][:, m:m + 1])) for d in ways for m in range(M)])

        around = {d: sb(k, stack, f"around_{d}", [P, CH, GROUP, LONG]) for d in ways}
        conved = sb(k, stack, "conved", [P, CH, GT])
        gate = {d: sb(k, stack, f"gate_{d}", [P, GROUP, INNER]) for d in ways}
        raw = {d: sb(k, stack, f"raw_{d}", [P, GROUP, HEADS]) for d in ways}
        dt, decay, e, u, miss, late, total = (sb(k, stack, m, [P, GROUP, HEADS])
                                              for m in ("dt", "decay", "e", "u", "miss", "late", "total"))
        scale = sb(k, stack, "scale", [P, GROUP])
        left = sb(k, stack, "left", [P, GROUP, HEADS])
        thirds = sb(k, stack, "thirds", [P, GROUP, 3, HEADS], BF16)
        thirdsT = sb(k, stack, "thirdsT", [3 * HEADS, GT], BF16)
        pairs = sb(k, stack, "pairs", [P, GROUP, P])
        inputs, skipped = sb(k, stack, "inputs", [P, GROUP, INNER]), sb(k, stack, "skipped", [P, GROUP, INNER])
        LB = 4
        lasting = sb(k, stack, "lasting", [P, LB, GROUP, P])
        yT = {d: sb(k, stack, f"yT_{d}", [P, M, GT]) for d in ways}
        with phase(k, "rates", "exped") as (block, s):
            @block.scalar
            def _(act):
                for d in ways:
                    last = nc.scalar.activation(small[d, "A"][:, :], small[d, "A"][:, :], ACT.Exp)
                last.then_inc(s["exped"], 1)

            @block.vector
            def _(dve):
                nc.vector.tensor_copy(select[:, :, :], select32[:, :, :])
                nc.vector.tensor_copy(ident[:, :], k.ident[:, :])
                for d in ways:
                    nc.vector.memset(around[d][:, :, :, :], 0.0)
                dve.wait_ge(s["exped"], 1)
                for d in ways:
                    nc.vector.tensor_scalar(small[d, "A"][:, :], small[d, "A"][:, :], -1.0, None, ALU.mult)

        def norm(g):
            part = Part("norm", "step measured rooted squared rooted2 normed turned")
            x4 = k.x[:, bass.ds(g * GROUP, GROUP), :]

            def source(j):
                return k.x[:, bass.ds(g * GROUP + j, 1), :].rearrange("p o d -> p (o d)")

            @part.vector
            def _(dve, s):
                link = Link(dve, s["step"])
                row_stats(k, dve, link, source, s["measured"])
                yield
                dve.wait_ge(s["rooted"], 1)
                for j in range(GROUP):
                    last = nc.vector.tensor_scalar(k.normed[:, j, :], source(j), k.moments[:, j, 0:1], k.rstd[:, j:j + 1],
                                                   ALU.subtract, ALU.mult)
                link(last)
                nc.vector.tensor_tensor(x4, x4, k.normed[:, :, :], ALU.add)
                for j in range(GROUP):
                    scratch = conved[:, M + j // 2, sl(j % 2, DIM)]
                    last = nc.vector.tensor_tensor_reduce(scratch, k.normed[:, j, :], k.normed[:, j, :], 1.0, 0.0,
                                                          ALU.mult, ALU.add, k.rstd[:, j:j + 1])
                link(last)
                link(nc.vector.tensor_scalar(k.rstd[:, :], k.rstd[:, :], 1.0 / DIM, LN_EPS, ALU.mult, ALU.add))
                nc.vector.reciprocal(k.rstd[:, :], k.rstd[:, :]).then_inc(s["squared"], 1)
                yield
                dve.wait_ge(s["rooted2"], 1)
                for j in range(GROUP):
                    nc.vector.tensor_scalar(k.normed[:, j, :], k.normed[:, j, :], k.rstd[:, j:j + 1], None, ALU.mult).then_inc(s["normed"], 1)
                yield
                yield
                dve.wait_ge(s["turned"], GROUP)
                nc.vector.tensor_scalar(k.xT[:, 1, :], k.ps[:, 1, :], norm_w[:, 1:2], None, ALU.mult)
                yield

            @part.scalar
            def _(act, s):
                row_rstd(k, act, s["measured"], s["rooted"])
                yield
                row_rstd(k, act, s["squared"], s["rooted2"])
                yield
                yield
                yield
                act.wait_ge(s["turned"], GROUP)
                nc.scalar.activation(k.xT[:, 0, :], k.ps[:, 0, :], ACT.Copy, scale=norm_w[:, 0:1])
                yield

            @part.tensor
            def _(pe, s):
                yield
                yield
                yield
                for j in range(GROUP):
                    pe.wait_ge(s["normed"], j + 1)
                    for kt in range(KD):
                        last = nc.tensor.transpose(k.ps[:, kt, sl(j)], k.normed[:, j, sl(kt)], k.ident[:, :])
                    last.then_inc(s["turned"], 1)
                yield
            return part

        def enter(d, banks=range(8)):
            w = in_w[d][0]
            lead = TAPS - 1 if d == "f" else 0

            def to_silu(dst):
                return lambda nc, engine, bank: nc.scalar.activation(dst, bank, ACT.Silu)

            def to_around(m):
                return to_copy4(around[d][:, m, :, lead:lead + SEQ])

            def to_copy4(dst):
                return lambda nc, engine, bank: to_copy(dst)(nc, engine, bank.rearrange("p (j t) -> p j t", j=GROUP))
            jobs = []
            for j in range(GROUP):
                jobs.append((P, INNER, token_pairs(k, k.xT, [P] * KD, j, w, slice(0, INNER)), "act", to_silu(gate[d][:, j, :])))
                pairs_dt = [(k.xT[:, kt, sl(j)], w[:, kt, COLS - HEADS:COLS]) for kt in range(KD)]
                pairs_dt.append((k.ones[0:1, 0:P], small[d, "dt_bias"][0:1, :]))
                jobs.append((P, HEADS, products(pairs_dt), "dve", to_copy(raw[d][:, j, :])))
            for m in range(CH):
                jobs.append((P, GT, products([(w[:, kt, INNER + m * P:INNER + (m + 1) * P], k.xT[:, kt, :]) for kt in range(KD)]),
                             turns(m), to_around(m)))
            return gemm_part(k, "in", jobs, banks)

        def convolve(d):
            part = Part("conv", "step started sized exped plussed logged conved")

            def tapped(m, tap):
                at = tap if d == "f" else TAPS - 1 - tap
                return around[d][:, m, :, at:at + SEQ], small[d, "conv_w"][:, m, tap:tap + 1]

            @part.vector
            def _(dve, s):
                link = Link(dve, s["step"])
                v = nc.vector
                for m in range(CH):
                    out = conved[:, m, :].rearrange("p (j t) -> p j t", j=GROUP)
                    dve.wait_ge(s["started"], m + 1)
                    for tap in range(1, TAPS):
                        last = v.scalar_tensor_tensor(out, *tapped(m, tap), out, ALU.mult, ALU.add)
                        if tap < TAPS - 1:
                            link(last)
                    last.then_inc(s["conved"], 1)
                    yield
                dve.wait_ge(s["exped"], 1)
                v.tensor_scalar(u[:, :, :], e[:, :, :], 1.0, None, ALU.add).then_inc(s["plussed"], 1)
                dve.wait_ge(s["plussed"], 1)
                link(v.tensor_scalar(late[:, :, :], u[:, :, :], 1.0, None, ALU.subtract))
                link(v.tensor_scalar(miss[:, :, :], late[:, :, :], 0.0, None, ALU.is_equal))
                link(v.tensor_tensor(late[:, :, :], late[:, :, :], miss[:, :, :], ALU.add))
                link(v.reciprocal(late[:, :, :], late[:, :, :]))
                link(v.tensor_tensor(late[:, :, :], late[:, :, :], e[:, :, :], ALU.mult))
                link(v.tensor_tensor(miss[:, :, :], miss[:, :, :], e[:, :, :], ALU.mult))
                yield
                dve.wait_ge(s["logged"], 1)
                link(v.tensor_tensor(u[:, :, :], u[:, :, :], late[:, :, :], ALU.mult))
                link(v.tensor_tensor(u[:, :, :], u[:, :, :], miss[:, :, :], ALU.add))
                link(v.scalar_tensor_tensor(dt[:, :, :], raw[d][:, :, :], 0.0, u[:, :, :], ALU.max, ALU.add))
                v.tensor_tensor(decay[:, :, :], dt[:, :, :], small[d, "A"][:, :].unsqueeze(1).broadcast_to([P, GROUP, HEADS]),
                                ALU.mult)
                yield

            @part.scalar
            def _(act, s):
                for m in range(CH):
                    window, weight = tapped(m, 0)
                    nc.scalar.activation(conved[:, m, :].rearrange("p (j t) -> p j t", j=GROUP), window, ACT.Copy,
                                         scale=weight).then_inc(s["started"], 1)
                nc.scalar.activation(e[:, :, :], raw[d][:, :, :], ACT.Abs).then_inc(s["sized"], 1)
                act.wait_ge(s["sized"], 1)
                nc.scalar.activation(e[:, :, :], e[:, :, :], ACT.Exp, scale=-1.0).then_inc(s["exped"], 1)
                for m in range(CH):
                    yield
                    if m % 3 == 2:
                        for ready in range(m - 2, m + 1):
                            act.wait_ge(s["conved"], ready + 1)
                            nc.scalar.activation(conved[:, ready, :], conved[:, ready, :], ACT.Silu,
                                                 bias=small[d, "conv_b"][:, ready:ready + 1])
                act.wait_ge(s["plussed"], 1)
                act.wait_ge(s["step"], CH * (TAPS - 2) + 1)
                nc.scalar.activation(u[:, :, :], u[:, :, :], ACT.Ln).then_inc(s["logged"], 1)
                yield
            return part

        def sums(d):
            part = Part("sum", "summed step split turned paired")

            def turned_thirds(rows):
                return k.ps[0:rows, 1, 0:GT // 2].bitcast(BF16)

            @part.tensor
            def _(pe, s):
                nc.tensor.matmul(k.ps[:, 0, 0:GROUP * HEADS], small[d, "mask"][:, :],
                                 decay[:, :, :].rearrange("p j h -> p (j h)"), start=True, stop=True).then_inc(s["summed"], 1)
                for j in range(GROUP):
                    last = nc.tensor.matmul(k.ps[:, 2, sl(j)], conved[:, M, sl(j)], conved[:, M + 1, sl(j)], start=True, stop=True)
                last.then_inc(s["paired"], 1)
                yield
                pe.wait_ge(s["split"], 1)
                for j in range(GROUP):
                    last = nc.tensor.transpose(turned_thirds(3 * HEADS)[:, sl(j)], thirds[:, j, :, :].rearrange("p t h -> p (t h)"),
                                               ident[:, :])
                last.then_inc(s["turned"], 1)
                yield

            @part.vector
            def _(dve, s):
                dve.wait_ge(s["summed"], 1)
                link = Link(dve, s["step"])
                link(nc.vector.tensor_copy(total[:, :, :].rearrange("p j h -> p (j h)"), k.ps[:, 0, 0:GROUP * HEADS]))
                link(nc.vector.tensor_copy(thirds[:, :, 0, :], total[:, :, :]))
                link(nc.vector.tensor_tensor(left[:, :, :], total[:, :, :], thirds[:, :, 0, :], ALU.subtract))
                link(nc.vector.tensor_copy(thirds[:, :, 1, :], left[:, :, :]))
                link(nc.vector.tensor_tensor(left[:, :, :], left[:, :, :], thirds[:, :, 1, :], ALU.subtract))
                nc.vector.tensor_copy(thirds[:, :, 2, :], left[:, :, :]).then_inc(s["split"], 1)
                yield
                dve.wait_ge(s["paired"], 1)
                nc.vector.tensor_tensor(pairs[:, :, :], k.ps[:, 2, :].rearrange("p (j t) -> p j t", j=GROUP),
                                        small[d, "mask"][:, :].unsqueeze(1).broadcast_to([P, GROUP, P]), ALU.mult)
                yield

            @part.scalar
            def _(act, s):
                yield
                act.wait_ge(s["turned"], 1)
                nc.scalar.activation(thirdsT[:, :], turned_thirds(3 * HEADS), ACT.Copy)
                yield
            return part

        def turn_inputs(d):
            def to_inputs(j):
                def evacuate(nc, engine, bank):
                    heads = bank.rearrange("p (h d) -> p h d", d=WIDTH)
                    nc.vector.tensor_tensor(inputs[:, j, :].rearrange("p (h d) -> p h d", d=WIDTH), heads,
                                            dt[:, j, :].unsqueeze(2).broadcast_to([P, HEADS, WIDTH]), ALU.mult)
                    return nc.vector.tensor_tensor(skipped[:, j, :].rearrange("p (h d) -> p h d", d=WIDTH), heads,
                                                   small[d, "D"][:, :].unsqueeze(2).broadcast_to([P, HEADS, WIDTH]), ALU.mult)
                return evacuate
            return gemm_part(k, "turn", [(P, INNER, turned([conved[:, m, sl(j)] for m in range(M)], k.ident[:, :]), "dve", to_inputs(j))
                                         for j in range(GROUP)], range(4, 8))

        def scan(d, SB):
            part = Part("scan", "spread read capped exped weighted mixed added")

            @part.tensor
            def _(pe, s):
                def mix(h):
                    pe.wait_ge(s["weighted"], h + 1)
                    for j in range(GROUP):
                        last = nc.tensor.matmul(k.ps[:, 4 + j, sl(h, WIDTH)], lasting[:, h % LB, j, :],
                                                inputs[:, j, sl(h, WIDTH)], start=True, stop=True)
                    last.then_inc(s["mixed"], 1)

                for h in range(HEADS + 3):
                    if h < HEADS:
                        if h >= SB:
                            pe.wait_ge(s["read"], h - SB + 1)
                        nc.tensor.matmul(k.ps[:, h % SB, :], select[:, h, :], thirdsT[:, :], start=True, stop=True).then_inc(s["spread"], 1)
                    if h >= 3:
                        mix(h - 3)
                    yield

            @part.vector
            def _(dve, s):
                for h in range(HEADS + 2):
                    if h < HEADS:
                        dve.wait_ge(s["spread"], h + 1)
                        if h >= LB:
                            dve.wait_ge(s["mixed"], h - LB + 1)
                        nc.vector.tensor_tensor(lasting[:, h % LB, :, :], k.ps[:, h % SB, :].rearrange("p (j t) -> p j t", j=GROUP),
                                                total[:, :, h].unsqueeze(2).broadcast_to([P, GROUP, P]), ALU.subtract).then_inc(s["read"], 1)
                    if h >= 2:
                        dve.wait_ge(s["exped"], h - 1)
                        nc.vector.tensor_tensor(lasting[:, (h - 2) % LB, :, :], lasting[:, (h - 2) % LB, :, :], pairs[:, :, :],
                                                ALU.mult).then_inc(s["weighted"], 1)
                    yield
                yield
                dve.wait_ge(s["mixed"], HEADS)
                for j in range(GROUP):
                    nc.vector.tensor_tensor(skipped[:, j, :], k.ps[:, 4 + j, :], skipped[:, j, :], ALU.add).then_inc(s["added"], 1)
                yield

            @part.gpsimd
            def _(pool, s):
                for h in range(HEADS):
                    pool.wait_ge(s["read"], h + 1)
                    nc.gpsimd.tensor_scalar(lasting[:, h % LB, :, :], lasting[:, h % LB, :, :], 0.0, None, ALU.min).then_inc(s["capped"], 1)
                    yield
                for j in range(GROUP):
                    pool.wait_ge(s["added"], j + 1)
                    nc.gpsimd.tensor_tensor(gate[d][:, j, :], gate[d][:, j, :], skipped[:, j, :], ALU.mult)
                yield

            @part.scalar
            def _(act, s):
                for h in range(HEADS):
                    act.wait_ge(s["capped"], h + 1)
                    nc.scalar.activation(lasting[:, h % LB, :, :], lasting[:, h % LB, :, :], ACT.Exp).then_inc(s["exped"], 1)
                    yield
            return part

        def finish(d):
            part = Part("finish", "step squared rooted normed turned act_took dve_took")
            y = gate[d]

            @part.vector
            def _(dve, s):
                link = Link(dve, s["step"])
                v = nc.vector
                for j in range(GROUP):
                    last = v.tensor_tensor_reduce(conved[:, j, :], y[:, j, :], y[:, j, :], 1.0, 0.0, ALU.mult, ALU.add,
                                                  scale[:, j:j + 1])
                link(last)
                link(v.tensor_scalar(scale[:, :], scale[:, :], 1.0 / INNER, LN_EPS, ALU.mult, ALU.add))
                v.reciprocal(scale[:, :], scale[:, :]).then_inc(s["squared"], 1)
                yield
                dve.wait_ge(s["rooted"], 1)
                for j in range(GROUP):
                    last = v.tensor_scalar(y[:, j, :], y[:, j, :], scale[:, j:j + 1], None, ALU.mult)
                last.then_inc(s["normed"], 1)
                yield
                yield
                yield
                for m in range(1, M, 2):
                    dve.wait_ge(s["turned"], m + 1)
                    nc.vector.tensor_copy(yT[d][:, m, :], k.ps[:, 2 + m % 2, :]).then_inc(s["dve_took"], 1)
                    yield

            @part.scalar
            def _(act, s):
                act.wait_ge(s["squared"], 1)
                nc.scalar.activation(scale[:, :], scale[:, :], ACT.Sqrt).then_inc(s["rooted"], 1)
                yield
                yield
                yield
                yield
                for m in range(0, M, 2):
                    act.wait_ge(s["turned"], m + 1)
                    nc.scalar.activation(yT[d][:, m, :], k.ps[:, 2 + m % 2, :], ACT.Copy).then_inc(s["act_took"], 1)
                    yield

            @part.tensor
            def _(pe, s):
                yield
                yield
                pe.wait_ge(s["normed"], 1)
                for m in range(M):
                    if m >= 2:
                        pe.wait_ge(s["dve_took" if m % 2 else "act_took"], m // 2)
                    for j in range(GROUP):
                        last = nc.tensor.transpose(k.ps[:, 2 + m % 2, sl(j)], y[:, j, sl(m)], k.ident[:, :])
                    last.then_inc(s["turned"], 1)
                    if m % 2:
                        yield
                        yield
            return part

        def leave(g):
            jobs = []
            for j in range(GROUP):
                x = k.x[:, bass.ds(g * GROUP + j, 1), :]
                both = [(yT[d][:, m, sl(j)], folded[d][:, m, :]) for d in ways for m in range(M)]
                both.append((k.ones[0:1, 0:P], out_b[0:1, :]))
                jobs.append((P, DIM, products(both), "dve",
                             lambda nc, engine, bank, x=x: nc.vector.tensor_tensor(x, bank.rearrange("p (o d) -> p o d", o=1), x, ALU.add)))
            return gemm_part(k, "out", jobs)

        def group(g, last=False):
            side_by_side(k, (enter("f"), 1))
            side_by_side(k, (convolve("f"), 1), (enter("b"), 2))
            side_by_side(k, (sums("f"), 1), (turn_inputs("f"), 2))
            side_by_side(k, (scan("f", 4), 1), (convolve("b"), 1))
            side_by_side(k, (sums("b"), 1), (turn_inputs("b"), 2))
            side_by_side(k, (scan("b", 2), 1), (finish("f"), 1))
            side_by_side(k, (finish("b"), 1), *([] if last else [(norm(g + 1), 1)]))
            side_by_side(k, (leave(g), 1))

        side_by_side(k, (norm(0), 1))
        with nc.Fori(0, GROUPS - 1) as g:
            group(g)
        group(GROUPS - 1, last=True)


def l3_attn(k):
    nc = k.nc
    H, D = 16, 16
    QT = TOKENS // P
    Q_PARTS, K_PARTS = (0, 0, 1, 0, 2, 1), (0, 1, 0, 2, 0, 1)
    ROWS = len(Q_PARTS) * D
    DEEP = ROWS + 3
    VW = D + 1
    CHUNK = 512
    n = "L3_attn_"
    parts_dram = nc.dram_tensor("parts", (6 * DIM, TOKENS), BF16, kind="Internal").ap()
    with ExitStack() as stack:
        wp, a = weights(k, stack, n + "proj_w", KD, DIM)
        wq, b = weights(k, stack, n + "wq", KD, P)
        wk, c = weights(k, stack, n + "wk", KD, P)
        bp, d = bias_columns(k, stack, n + "proj_b", KD)
        bp_row, e = bias_row(k, stack, n + "proj_b_row", DIM)
        values = sb(k, stack, "values", [P, QT, H, VW])
        load_phase(k, a + b + c + d + e)
        with ExitStack() as inner:
            flat = sb(k, inner, "flat", [P, KD, GT])
            whole, left = sb(k, inner, "whole", [P, 2 * KD, GT]), sb(k, inner, "left", [P, 2 * KD, GT])
            parts = sb(k, inner, "parts", [P, 3, 2 * KD, GT], BF16)
            with phase(k, "fill", "none") as (block, s):
                @block.vector
                def _(dve):
                    nc.vector.memset(values[:, :, :, :], 1.0)
            with nc.Fori(0, GROUPS) as g:
                norm_phase(k, g, lambda kt: k.xT[:, kt, :])

                def to_values(j):
                    def evacuate(nc, engine, bank):
                        return nc.vector.tensor_copy(values[:, bass.ds(g * GROUP + j, 1), :, 0:D],
                                                     bank.rearrange("p (o h d) -> p o h d", o=1, d=D))
                    return evacuate
                jobs = feature_jobs(flat, wp, k.xT, [P] * KD, DIM, bp)
                jobs += [(P, DIM, token_pairs(k, k.xT, [P] * KD, j, wp, slice(0, DIM), bp_row), "dve", to_values(j))
                         for j in range(GROUP)]
                gemm_phase(k, "flat", jobs)
                gemm_phase(k, "qk", [(P, GT, products([(w[:, m, :], flat[:, m, :])]), turns(m), to_copy(whole[:, KD * i + m, :]))
                                     for i, w in enumerate((wq, wk)) for m in range(KD)])
                with phase(k, "split", "step stored") as (block, s):
                    @block.vector
                    def _(dve):
                        link = Link(dve, s["step"])
                        v = nc.vector
                        link(v.tensor_copy(parts[:, 0], whole[:, :, :]))
                        link(v.tensor_tensor(left[:, :, :], whole[:, :, :], parts[:, 0], ALU.subtract))
                        link(v.tensor_copy(parts[:, 1], left[:, :, :]))
                        link(v.tensor_tensor(parts[:, 2], left[:, :, :], parts[:, 1], ALU.subtract))

                    @block.sync
                    def _(sp):
                        for part, ready in enumerate((1, 3, 4)):
                            sp.wait_ge(s["step"], ready)
                            for i in range(2 * KD):
                                row0 = ((i // KD) * 3 + part) * DIM + (i % KD) * P
                                sp.dma_start(parts_dram[row0:row0 + P, bass.ds(g * GT, GT)], parts[:, part, i, :]).then_inc(s["stored"], 16)
                        sp.wait_ge(s["stored"], 16 * 3 * 2 * KD)

        queries = [sb(k, stack, f"queries{i}", [P, TOKENS], BF16) for i in range(3)]
        keys = [sb(k, stack, f"keys{i}", [P, TOKENS], BF16) for i in range(3)]
        attn = sb(k, stack, "attn", [P, 2, TOKENS])
        head_values = sb(k, stack, "head_values", [P, QT, PAD])
        peaks = sb(k, stack, "peaks", [P, QT, TOKENS // CHUNK])
        minus, left = sb(k, stack, "minus", [P, QT]), sb(k, stack, "left", [P, QT])
        minus_b = sb(k, stack, "minus_b", [P, QT], BF16)
        minus_parts = sb(k, stack, "minus_parts", [P, 3, QT])
        minus_rows = sb(k, stack, "minus_rows", [3 * QT, P], BF16)
        output = sb(k, stack, "output", [P, CHUNK])
        share, fresh = sb(k, stack, "share", [P, QT]), sb(k, stack, "fresh", [P, 4, 4, D])

        def load_head(sp, loaded, i, head):
            for side, (dst, order) in enumerate(((queries[i], Q_PARTS), (keys[i], K_PARTS))):
                for block_, part in enumerate(order):
                    sp.dma_start(dst[sl(block_, D), :], parts_dram[bass.ds(head * D + (side * 3 + part) * DIM, D), :]).then_inc(loaded, 16)

        with phase(k, "start", "loaded") as (block, s):
            @block.vector
            def _(dve):
                nc.vector.memset(head_values[:, :, :], 0.0)
                for i in range(3):
                    nc.vector.memset(keys[i][ROWS:P, :], 1.0)

            @block.sync
            def _(sp):
                for i in range(2):
                    load_head(sp, s["loaded"], i, i)
                sp.wait_ge(s["loaded"], 16 * 24)

        PROBES = QT * TOKENS // CHUNK
        PER_STEP = 5

        def head_phase(here, ahead, later, head, before=None):
            with phase(k, "head", "step loaded scored exped mixed probed maxed parted turned rowed moved fetched unturned emptied") as (block, s):
                @block.sync
                def _(sp):
                    if later is not None:
                        load_head(sp, s["loaded"], *later)
                        sp.wait_ge(s["loaded"], 16 * 12)
                    if ahead is not None:
                        sp.wait_ge(s["rowed"], 1)
                        for part in range(3):
                            sp.dma_start(queries[ahead][ROWS + part:ROWS + part + 1, :].rearrange("o (t q) -> o t q", q=P),
                                         minus_rows[sl(part, QT), :]).then_inc(s["moved"], 16)
                        sp.wait_ge(s["moved"], 48)

                @block.gpsimd
                def _(pool):
                    if here is not None:
                        nc.gpsimd.tensor_copy(head_values[:, :, 0:VW].unsqueeze(2), values[:, :, bass.ds(head, 1), :]).then_inc(s["fetched"], 1)

                @block.tensor
                def _(pe):
                    def score(kt, half):
                        if here is None:
                            return
                        if kt >= 1:
                            pe.wait_ge(s["exped"], 2 * (kt - 1) + half + 1)
                        for c in range(2 * half, 2 * half + 2):
                            last = nc.tensor.matmul(k.ps[:, c, :], keys[here][0:DEEP, sl(kt)], queries[here][0:DEEP, sl(c, CHUNK)],
                                                    start=True, stop=True)
                        last.then_inc(s["scored"], 1)

                    def probe(u):
                        if ahead is None or u >= PROBES:
                            return
                        if u == 2 and before is not None:
                            pe.wait_ge(s["emptied"], 1)
                        if u >= 3:
                            pe.wait_ge(s["maxed"], u - 2)
                        nc.tensor.matmul(k.ps[:, 5 + u % 3, :], queries[ahead][0:ROWS, sl(u // 4)], keys[ahead][0:ROWS, sl(u % 4, CHUNK)],
                                         start=True, stop=True).then_inc(s["probed"], 1)

                    def mix(kt):
                        if here is None or kt < 0:
                            return
                        pe.wait_ge(s["exped"], 2 * kt + 2)
                        if kt == 0:
                            pe.wait_ge(s["fetched"], 1)
                        for c in range(4):
                            last = nc.tensor.matmul(k.ps[sl(c, PAD), 4, :], head_values[:, kt, :], attn[:, kt % 2, sl(c, CHUNK)],
                                                    start=kt == 0, stop=kt == QT - 1)
                        last.then_inc(s["mixed"], 1)

                    if before is not None:
                        for b_ in range(4):
                            last = nc.tensor.transpose(k.ps[:, 7, sl(b_)], output[:, sl(b_)], k.ident[:, :])
                        last.then_inc(s["unturned"], 1)
                    for kt in range(QT):
                        u = PER_STEP * kt
                        score(kt, 0)
                        probe(u)
                        probe(u + 1)
                        score(kt, 1)
                        probe(u + 2)
                        probe(u + 3)
                        mix(kt - 1)
                        probe(u + 4)
                    if ahead is not None:
                        pe.wait_ge(s["parted"], 1)
                        nc.tensor.transpose(k.ps[0:3 * QT, 7, 0:P], minus_parts[:, :, :].rearrange("p a b -> p (a b)"),
                                            k.ident[:, :]).then_inc(s["turned"], 1)
                    mix(QT - 1)

                @block.scalar
                def _(act):
                    if here is not None:
                        for kt in range(QT):
                            for half in range(2):
                                act.wait_ge(s["scored"], 2 * kt + half + 1)
                                if kt >= 2:
                                    act.wait_ge(s["mixed"], kt - 1)
                                nc.scalar.activation(attn[:, kt % 2, sl(half, 2 * CHUNK)].rearrange("p (c q) -> p c q", c=2),
                                                     k.ps[:, 2 * half:2 * half + 2, :], ACT.Exp, scale=1.0 / 16.0).then_inc(s["exped"], 1)
                    if ahead is not None:
                        act.wait_ge(s["turned"], 1)
                        nc.scalar.activation(minus_rows[:, :], k.ps[0:3 * QT, 7, 0:P], ACT.Copy).then_inc(s["rowed"], 1)
                    if here is not None:
                        if before is not None:
                            act.wait_ge(s["unturned"], 1)
                        act.wait_ge(s["mixed"], QT)
                        nc.scalar.activation(output[:, :], k.ps[:, 4, :], ACT.Copy)

                @block.vector
                def _(dve):
                    link = Link(dve, s["step"])
                    v = nc.vector
                    if before is not None:
                        dve.wait_ge(s["unturned"], 1)
                        turned_ = k.ps[:, 7, :].rearrange("p (b c w) -> p b c w", b=4, c=4)
                        share_ = share[:, :].rearrange("p (b c) -> p b c", b=4)
                        link(v.reciprocal(share_.unsqueeze(3), turned_[:, :, :, D:VW]))
                        v.tensor_tensor(fresh[:, :, :, :], turned_[:, :, :, 0:D], share_.unsqueeze(3).broadcast_to([P, 4, 4, D]),
                                        ALU.mult).then_inc(s["emptied"], 1)
                        dve.wait_ge(s["emptied"], 1)
                        for b_ in range(4):
                            x = k.x[:, :, bass.ds(before * D, D)].rearrange("p (c b) d -> p c b d", b=4)[:, :, b_, :]
                            v.tensor_tensor(x, x, fresh[:, b_, :, :], ALU.add)
                    if ahead is not None:
                        for u in range(PROBES):
                            dve.wait_ge(s["probed"], u + 1)
                            v.tensor_reduce(peaks[:, u // 4, u % 4:u % 4 + 1], k.ps[:, 5 + u % 3, :], AX.X, ALU.max).then_inc(s["maxed"], 1)
                        dve.wait_ge(s["maxed"], PROBES)
                        link(v.tensor_reduce(minus[:, :], peaks[:, :, :], AX.X, ALU.max))
                        link(v.tensor_scalar(minus[:, :], minus[:, :], -1.0, None, ALU.mult))
                        link(v.tensor_copy(minus_b[:, :], minus[:, :]))
                        link(v.tensor_copy(minus_parts[:, 0, :], minus_b[:, :]))
                        link(v.tensor_tensor(left[:, :], minus[:, :], minus_parts[:, 0, :], ALU.subtract))
                        link(v.tensor_copy(minus_b[:, :], left[:, :]))
                        link(v.tensor_copy(minus_parts[:, 1, :], minus_b[:, :]))
                        v.tensor_tensor(minus_parts[:, 2, :], left[:, :], minus_parts[:, 1, :], ALU.subtract).then_inc(s["parted"], 1)

        def one_head(m, h):
            head_phase(m, (m + 1) % 3, ((m + 2) % 3, h + 2), h, h - 1)

        head_phase(None, 0, None, None)
        head_phase(0, 1, (2, 2), 0)
        with nc.Fori(0, 4) as i:
            for m in range(3):
                one_head((m + 1) % 3, 3 * i + m + 1)
            empty_phase(k)
        one_head(1, 13)
        head_phase(2, 0, None, 14, 13)
        head_phase(0, None, None, 15, 14)
        head_phase(None, None, None, None, 15)


def lay_out_rest(i, w):
    n = "L0_xattn_"
    w[n + "Wq"], w[n + "Wk"], w[n + "Wv"] = i[n + "Wq"], i[n + "Wk"], pad_heads(i[n + "Wv"], 1)
    w[n + "Wo"] = wo_order(pad_heads(i[n + "Wo"], 0), 16, PAD)
    w[n + "bv"] = row(pad_heads(i[n + "bv"], 0))
    for m in ("bq", "bk", "bo"):
        w[n + m] = row(i[n + m])
    for m in ("ln_gamma", "ln_beta"):
        w[n + m] = np.repeat(row(i[n + m]), P, axis=0)

    n = "L0_ffn_"
    w[n + "Wr"], w[n + "br"] = i[n + "Wr"], row(i[n + "br"])
    w[n + "bd"] = np.concatenate([i[n + "bd"], row(i[n + "bd_s"])])

    def expert_parts(name):
        return np.concatenate([i[n + name], i[n + name + "_s"][None]])

    def by_partition(a, tiles):
        return a.reshape(len(a), tiles, P, -1).transpose(0, 2, 1, 3).reshape(len(a), P, -1)
    packed = np.concatenate([by_partition(expert_parts("Wg"), 2), by_partition(expert_parts("Wu"), 2), expert_parts("Wd"),
                             expert_parts("bg")[:, :, None], expert_parts("bu")[:, :, None]], axis=2)
    w[n + "experts"] = packed.reshape(11, 3, P, -1).transpose(0, 2, 1, 3)

    n = "L2_ffn_"
    w[n + "Wg"] = i[n + "Wg"]
    w[n + "experts"] = np.concatenate([by_partition(i[n + "W1"], 2), by_partition(i[n + "W2"], 4)], axis=2)
    w["order"] = np.broadcast_to(np.arange(8, 0, -1, dtype=np.float32), (P, BATCH, 8))

    n = "L3_ffn_"
    for m in ("W_fc", "W_proj", "B_fc", "B_proj"):
        w[n + m] = i[n + m].T
    w[n + "A_fc"], w[n + "A_proj"] = i[n + "A_fc"], i[n + "A_proj"]
    w[n + "b_fc"], w[n + "b_proj"] = columns(i[n + "b_fc"]), row(i[n + "b_proj"])

    n = "L1_attn_"
    w[n + "W_q"], w[n + "W_k"] = pad_heads(i[n + "W_q"], 1), pad_heads(i[n + "W_k"], 1)
    w[n + "W_v"], w[n + "W_o"] = i[n + "W_v"], i[n + "W_o"]
    blocks, where = np.zeros((P, 8, P), np.float32), np.zeros((P, 8, P), np.float32)
    for h in range(16):
        at = PAD * (h % 4)
        blocks[at:at + 16, h // 2, sl(h % 2, 64)] = i[n + "centers"][h].T
        where[at:at + 16, h // 2, sl(h % 2, 64)] = 1
    w[n + "centers"], w[n + "where"] = blocks, where
    for m in ("log_scales", "amplitudes"):
        w[n + m] = columns(i[n + m].reshape(-1))

    n = "L1_ffn_"
    for m in ("w_gate", "w_up", "w_down"):
        w[n + m] = i[n + m].T

    n = "L2_attn_"
    w[n + "norm_w"], w[n + "out_b"] = columns(i[n + "norm_w"]), row(i[n + "out_b_blk"])
    w[n + "select"] = np.tile(np.repeat(np.eye(8, dtype=np.float32)[:, :, None], P, axis=2), (3, 1, 1))
    for number, d in enumerate("fb"):
        m = n + d + "_"
        w[m + "in_w"], w[m + "out_w"] = i[m + "in_w"].T, i[m + "out_w"]
        w[m + "block_w"] = i[n + "out_w_blk"][:, sl(number, DIM)].T
        w[m + "gnorm_w"], w[m + "conv_b"] = columns(i[m + "gnorm_w"]), columns(i[m + "conv_b"])
        w[m + "conv_w"] = i[m + "conv_w"].reshape(6, P, 4).transpose(1, 0, 2)
        w[m + "A"], w[m + "D"] = np.repeat(row(i[m + "A_log"]), P, axis=0), np.repeat(row(i[m + "D"]), P, axis=0)
        w[m + "dt_bias"] = row(i[m + "dt_bias"])
        w[m + "mask"] = np.tri(P, dtype=np.float32).T if d == "f" else np.tri(P, dtype=np.float32)

    n = "L3_attn_"
    w[n + "proj_w"] = i[n + "proj_w"].T
    w[n + "proj_b"], w[n + "proj_b_row"] = columns(i[n + "proj_b"]), row(i[n + "proj_b"])
    for m in ("wq", "wk"):
        blocks = np.zeros((2, P, P), np.float32)
        for h in range(16):
            blocks[h // 8, sl(h % 8, 16), sl(h % 8, 16)] = i[n + m][h]
        w[n + m] = blocks.reshape(2 * P, P)


def layers(k):
    l0_attn(k)
    l0_xattn(k)
    l0_ffn(k)
    l1_attn(k)
    cross_attention(k, "L1_xattn", 16, "L1_xattn_Wo", "L1_xattn_bo")
    l1_ffn(k)
    l2_attn(k)
    cross_attention(k, "L2_xattn", 8, "L2_xattn_Wout", "L2_xattn_bout")
    l2_ffn(k)
    l3_attn(k)
    cross_attention(k, "L3_xattn", 8, "L3_xattn_Wo", "L3_xattn_bo")
    l3_ffn(k)


def build(nc, w, out):
    with ExitStack() as stack:
        k = Core(nc, w)
        free = sorted(nc.free_semaphores)[-2 * SIGNALS:]
        k.banks = (free[:SIGNALS], free[SIGNALS:])
        k.ps = stack.enter_context(nc.psum_tensor("ps", [P, 8, 512], F32))
        k.x = sb(k, stack, "x", [P, BATCH, DIM])
        k.ctxT = sb(k, stack, "ctxT", [P, 2, TOKENS])
        k.ctxG = sb(k, stack, "ctxG", [P, 2, GT])
        k.xT = sb(k, stack, "xT", [P, KD, GT])
        k.normed = sb(k, stack, "normed", [P, GROUP, DIM])
        k.ident = sb(k, stack, "ident", [P, P])
        k.ones = sb(k, stack, "ones", [P, P])
        k.stats = sb(k, stack, "stats", [P, GROUP, 6])
        k.moments = sb(k, stack, "moments", [P, GROUP, 2])
        k.rstd = sb(k, stack, "rstd", [P, GROUP])
        load_phase(k, [(k.x[:, :, :], w["x"].rearrange("b t d -> t b d")), (k.ident[:, :], w["ident"]),
                       (k.ones[:, :], w["ones"]),
                       (k.ctxT[:, 0, :], w["ctxT"][0:P, :]), (k.ctxT[0:CTX - P, 1, :], w["ctxT"][P:CTX, :])])
        layers(k)
        with phase(k, "store", "stored") as (block, s):
            @block.sync
            def _(sp):
                sp.dma_start(out.rearrange("b t d -> t b d"), k.x[:, :, :]).then_inc(s["stored"], 16)
                sp.wait_ge(s["stored"], 16)


def pad_heads(a, axis):
    a = np.moveaxis(a, axis, -1)
    b = np.zeros(a.shape[:-1] + (16, PAD), a.dtype)
    b[..., :16] = a.reshape(a.shape[:-1] + (16, 16))
    return np.ascontiguousarray(np.moveaxis(b.reshape(a.shape[:-1] + (16 * PAD,)), -1, axis))


def columns(b):
    return np.ascontiguousarray(b.reshape(-1, P).T)


def row(b):
    return b.reshape(1, -1)


def wo_order(a, heads, width):
    per = P // width
    order = [(u // per * 4 + i) * per + u % per for u in range(heads // 4) for i in range(4)]
    return a.reshape(heads, width, -1)[order].reshape(heads * width, -1)


def lay_out(i):
    i = {n: np.asarray(a) for n, a in i.items()}
    w = {"x": i["x"], "ctxT": i["ctx_768"].reshape(TOKENS, CTX).T,
         "ident": np.eye(P, dtype=np.float32), "ones": np.ones((P, P), np.float32)}
    future = (np.arange(P)[None, :] > np.arange(P)[:, None]).astype(np.int32)
    w["future"] = np.repeat(future[:, None, :], 4, axis=1)
    n = "L0_attn_"
    for m in "qkv":
        w[n + "W" + m] = pad_heads(i[n + "W" + m], 1)
    w[n + "bq"], w[n + "bk"] = columns(pad_heads(i[n + "bq"], 0)), columns(pad_heads(i[n + "bk"], 0))
    w[n + "bv"], w[n + "bo"] = row(pad_heads(i[n + "bv"], 0)), row(i[n + "bo"])
    w[n + "Wo"] = wo_order(pad_heads(i[n + "Wo"], 0), 16, PAD)
    for n in ("L1_xattn_", "L2_xattn_", "L3_xattn_"):
        for m in ("Wq", "Wk", "Wv", "Wo", "Wout", "bo", "bout"):
            if n + m in i:
                w[n + m] = i[n + m] if m[0] == "W" else row(i[n + m])
            if n + m in i and m in ("Wo", "Wout"):
                w[n + m] = wo_order(i[n + m], len(i[n + m]) // 64, 64)
    lay_out_rest(i, w)
    return {n: np.ascontiguousarray(a) for n, a in w.items()}


def kernel(**inputs):
    import concourse.bacc as bacc
    from concourse.bass_utils import run_bass_kernel_spmd

    arrays = {f"in_{n}": a for n, a in lay_out(inputs).items()}
    nc = bacc.Bacc("TRN2", target_bir_lowering=False, num_devices=1)
    w = {n[3:]: nc.dram_tensor(n, a.shape, mybir.dt.from_np(a.dtype), kind="ExternalInput").ap() for n, a in arrays.items()}
    out = nc.dram_tensor("out_0_dram", (BATCH, SEQ, DIM), F32, kind="ExternalOutput").ap()
    build(nc, w, out)
    return run_bass_kernel_spmd(nc, [arrays], core_ids=[0]).results[0]["out_0_dram"]
```
